# Optimizing a Trainium2 kernel written in Bass

```python
import numpy as np
import jax
import jax.numpy as jnp

def _softmax(x, axis=-1):
    return jax.nn.softmax(x, axis=axis)

def _gelu(x):
    return jax.nn.gelu(x, approximate=True)

def _silu(x):
    return jax.nn.silu(x)

def _sigmoid(x):
    return jax.nn.sigmoid(x)

def _layernorm(x, axis=-1, eps=1e-05):
    m = jnp.mean(x, axis=axis, keepdims=True)
    v = jnp.var(x, axis=axis, keepdims=True)
    return (x - m) / jnp.sqrt(v + eps)

def _scatter_add(tgt, idx, src, axis=0):
    return tgt.at[idx].add(src)

def _segment_sum(src, seg, n):
    return jax.ops.segment_sum(src, seg, n)
kernel_name = 'mk_decoder_postln_d4_seqx_r8_b645d0'

def setup_inputs(seed: int=0):
    np.random.seed(seed)
    _w = jnp.asarray

    def _rec_inputs():
        import jax
        import jax.numpy as jnp
        _rk = jax.random.key(seed)
        x = -1.394e-06 + 0.9999 * jax.random.normal(jax.random.fold_in(_rk, 1), (4, 512, 128), jnp.float32)
        _lenS = 512 - jax.random.randint(jax.random.fold_in(_rk, 7), (4,), 0, max(1, 512 // 4) + 1, jnp.int32)
        _lenS2 = 154 - jax.random.randint(jax.random.fold_in(_rk, 8), (4,), 0, max(1, 154 // 4) + 1, jnp.int32)
        _ctx_1024P = jax.random.normal(jax.random.fold_in(_rk, 11), (4, 16, 128), jnp.float32)
        _ctx_1024c = jax.random.dirichlet(jax.random.fold_in(_rk, 511), 0.3 * jnp.ones((16,), jnp.float32), (4, 154))
        _ctx_1024t = jnp.einsum('bsk,bkd->bsd', _ctx_1024c, _ctx_1024P)
        _ctx_1024t = _ctx_1024t * jax.lax.rsqrt(jnp.mean(jnp.square(_ctx_1024t)) + 1e-12) * 0.953939
        ctx_1024 = -0.000292821 + 1.00034 * (_ctx_1024t + 0.3 * jax.random.normal(jax.random.fold_in(_rk, 611), (4, 154, 128), jnp.float32))
        _validS = jnp.arange(512)[None, :] < _lenS[:, None]
        _validS2 = jnp.arange(154)[None, :] < _lenS2[:, None]
        _causal = jnp.tril(jnp.ones((512, 512), dtype=bool))
        mask_BxSxS2_ik1 = jnp.where(jnp.broadcast_to(_validS2[:, None, :], (4, 512, 154)), 1, 0).astype(jnp.int32)
        mask_Bx1xSxS2_bk1 = jnp.broadcast_to(_validS2[:, None, None, :], (4, 1, 512, 154))
        return (x, ctx_1024, mask_BxSxS2_ik1, mask_Bx1xSxS2_bk1)
    x, ctx_1024, mask_BxSxS2_ik1, mask_Bx1xSxS2_bk1 = _rec_inputs()

    def _L0_attn_setup():
        import jax, jax.numpy as jnp
        import numpy as np
        B, S, D, H = (4, 256, 128, 16)

        def _apply_rope(x):
            b, s, d = x.shape
            half = d // 2
            freq = jnp.exp(jnp.arange(0, d, 2, dtype=jnp.float32) * (-np.log(10000.0) / d))
            ang = jnp.arange(s, dtype=jnp.float32)[:, None] * freq[None, :]
            cos, sin = (jnp.cos(ang), jnp.sin(ang))
            x1, x2 = (x[..., :half], x[..., half:])
            return jnp.concatenate([x1 * cos - x2 * sin, x1 * sin + x2 * cos], axis=-1)
        key = jax.random.key(seed)
        ks = jax.random.split(key, 9)
        scale = 0.02
        x = jax.random.normal(ks[0], (B, S, D), dtype=jnp.float32)
        Wq = jax.random.normal(ks[1], (D, D), dtype=jnp.float32) * scale
        bq = jax.random.normal(ks[2], (D,), dtype=jnp.float32) * scale
        Wk = jax.random.normal(ks[3], (D, D), dtype=jnp.float32) * scale
        bk = jax.random.normal(ks[4], (D,), dtype=jnp.float32) * scale
        Wv = jax.random.normal(ks[5], (D, D), dtype=jnp.float32) * scale
        bv = jax.random.normal(ks[6], (D,), dtype=jnp.float32) * scale
        Wo = jax.random.normal(ks[7], (D, D), dtype=jnp.float32) * scale
        bo = jax.random.normal(ks[8], (D,), dtype=jnp.float32) * scale
        return {'x': x, 'Wq': Wq, 'bq': bq, 'Wk': Wk, 'bk': bk, 'Wv': Wv, 'bv': bv, 'Wo': Wo, 'bo': bo}
    _L0_attn_all = _L0_attn_setup()
    _L0_attn_in = {k: v for k, v in _L0_attn_all.items() if k in ('Wq', 'bq', 'Wk', 'bk', 'Wv', 'bv', 'Wo', 'bo')}
    del _L0_attn_all

    def _L0_xattn_setup():
        import jax, jax.numpy as jnp
        import numpy as np
        NUM_HEADS = 16
        D_MODEL = 128
        LN_EPS = 1e-05
        key = jax.random.key(seed)
        ks = jax.random.split(key, 10)
        B, S, D = (2, 256, D_MODEL)
        s = 1.0 / np.sqrt(D)
        return {'encoded': jax.random.normal(ks[0], (B, S, D), jnp.float32), 'decoded': jax.random.normal(ks[1], (B, S, D), jnp.float32), 'Wq': jax.random.normal(ks[2], (D, D), jnp.float32) * s, 'bq': jax.random.normal(ks[3], (D,), jnp.float32) * s, 'Wk': jax.random.normal(ks[4], (D, D), jnp.float32) * s, 'bk': jax.random.normal(ks[5], (D,), jnp.float32) * s, 'Wv': jax.random.normal(ks[6], (D, D), jnp.float32) * s, 'bv': jax.random.normal(ks[7], (D,), jnp.float32) * s, 'gamma': jnp.ones((D,), jnp.float32), 'beta': jnp.zeros((D,), jnp.float32)}
    _L0_xattn_all = _L0_xattn_setup()
    _L0_xattn_in = {k: v for k, v in _L0_xattn_all.items() if k in ('Wq', 'bq', 'Wk', 'bk', 'Wv', 'bv', 'gamma', 'beta')}
    del _L0_xattn_all

    def _L0_ffn_setup():
        import jax, jax.numpy as jnp
        import numpy as np
        D_IN, D_HID = (128, 512)

        def _ternary(key, shape):
            return jax.random.randint(key, shape, -1, 2).astype(jnp.float32)

        def _tlin(x, w, s):
            return jnp.einsum('bsi,oi->bso', x, w) * s
        key = jax.random.key(seed)
        ks = jax.random.split(key, 12)
        inv = lambda fan: 1.0 / np.sqrt(fan).astype(np.float32)
        return {'x': jax.random.normal(ks[0], (4, 256, D_IN), dtype=jnp.float32), 'w1_w': _ternary(ks[1], (D_HID, D_IN)), 'w1_s': jax.random.uniform(ks[2], (D_HID,), dtype=jnp.float32) * inv(D_IN), 'w2_w': _ternary(ks[3], (D_HID, D_IN)), 'w2_s': jax.random.uniform(ks[4], (D_HID,), dtype=jnp.float32) * inv(D_IN), 'h1_w': _ternary(ks[5], (D_HID, D_HID)), 'h1_s': jax.random.uniform(ks[6], (D_HID,), dtype=jnp.float32) * inv(D_HID), 'h2_w': _ternary(ks[7], (D_HID, D_HID)), 'h2_s': jax.random.uniform(ks[8], (D_HID,), dtype=jnp.float32) * inv(D_HID), 'w3_w': _ternary(ks[9], (D_IN, D_HID)), 'w3_s': jax.random.uniform(ks[10], (D_IN,), dtype=jnp.float32) * inv(D_HID)}
    _L0_ffn_all = _L0_ffn_setup()
    _L0_ffn_in = {k: v for k, v in _L0_ffn_all.items() if k in ('w1_w', 'w1_s', 'w2_w', 'w2_s', 'h1_w', 'h1_s', 'h2_w', 'h2_s', 'w3_w', 'w3_s')}
    del _L0_ffn_all

    def _L1_attn_setup():
        import jax, jax.numpy as jnp
        from jax import lax
        import numpy as np
        D_MODEL = 128
        D_STATE = 16
        D_CONV = 4
        EXPAND = 2
        D_INNER = D_MODEL * EXPAND
        DT_RANK = (D_MODEL + 15) // 16
        B, T = (2, 256)

        def _silu(v):
            return v * jax.nn.sigmoid(v)
        key = jax.random.key(seed)
        ks = jax.random.split(key, 8)

        def rn(k, shape, scale):
            return jax.random.normal(k, shape, dtype=jnp.float32) * scale
        x = rn(ks[0], (B, T, D_MODEL), 1.0)
        W_in = rn(ks[1], (D_MODEL, 2 * D_INNER), D_MODEL ** (-0.5))
        conv_w = rn(ks[2], (D_INNER, D_CONV), D_CONV ** (-0.5))
        conv_b = jnp.zeros((D_INNER,), jnp.float32)
        W_x = rn(ks[3], (D_INNER, DT_RANK + 2 * D_STATE), D_INNER ** (-0.5))
        W_dt = rn(ks[4], (DT_RANK, D_INNER), DT_RANK ** (-0.5))
        b_dt = jnp.log(jnp.expm1(jnp.full((D_INNER,), 0.01, jnp.float32)))
        A_log = jnp.log(jnp.broadcast_to(jnp.arange(1, D_STATE + 1, dtype=jnp.float32), (D_INNER, D_STATE)))
        Dp = jnp.ones((D_INNER,), jnp.float32)
        W_out = rn(ks[5], (D_INNER, D_MODEL), D_INNER ** (-0.5))
        return dict(x=x, W_in=W_in, conv_w=conv_w, conv_b=conv_b, W_x=W_x, W_dt=W_dt, b_dt=b_dt, A_log=A_log, D=Dp, W_out=W_out)
    _L1_attn_all = _L1_attn_setup()
    _L1_attn_in = {k: v for k, v in _L1_attn_all.items() if k in ('W_in', 'conv_w', 'conv_b', 'W_x', 'W_dt', 'b_dt', 'A_log', 'D', 'W_out')}
    del _L1_attn_all

    def _L1_xattn_setup():
        import jax, jax.numpy as jnp
        import numpy as np
        INPUT_DIM = 128
        HEADS = 16
        D_K = INPUT_DIM // HEADS
        B, S = (4, 256)
        key = jax.random.key(seed)
        ks = jax.random.split(key, 12)
        scale = 1.0 / np.sqrt(INPUT_DIM)
        inp = {'q': jax.random.normal(ks[0], (B, S, INPUT_DIM), jnp.float32), 'k': jax.random.normal(ks[1], (B, S, INPUT_DIM), jnp.float32), 'v': jax.random.normal(ks[2], (B, S, INPUT_DIM), jnp.float32), 'mask': jax.random.randint(ks[3], (B, S, S), 0, 2, jnp.int32), 'Wq': jax.random.normal(ks[4], (INPUT_DIM, INPUT_DIM), jnp.float32) * scale, 'bq': jnp.zeros((INPUT_DIM,), jnp.float32), 'Wk': jax.random.normal(ks[5], (INPUT_DIM, INPUT_DIM), jnp.float32) * scale, 'bk': jnp.zeros((INPUT_DIM,), jnp.float32), 'Wv': jax.random.normal(ks[6], (INPUT_DIM, INPUT_DIM), jnp.float32) * scale, 'bv': jnp.zeros((INPUT_DIM,), jnp.float32), 'Wo': jax.random.normal(ks[7], (INPUT_DIM, INPUT_DIM), jnp.float32) * scale, 'bo': jnp.zeros((INPUT_DIM,), jnp.float32)}
        return inp
    _L1_xattn_all = _L1_xattn_setup()
    _L1_xattn_in = {k: v for k, v in _L1_xattn_all.items() if k in ('Wq', 'bq', 'Wk', 'bk', 'Wv', 'bv', 'Wo', 'bo')}
    del _L1_xattn_all

    def _L1_ffn_setup():
        import jax, jax.numpy as jnp
        import numpy as np
        B, N, DIM = (2, 256, 128)
        HEADS, DIM_HEAD, EXPERTS = (8, 64, 8)
        SCALE = DIM_HEAD ** (-0.5)
        key = jax.random.key(seed)
        ks = jax.random.split(key, 6)
        dim_inner = HEADS * DIM_HEAD
        return {'x': jax.random.normal(ks[0], (B, N, DIM), jnp.float32), 'w_q': jax.random.normal(ks[1], (DIM, dim_inner), jnp.float32) * 0.02, 'w_k': jax.random.normal(ks[2], (DIM, dim_inner), jnp.float32) * 0.02, 'w_gate': jax.random.normal(ks[3], (DIM, HEADS * EXPERTS), jnp.float32) * 0.02, 'value_experts': jax.random.normal(ks[4], (EXPERTS, HEADS, DIM, DIM_HEAD), jnp.float32) * 0.02, 'output_experts': jax.random.normal(ks[5], (EXPERTS, HEADS, DIM_HEAD, DIM), jnp.float32) * 0.02}
    _L1_ffn_all = _L1_ffn_setup()
    _L1_ffn_in = {k: v for k, v in _L1_ffn_all.items() if k in ('w_q', 'w_k', 'w_gate', 'value_experts', 'output_experts')}
    del _L1_ffn_all

    def _L2_attn_setup():
        import jax, jax.numpy as jnp
        import numpy as np
        NUM_HEADS = 16
        VALUE_SIZE = 64
        MODEL_SIZE = 128
        BATCH = 4
        SEQ = 128
        key = jax.random.key(seed)
        ks = jax.random.split(key, 5)
        scale = 1.0 / np.sqrt(MODEL_SIZE)
        x = jax.random.normal(ks[0], (BATCH, SEQ, MODEL_SIZE), dtype=jnp.float32)
        w_q = jax.random.normal(ks[1], (MODEL_SIZE, NUM_HEADS * VALUE_SIZE), dtype=jnp.float32) * scale
        w_kv = jax.random.normal(ks[2], (MODEL_SIZE, NUM_HEADS * VALUE_SIZE), dtype=jnp.float32) * scale
        w_o = jax.random.normal(ks[3], (NUM_HEADS * VALUE_SIZE, MODEL_SIZE), dtype=jnp.float32) * scale
        k_weights = jax.random.normal(ks[4], (1, NUM_HEADS, 1, VALUE_SIZE), dtype=jnp.float32) * 0.02
        return {'x': x, 'w_q': w_q, 'w_kv': w_kv, 'w_o': w_o, 'k_weights': k_weights}
    _L2_attn_all = _L2_attn_setup()
    _L2_attn_in = {k: v for k, v in _L2_attn_all.items() if k in ('w_q', 'w_kv', 'w_o', 'k_weights')}
    del _L2_attn_all

    def _L2_xattn_setup():
        import jax, jax.numpy as jnp
        import numpy as np
        H = 16
        key = jax.random.key(seed)
        ks = jax.random.split(key, 11)
        B, S, D = (4, 256, 128)
        s = 1.0 / np.sqrt(D)
        return {'query': jax.random.normal(ks[0], (B, S, D), jnp.float32), 'key': jax.random.normal(ks[1], (B, S, D), jnp.float32), 'value': jax.random.normal(ks[2], (B, S, D), jnp.float32), 'Wq': jax.random.normal(ks[3], (D, D), jnp.float32) * s, 'bq': jax.random.normal(ks[4], (D,), jnp.float32) * 0.01, 'Wk': jax.random.normal(ks[5], (D, D), jnp.float32) * s, 'bk': jax.random.normal(ks[6], (D,), jnp.float32) * 0.01, 'Wv': jax.random.normal(ks[7], (D, D), jnp.float32) * s, 'bv': jax.random.normal(ks[8], (D,), jnp.float32) * 0.01, 'Wo': jax.random.normal(ks[9], (D, D), jnp.float32) * s, 'bo': jax.random.normal(ks[10], (D,), jnp.float32) * 0.01}
    _L2_xattn_all = _L2_xattn_setup()
    _L2_xattn_in = {k: v for k, v in _L2_xattn_all.items() if k in ('Wq', 'bq', 'Wk', 'bk', 'Wv', 'bv', 'Wo', 'bo')}
    del _L2_xattn_all

    def _L2_ffn_setup():
        import jax, jax.numpy as jnp
        import numpy as np
        from jax import lax
        B, L, D = (4, 256, 128)
        E, TOPK = (8, 2)
        K, DIL = (3, 1)
        HID = D // 4
        EPS = 1e-06

        def _rmsnorm(h, w):
            rms = jnp.sqrt(jnp.mean(h * h, axis=-1, keepdims=True) + EPS)
            return w * (h / rms)

        def _forward(x, dw_kernel, dw_bias, pw_w, pw_b, router_w, router_b, expert_w, expert_b, out_w, out_b, norm_w, ff_down_w, ff_down_b, ff_up_w, ff_up_b):
            pad = (K - 1) * DIL
            xc = jnp.transpose(x, (0, 2, 1))
            xc = lax.conv_general_dilated(xc, dw_kernel, window_strides=(1,), padding=((pad, 0),), rhs_dilation=(DIL,), dimension_numbers=('NCH', 'OIH', 'NCH'), feature_group_count=D) + dw_bias[None, :, None]
            xc = jax.nn.silu(jnp.einsum('bdl,ed->bel', xc, pw_w) + pw_b[None, :, None])
            x1 = x + jnp.transpose(xc, (0, 2, 1))
            logits = jnp.einsum('bsd,ed->bse', x1, router_w) + router_b
            top_v, top_i = lax.top_k(logits, TOPK)
            top_w = jax.nn.softmax(top_v, axis=-1)
            rw = jnp.sum(jax.nn.one_hot(top_i, E, dtype=x1.dtype) * top_w[..., None], axis=-2)
            ye = jax.nn.silu(jnp.einsum('bsd,eod->bseo', x1, expert_w) + expert_b)
            combined = jnp.einsum('bse,bseo->bso', rw, ye)
            moe_out = jnp.einsum('bsd,od->bso', combined, out_w) + out_b
            h = _rmsnorm(x1 + moe_out, norm_w)
            ff = jax.nn.gelu(jnp.einsum('bsd,hd->bsh', h, ff_down_w) + ff_down_b, approximate=False)
            ff = jnp.einsum('bsh,dh->bsd', ff, ff_up_w) + ff_up_b
            return h + ff
        key = jax.random.key(seed)
        ks = jax.random.split(key, 16)
        s = 0.02
        return {'x': jax.random.normal(ks[0], (B, L, D), dtype=jnp.float32), 'dw_kernel': jax.random.normal(ks[1], (D, 1, K), dtype=jnp.float32) * s, 'dw_bias': jnp.zeros((D,), dtype=jnp.float32), 'pw_w': jax.random.normal(ks[2], (D, D), dtype=jnp.float32) * s, 'pw_b': jnp.zeros((D,), dtype=jnp.float32), 'router_w': jax.random.normal(ks[3], (E, D), dtype=jnp.float32) * s, 'router_b': jnp.zeros((E,), dtype=jnp.float32), 'expert_w': jax.random.normal(ks[4], (E, D, D), dtype=jnp.float32) * s, 'expert_b': jnp.zeros((E, D), dtype=jnp.float32), 'out_w': jax.random.normal(ks[5], (D, D), dtype=jnp.float32) * s, 'out_b': jnp.zeros((D,), dtype=jnp.float32), 'norm_w': jnp.ones((D,), dtype=jnp.float32), 'ff_down_w': jax.random.normal(ks[6], (HID, D), dtype=jnp.float32) * s, 'ff_down_b': jnp.zeros((HID,), dtype=jnp.float32), 'ff_up_w': jax.random.normal(ks[7], (D, HID), dtype=jnp.float32) * s, 'ff_up_b': jnp.zeros((D,), dtype=jnp.float32)}
    _L2_ffn_all = _L2_ffn_setup()
    _L2_ffn_in = {k: v for k, v in _L2_ffn_all.items() if k in ('dw_kernel', 'dw_bias', 'pw_w', 'pw_b', 'router_w', 'router_b', 'expert_w', 'expert_b', 'out_w', 'out_b', 'norm_w', 'ff_down_w', 'ff_down_b', 'ff_up_w', 'ff_up_b')}
    del _L2_ffn_all

    def _L3_attn_setup():
        import jax, jax.numpy as jnp
        import numpy as np
        EMB, HEADS = (128, 16)
        S = EMB // HEADS
        key = jax.random.key(seed)
        ks = jax.random.split(key, 7)
        b, t = (2, 256)
        sc = 0.02
        return {'x': jax.random.normal(ks[0], (b, t, EMB), jnp.float32), 'W_down': jax.random.normal(ks[1], (EMB, EMB), jnp.float32) * sc, 'tokeys': jax.random.normal(ks[2], (HEADS, S, S), jnp.float32) * sc, 'toqueries': jax.random.normal(ks[3], (HEADS, S, S), jnp.float32) * sc, 'tovalues': jax.random.normal(ks[4], (HEADS, S, S), jnp.float32) * sc, 'W_unify': jax.random.normal(ks[5], (EMB, EMB), jnp.float32) * sc, 'b_unify': jax.random.normal(ks[6], (EMB,), jnp.float32) * sc}
    _L3_attn_all = _L3_attn_setup()
    _L3_attn_in = {k: v for k, v in _L3_attn_all.items() if k in ('W_down', 'tokeys', 'toqueries', 'tovalues', 'W_unify', 'b_unify')}
    del _L3_attn_all

    def _L3_xattn_setup():
        import jax, jax.numpy as jnp
        import numpy as np
        HEADS = 16
        D_MODEL = 128
        D_K = D_MODEL // HEADS
        B, S = (2, 256)
        NEG = -1000000000.0
        key = jax.random.key(seed)
        ks = jax.random.split(key, 8)
        q = jax.random.normal(ks[0], (B, S, D_MODEL), dtype=jnp.float32)
        k = jax.random.normal(ks[1], (B, S, D_MODEL), dtype=jnp.float32)
        v = jax.random.normal(ks[2], (B, S, D_MODEL), dtype=jnp.float32)
        mask = jax.random.randint(ks[3], (B, 1, S, S), 0, 2) > 0
        scale = 1.0 / np.sqrt(D_MODEL)
        Wq = jax.random.normal(ks[4], (D_MODEL, D_MODEL), dtype=jnp.float32) * scale
        Wk = jax.random.normal(ks[5], (D_MODEL, D_MODEL), dtype=jnp.float32) * scale
        Wv = jax.random.normal(ks[6], (D_MODEL, D_MODEL), dtype=jnp.float32) * scale
        Wo = jax.random.normal(ks[7], (D_MODEL, D_MODEL), dtype=jnp.float32) * scale
        return {'q': q, 'k': k, 'v': v, 'mask': mask, 'Wq': Wq, 'Wk': Wk, 'Wv': Wv, 'Wo': Wo}
    _L3_xattn_all = _L3_xattn_setup()
    _L3_xattn_in = {k: v for k, v in _L3_xattn_all.items() if k in ('Wq', 'Wk', 'Wv', 'Wo')}
    del _L3_xattn_all

    def _L3_ffn_setup():
        import jax, jax.numpy as jnp
        import numpy as np
        DIM = 128
        HID = 352
        N_ROUTED = 7
        TOPK = 2
        B, S = (4, 256)

        def _expert(x, wg, wu, wd):
            return jax.nn.silu(x @ wg) * (x @ wu) @ wd
        key = jax.random.key(seed)
        ks = jax.random.split(key, 9)
        s = 0.02
        x = jax.random.normal(ks[0], (B, S, DIM), jnp.float32)
        shared_gate = jax.random.normal(ks[1], (DIM, HID), jnp.float32) * s
        shared_up = jax.random.normal(ks[2], (DIM, HID), jnp.float32) * s
        shared_down = jax.random.normal(ks[3], (HID, DIM), jnp.float32) * s
        routed_gate = jax.random.normal(ks[4], (N_ROUTED, DIM, HID), jnp.float32) * s
        routed_up = jax.random.normal(ks[5], (N_ROUTED, DIM, HID), jnp.float32) * s
        routed_down = jax.random.normal(ks[6], (N_ROUTED, HID, DIM), jnp.float32) * s
        Wr = jax.random.normal(ks[7], (DIM, N_ROUTED), jnp.float32) * s
        routing_bias = jax.random.normal(ks[8], (N_ROUTED,), jnp.float32)
        return dict(x=x, shared_gate=shared_gate, shared_up=shared_up, shared_down=shared_down, routed_gate=routed_gate, routed_up=routed_up, routed_down=routed_down, Wr=Wr, routing_bias=routing_bias)
    _L3_ffn_all = _L3_ffn_setup()
    _L3_ffn_in = {k: v for k, v in _L3_ffn_all.items() if k in ('shared_gate', 'shared_up', 'shared_down', 'routed_gate', 'routed_up', 'routed_down', 'Wr', 'routing_bias')}
    del _L3_ffn_all
    return {'x': x, 'ctx_1024': ctx_1024, 'mask_BxSxS2_ik1': mask_BxSxS2_ik1, 'mask_Bx1xSxS2_bk1': mask_Bx1xSxS2_bk1, 'L0_attn_Wq': _L0_attn_in['Wq'], 'L0_attn_bq': _L0_attn_in['bq'], 'L0_attn_Wk': _L0_attn_in['Wk'], 'L0_attn_bk': _L0_attn_in['bk'], 'L0_attn_Wv': _L0_attn_in['Wv'], 'L0_attn_bv': _L0_attn_in['bv'], 'L0_attn_Wo': _L0_attn_in['Wo'], 'L0_attn_bo': _L0_attn_in['bo'], 'L0_xattn_Wq': _L0_xattn_in['Wq'], 'L0_xattn_bq': _L0_xattn_in['bq'], 'L0_xattn_Wk': _L0_xattn_in['Wk'], 'L0_xattn_bk': _L0_xattn_in['bk'], 'L0_xattn_Wv': _L0_xattn_in['Wv'], 'L0_xattn_bv': _L0_xattn_in['bv'], 'L0_xattn_gamma': _L0_xattn_in['gamma'], 'L0_xattn_beta': _L0_xattn_in['beta'], 'L0_ffn_w1_w': _L0_ffn_in['w1_w'], 'L0_ffn_w1_s': _L0_ffn_in['w1_s'], 'L0_ffn_w2_w': _L0_ffn_in['w2_w'], 'L0_ffn_w2_s': _L0_ffn_in['w2_s'], 'L0_ffn_h1_w': _L0_ffn_in['h1_w'], 'L0_ffn_h1_s': _L0_ffn_in['h1_s'], 'L0_ffn_h2_w': _L0_ffn_in['h2_w'], 'L0_ffn_h2_s': _L0_ffn_in['h2_s'], 'L0_ffn_w3_w': _L0_ffn_in['w3_w'], 'L0_ffn_w3_s': _L0_ffn_in['w3_s'], 'L1_attn_W_in': _L1_attn_in['W_in'], 'L1_attn_conv_w': _L1_attn_in['conv_w'], 'L1_attn_conv_b': _L1_attn_in['conv_b'], 'L1_attn_W_x': _L1_attn_in['W_x'], 'L1_attn_W_dt': _L1_attn_in['W_dt'], 'L1_attn_b_dt': _L1_attn_in['b_dt'], 'L1_attn_A_log': _L1_attn_in['A_log'], 'L1_attn_D': _L1_attn_in['D'], 'L1_attn_W_out': _L1_attn_in['W_out'], 'L1_xattn_Wq': _L1_xattn_in['Wq'], 'L1_xattn_bq': _L1_xattn_in['bq'], 'L1_xattn_Wk': _L1_xattn_in['Wk'], 'L1_xattn_bk': _L1_xattn_in['bk'], 'L1_xattn_Wv': _L1_xattn_in['Wv'], 'L1_xattn_bv': _L1_xattn_in['bv'], 'L1_xattn_Wo': _L1_xattn_in['Wo'], 'L1_xattn_bo': _L1_xattn_in['bo'], 'L1_ffn_w_q': _L1_ffn_in['w_q'], 'L1_ffn_w_k': _L1_ffn_in['w_k'], 'L1_ffn_w_gate': _L1_ffn_in['w_gate'], 'L1_ffn_value_experts': _L1_ffn_in['value_experts'], 'L1_ffn_output_experts': _L1_ffn_in['output_experts'], 'L2_attn_w_q': _L2_attn_in['w_q'], 'L2_attn_w_kv': _L2_attn_in['w_kv'], 'L2_attn_w_o': _L2_attn_in['w_o'], 'L2_attn_k_weights': _L2_attn_in['k_weights'], 'L2_xattn_Wq': _L2_xattn_in['Wq'], 'L2_xattn_bq': _L2_xattn_in['bq'], 'L2_xattn_Wk': _L2_xattn_in['Wk'], 'L2_xattn_bk': _L2_xattn_in['bk'], 'L2_xattn_Wv': _L2_xattn_in['Wv'], 'L2_xattn_bv': _L2_xattn_in['bv'], 'L2_xattn_Wo': _L2_xattn_in['Wo'], 'L2_xattn_bo': _L2_xattn_in['bo'], 'L2_ffn_dw_kernel': _L2_ffn_in['dw_kernel'], 'L2_ffn_dw_bias': _L2_ffn_in['dw_bias'], 'L2_ffn_pw_w': _L2_ffn_in['pw_w'], 'L2_ffn_pw_b': _L2_ffn_in['pw_b'], 'L2_ffn_router_w': _L2_ffn_in['router_w'], 'L2_ffn_router_b': _L2_ffn_in['router_b'], 'L2_ffn_expert_w': _L2_ffn_in['expert_w'], 'L2_ffn_expert_b': _L2_ffn_in['expert_b'], 'L2_ffn_out_w': _L2_ffn_in['out_w'], 'L2_ffn_out_b': _L2_ffn_in['out_b'], 'L2_ffn_norm_w': _L2_ffn_in['norm_w'], 'L2_ffn_ff_down_w': _L2_ffn_in['ff_down_w'], 'L2_ffn_ff_down_b': _L2_ffn_in['ff_down_b'], 'L2_ffn_ff_up_w': _L2_ffn_in['ff_up_w'], 'L2_ffn_ff_up_b': _L2_ffn_in['ff_up_b'], 'L3_attn_W_down': _L3_attn_in['W_down'], 'L3_attn_tokeys': _L3_attn_in['tokeys'], 'L3_attn_toqueries': _L3_attn_in['toqueries'], 'L3_attn_tovalues': _L3_attn_in['tovalues'], 'L3_attn_W_unify': _L3_attn_in['W_unify'], 'L3_attn_b_unify': _L3_attn_in['b_unify'], 'L3_xattn_Wq': _L3_xattn_in['Wq'], 'L3_xattn_Wk': _L3_xattn_in['Wk'], 'L3_xattn_Wv': _L3_xattn_in['Wv'], 'L3_xattn_Wo': _L3_xattn_in['Wo'], 'L3_ffn_shared_gate': _L3_ffn_in['shared_gate'], 'L3_ffn_shared_up': _L3_ffn_in['shared_up'], 'L3_ffn_shared_down': _L3_ffn_in['shared_down'], 'L3_ffn_routed_gate': _L3_ffn_in['routed_gate'], 'L3_ffn_routed_up': _L3_ffn_in['routed_up'], 'L3_ffn_routed_down': _L3_ffn_in['routed_down'], 'L3_ffn_Wr': _L3_ffn_in['Wr'], 'L3_ffn_routing_bias': _L3_ffn_in['routing_bias']}

def reference(x, ctx_1024, mask_BxSxS2_ik1, mask_Bx1xSxS2_bk1, L0_attn_Wq, L0_attn_bq, L0_attn_Wk, L0_attn_bk, L0_attn_Wv, L0_attn_bv, L0_attn_Wo, L0_attn_bo, L0_xattn_Wq, L0_xattn_bq, L0_xattn_Wk, L0_xattn_bk, L0_xattn_Wv, L0_xattn_bv, L0_xattn_gamma, L0_xattn_beta, L0_ffn_w1_w, L0_ffn_w1_s, L0_ffn_w2_w, L0_ffn_w2_s, L0_ffn_h1_w, L0_ffn_h1_s, L0_ffn_h2_w, L0_ffn_h2_s, L0_ffn_w3_w, L0_ffn_w3_s, L1_attn_W_in, L1_attn_conv_w, L1_attn_conv_b, L1_attn_W_x, L1_attn_W_dt, L1_attn_b_dt, L1_attn_A_log, L1_attn_D, L1_attn_W_out, L1_xattn_Wq, L1_xattn_bq, L1_xattn_Wk, L1_xattn_bk, L1_xattn_Wv, L1_xattn_bv, L1_xattn_Wo, L1_xattn_bo, L1_ffn_w_q, L1_ffn_w_k, L1_ffn_w_gate, L1_ffn_value_experts, L1_ffn_output_experts, L2_attn_w_q, L2_attn_w_kv, L2_attn_w_o, L2_attn_k_weights, L2_xattn_Wq, L2_xattn_bq, L2_xattn_Wk, L2_xattn_bk, L2_xattn_Wv, L2_xattn_bv, L2_xattn_Wo, L2_xattn_bo, L2_ffn_dw_kernel, L2_ffn_dw_bias, L2_ffn_pw_w, L2_ffn_pw_b, L2_ffn_router_w, L2_ffn_router_b, L2_ffn_expert_w, L2_ffn_expert_b, L2_ffn_out_w, L2_ffn_out_b, L2_ffn_norm_w, L2_ffn_ff_down_w, L2_ffn_ff_down_b, L2_ffn_ff_up_w, L2_ffn_ff_up_b, L3_attn_W_down, L3_attn_tokeys, L3_attn_toqueries, L3_attn_tovalues, L3_attn_W_unify, L3_attn_b_unify, L3_xattn_Wq, L3_xattn_Wk, L3_xattn_Wv, L3_xattn_Wo, L3_ffn_shared_gate, L3_ffn_shared_up, L3_ffn_shared_down, L3_ffn_routed_gate, L3_ffn_routed_up, L3_ffn_routed_down, L3_ffn_Wr, L3_ffn_routing_bias):
    import jax
    import jax.numpy as jnp

    def _L0_attn_ref(x, Wq, bq, Wk, bk, Wv, bv, Wo, bo):
        import jax, jax.numpy as jnp
        import numpy as np
        B, S, D, H = (4, 256, 128, 16)

        def _apply_rope(x):
            b, s, d = x.shape
            half = d // 2
            freq = jnp.exp(jnp.arange(0, d, 2, dtype=jnp.float32) * (-np.log(10000.0) / d))
            ang = jnp.arange(s, dtype=jnp.float32)[:, None] * freq[None, :]
            cos, sin = (jnp.cos(ang), jnp.sin(ang))
            x1, x2 = (x[..., :half], x[..., half:])
            return jnp.concatenate([x1 * cos - x2 * sin, x1 * sin + x2 * cos], axis=-1)
        b, s, d = x.shape
        h = H
        hd = d // h
        rx = _apply_rope(x)

        def proj(W, bias):
            y = rx @ W.T + bias
            return y.reshape(b, s, h, hd).transpose(0, 2, 1, 3)
        q, k, v = (proj(Wq, bq), proj(Wk, bk), proj(Wv, bv))
        scores = jnp.einsum('bhqd,bhkd->bhqk', q, k) / np.sqrt(hd)
        attn = jax.nn.softmax(scores, axis=-1)
        attended = jnp.einsum('bhqk,bhkd->bhqd', attn, v)
        attended = attended.transpose(0, 2, 1, 3).reshape(b, s, d)
        return attended @ Wo.T + bo

    def _L0_xattn_ref(encoded, decoded, Wq, bq, Wk, bk, Wv, bv, gamma, beta):
        import jax, jax.numpy as jnp
        import numpy as np
        NUM_HEADS = 16
        D_MODEL = 128
        LN_EPS = 1e-05
        B, Sq, D = decoded.shape
        H = NUM_HEADS
        dh = D // H
        q = decoded @ Wq.T + bq
        k = encoded @ Wk.T + bk
        v = encoded @ Wv.T + bv
        q = q.reshape(B, Sq, H, dh).transpose(0, 2, 1, 3)
        k = k.reshape(B, -1, H, dh).transpose(0, 2, 1, 3)
        v = v.reshape(B, -1, H, dh).transpose(0, 2, 1, 3)
        qk = jnp.einsum('bhqd,bhkd->bhqk', q, k)
        qk = jnp.where(jnp.isnan(qk), -jnp.inf, qk)
        attn = jax.nn.softmax(qk, axis=-1)
        attn = jnp.where(jnp.isnan(attn), 0.0, attn)
        v = jnp.where(jnp.isnan(v), 0.0, v)
        z = jnp.einsum('bhqk,bhkd->bhqd', attn, v)
        z = z.reshape(B, Sq, D)
        x = z + decoded
        mu = jnp.mean(x, axis=-1, keepdims=True)
        var = jnp.var(x, axis=-1, keepdims=True)
        return (x - mu) * jax.lax.rsqrt(var + LN_EPS) * gamma + beta

    def _L0_ffn_ref(x, w1_w, w1_s, w2_w, w2_s, h1_w, h1_s, h2_w, h2_s, w3_w, w3_s):
        import jax, jax.numpy as jnp
        import numpy as np
        D_IN, D_HID = (128, 512)

        def _ternary(key, shape):
            return jax.random.randint(key, shape, -1, 2).astype(jnp.float32)

        def _tlin(x, w, s):
            return jnp.einsum('bsi,oi->bso', x, w) * s
        h = jax.nn.silu(_tlin(x, w1_w, w1_s)) * _tlin(x, w2_w, w2_s)
        h = jax.nn.gelu(_tlin(h, h1_w, h1_s), approximate=False)
        h = jax.nn.gelu(_tlin(h, h2_w, h2_s), approximate=False)
        return _tlin(h, w3_w, w3_s)

    def _L1_attn_ref(x, W_in, conv_w, conv_b, W_x, W_dt, b_dt, A_log, D, W_out):
        import jax, jax.numpy as jnp
        from jax import lax
        import numpy as np
        D_MODEL = 128
        D_STATE = 16
        D_CONV = 4
        EXPAND = 2
        D_INNER = D_MODEL * EXPAND
        DT_RANK = (D_MODEL + 15) // 16
        B, T = (2, 256)

        def _silu(v):
            return v * jax.nn.sigmoid(v)
        Bb, Tt, _ = x.shape
        xz = x @ W_in
        xi, z = jnp.split(xz, 2, axis=-1)
        xi_nch = jnp.transpose(xi, (0, 2, 1))
        xc = lax.conv_general_dilated(xi_nch, conv_w[:, None, :], (1,), [(D_CONV - 1, 0)], feature_group_count=D_INNER, dimension_numbers=('NCH', 'OIH', 'NCH'))
        xc = _silu(jnp.transpose(xc, (0, 2, 1)) + conv_b)
        x_dbl = xc @ W_x
        dt, Bm, Cm = jnp.split(x_dbl, [DT_RANK, DT_RANK + D_STATE], axis=-1)
        delta = jax.nn.softplus(dt @ W_dt + b_dt)
        A = -jnp.exp(A_log)
        dA = jnp.exp(delta[..., None] * A)
        dBu = delta[..., None] * Bm[:, :, None, :] * xc[..., None]

        def step(h, inp):
            dA_t, dBu_t, C_t = inp
            h = dA_t * h + dBu_t
            y = jnp.einsum('bdn,bn->bd', h, C_t)
            return (h, y)
        h0 = jnp.zeros((Bb, D_INNER, D_STATE), x.dtype)
        _, ys = lax.scan(step, h0, (jnp.transpose(dA, (1, 0, 2, 3)), jnp.transpose(dBu, (1, 0, 2, 3)), jnp.transpose(Cm, (1, 0, 2))))
        y = jnp.transpose(ys, (1, 0, 2)) + xc * D
        return y * _silu(z) @ W_out

    def _L1_xattn_ref(q, k, v, mask, Wq, bq, Wk, bk, Wv, bv, Wo, bo):
        import jax, jax.numpy as jnp
        import numpy as np
        INPUT_DIM = 128
        HEADS = 16
        D_K = INPUT_DIM // HEADS
        B, S = (4, 256)
        bs = q.shape[0]

        def proj(x, W, b):
            return (x @ W.T + b).reshape(bs, -1, HEADS, D_K).transpose(0, 2, 1, 3)
        qh, kh, vh = (proj(q, Wq, bq), proj(k, Wk, bk), proj(v, Wv, bv))
        scores = jnp.einsum('bhqd,bhkd->bhqk', qh, kh) / jnp.sqrt(jnp.float32(D_K))
        scores = jnp.where(mask[:, None] == 0, jnp.float32(-1000000000.0), scores)
        attn = jax.nn.softmax(scores, axis=-1)
        ctx = jnp.einsum('bhqk,bhkd->bhqd', attn, vh)
        concat = ctx.transpose(0, 2, 1, 3).reshape(bs, -1, INPUT_DIM)
        return concat @ Wo.T + bo

    def _L1_ffn_ref(x, w_q, w_k, w_gate, value_experts, output_experts):
        import jax, jax.numpy as jnp
        import numpy as np
        B, N, DIM = (2, 256, 128)
        HEADS, DIM_HEAD, EXPERTS = (8, 64, 8)
        SCALE = DIM_HEAD ** (-0.5)
        b, n, _ = x.shape
        q = (x @ w_q).reshape(b, n, HEADS, DIM_HEAD).transpose(0, 2, 1, 3)
        k = (x @ w_k).reshape(b, n, HEADS, DIM_HEAD).transpose(0, 2, 1, 3)
        gates = jax.nn.sigmoid((x @ w_gate).reshape(b, n, HEADS, EXPERTS).transpose(0, 2, 1, 3))
        sel = jnp.argmax(gates, axis=-1)
        gm = jax.nn.one_hot(sel, EXPERTS, dtype=x.dtype) * gates
        values = jnp.einsum('bhne,ehdk,bnd->bhnk', gm, value_experts, x)
        sim = jnp.einsum('bhid,bhjd->bhij', q * SCALE, k)
        causal_mask = jnp.triu(jnp.ones((n, n), dtype=bool), 1)
        sim = jnp.where(causal_mask, jnp.finfo(sim.dtype).min, sim)
        attn = jax.nn.softmax(sim, axis=-1)
        out = jnp.einsum('bhij,bhjk->bhik', attn, values)
        out = jnp.einsum('bhne,ehkd,bhnk->bhnd', gm, output_experts, out)
        return out.sum(axis=1)

    def _L2_attn_ref(x, w_q, w_kv, w_o, k_weights):
        import jax, jax.numpy as jnp
        import numpy as np
        NUM_HEADS = 16
        VALUE_SIZE = 64
        MODEL_SIZE = 128
        BATCH = 4
        SEQ = 128
        b, L, d = x.shape
        h, v = (NUM_HEADS, VALUE_SIZE)
        q = x @ w_q * (1.0 / jnp.sqrt(jnp.asarray(d, x.dtype)))
        q = q.reshape(b, L, h, v).transpose(0, 2, 1, 3)
        kv = (x @ w_kv).reshape(b, L, h, v).transpose(0, 2, 1, 3)
        k = kv * (1.0 + k_weights)
        logits = jnp.einsum('bhik,bhjk->bhij', q, k)
        mask = jnp.tril(jnp.ones((L, L), dtype=bool))
        logits = jnp.where(mask, logits, jnp.asarray(-1000000.0, logits.dtype))
        a = jax.nn.softmax(logits, axis=-1)
        y = jnp.einsum('bhij,bhjv->bhiv', a, kv)
        y = y.transpose(0, 2, 1, 3).reshape(b, L, h * v)
        return y @ w_o

    def _L2_xattn_ref(query, key, value, Wq, bq, Wk, bk, Wv, bv, Wo, bo):
        import jax, jax.numpy as jnp
        import numpy as np
        H = 16
        B, S, D = query.shape
        d_k = D // H

        def proj(x, W, b):
            y = jnp.einsum('bsd,ed->bse', x, W) + b
            return y.reshape(B, -1, H, d_k).transpose(0, 2, 1, 3)
        q = proj(query, Wq, bq)
        k = proj(key, Wk, bk)
        v = proj(value, Wv, bv)
        scores = jnp.einsum('bhqd,bhkd->bhqk', q, k) / jnp.sqrt(jnp.float32(d_k))
        p = jax.nn.softmax(scores, axis=-1)
        x = jnp.einsum('bhqk,bhkd->bhqd', p, v)
        x = x.transpose(0, 2, 1, 3).reshape(B, S, D)
        return jnp.einsum('bsd,ed->bse', x, Wo) + bo

    def _L2_ffn_ref(x, dw_kernel, dw_bias, pw_w, pw_b, router_w, router_b, expert_w, expert_b, out_w, out_b, norm_w, ff_down_w, ff_down_b, ff_up_w, ff_up_b):
        import jax, jax.numpy as jnp
        import numpy as np
        from jax import lax
        B, L, D = (4, 256, 128)
        E, TOPK = (8, 2)
        K, DIL = (3, 1)
        HID = D // 4
        EPS = 1e-06

        def _rmsnorm(h, w):
            rms = jnp.sqrt(jnp.mean(h * h, axis=-1, keepdims=True) + EPS)
            return w * (h / rms)

        def _forward(x, dw_kernel, dw_bias, pw_w, pw_b, router_w, router_b, expert_w, expert_b, out_w, out_b, norm_w, ff_down_w, ff_down_b, ff_up_w, ff_up_b):
            pad = (K - 1) * DIL
            xc = jnp.transpose(x, (0, 2, 1))
            xc = lax.conv_general_dilated(xc, dw_kernel, window_strides=(1,), padding=((pad, 0),), rhs_dilation=(DIL,), dimension_numbers=('NCH', 'OIH', 'NCH'), feature_group_count=D) + dw_bias[None, :, None]
            xc = jax.nn.silu(jnp.einsum('bdl,ed->bel', xc, pw_w) + pw_b[None, :, None])
            x1 = x + jnp.transpose(xc, (0, 2, 1))
            logits = jnp.einsum('bsd,ed->bse', x1, router_w) + router_b
            top_v, top_i = lax.top_k(logits, TOPK)
            top_w = jax.nn.softmax(top_v, axis=-1)
            rw = jnp.sum(jax.nn.one_hot(top_i, E, dtype=x1.dtype) * top_w[..., None], axis=-2)
            ye = jax.nn.silu(jnp.einsum('bsd,eod->bseo', x1, expert_w) + expert_b)
            combined = jnp.einsum('bse,bseo->bso', rw, ye)
            moe_out = jnp.einsum('bsd,od->bso', combined, out_w) + out_b
            h = _rmsnorm(x1 + moe_out, norm_w)
            ff = jax.nn.gelu(jnp.einsum('bsd,hd->bsh', h, ff_down_w) + ff_down_b, approximate=False)
            ff = jnp.einsum('bsh,dh->bsd', ff, ff_up_w) + ff_up_b
            return h + ff
        return _forward(x, dw_kernel, dw_bias, pw_w, pw_b, router_w, router_b, expert_w, expert_b, out_w, out_b, norm_w, ff_down_w, ff_down_b, ff_up_w, ff_up_b)

    def _L3_attn_ref(x, W_down, tokeys, toqueries, tovalues, W_unify, b_unify):
        import jax, jax.numpy as jnp
        import numpy as np
        EMB, HEADS = (128, 16)
        S = EMB // HEADS
        b, t, e = x.shape
        h, s = (HEADS, S)
        scale = s ** (-0.25)
        xd = (x @ W_down).reshape(b, t, h, s)
        keys = jnp.einsum('bthk,hik->bthi', xd, tokeys) * scale
        queries = jnp.einsum('bthk,hik->bthi', xd, toqueries) * scale
        values = jnp.einsum('bthk,hik->bthi', xd, tovalues)
        dot = jnp.einsum('bqhs,bkhs->bhqk', queries, keys)
        attn = jax.nn.softmax(dot, axis=-1)
        out = jnp.einsum('bhqk,bkhs->bqhs', attn, values).reshape(b, t, e)
        return out @ W_unify + b_unify

    def _L3_xattn_ref(q, k, v, mask, Wq, Wk, Wv, Wo):
        import jax, jax.numpy as jnp
        import numpy as np
        HEADS = 16
        D_MODEL = 128
        D_K = D_MODEL // HEADS
        B, S = (2, 256)
        NEG = -1000000000.0
        b, s, _ = q.shape

        def proj(x, W):
            return (x @ W.T).reshape(b, -1, HEADS, D_K).transpose(0, 2, 1, 3)
        qh, kh, vh = (proj(q, Wq), proj(k, Wk), proj(v, Wv))
        att = jnp.einsum('bhqd,bhkd->bhqk', qh, kh) / jnp.sqrt(jnp.float32(D_K))
        att = jnp.where(mask, NEG, att)
        att = jax.nn.softmax(att, axis=-1)
        out = jnp.einsum('bhqk,bhkd->bhqd', att, vh)
        out = out.transpose(0, 2, 1, 3).reshape(b, -1, D_MODEL)
        return out @ Wo.T

    def _L3_ffn_ref(x, shared_gate, shared_up, shared_down, routed_gate, routed_up, routed_down, Wr, routing_bias):
        import jax, jax.numpy as jnp
        import numpy as np
        DIM = 128
        HID = 352
        N_ROUTED = 7
        TOPK = 2
        B, S = (4, 256)

        def _expert(x, wg, wu, wd):
            return jax.nn.silu(x @ wg) * (x @ wu) @ wd
        b, s, d = x.shape
        n_exp = routed_gate.shape[0]
        shared_out = _expert(x, shared_gate, shared_up, shared_down)
        logits = x @ Wr * routing_bias
        probs = jax.nn.sigmoid(logits)
        scores, idx = jax.lax.top_k(probs, TOPK)
        scores = scores / scores.sum(-1, keepdims=True)
        t = b * s
        xf = x.reshape(t, d)
        weights = jnp.zeros((t, n_exp), x.dtype).at[jnp.arange(t)[:, None], idx.reshape(t, TOPK)].add(scores.reshape(t, TOPK))
        combined = jnp.zeros_like(xf)
        for e in range(n_exp):
            combined = combined + _expert(xf, routed_gate[e], routed_up[e], routed_down[e]) * weights[:, e:e + 1]
        return shared_out + combined.reshape(b, s, d)
    x = _layernorm(x + _L0_attn_ref(x, L0_attn_Wq, L0_attn_bq, L0_attn_Wk, L0_attn_bk, L0_attn_Wv, L0_attn_bv, L0_attn_Wo, L0_attn_bo), axis=-1)
    x = _layernorm(x + _L0_xattn_ref(ctx_1024, x, L0_xattn_Wq, L0_xattn_bq, L0_xattn_Wk, L0_xattn_bk, L0_xattn_Wv, L0_xattn_bv, L0_xattn_gamma, L0_xattn_beta), axis=-1)
    x = _layernorm(x + _L0_ffn_ref(x, L0_ffn_w1_w, L0_ffn_w1_s, L0_ffn_w2_w, L0_ffn_w2_s, L0_ffn_h1_w, L0_ffn_h1_s, L0_ffn_h2_w, L0_ffn_h2_s, L0_ffn_w3_w, L0_ffn_w3_s), axis=-1)
    x = _layernorm(x + _L1_attn_ref(x, L1_attn_W_in, L1_attn_conv_w, L1_attn_conv_b, L1_attn_W_x, L1_attn_W_dt, L1_attn_b_dt, L1_attn_A_log, L1_attn_D, L1_attn_W_out), axis=-1)
    x = _layernorm(x + _L1_xattn_ref(x, ctx_1024, ctx_1024, mask_BxSxS2_ik1, L1_xattn_Wq, L1_xattn_bq, L1_xattn_Wk, L1_xattn_bk, L1_xattn_Wv, L1_xattn_bv, L1_xattn_Wo, L1_xattn_bo), axis=-1)
    x = _layernorm(x + _L1_ffn_ref(x, L1_ffn_w_q, L1_ffn_w_k, L1_ffn_w_gate, L1_ffn_value_experts, L1_ffn_output_experts), axis=-1)
    x = _layernorm(x + _L2_attn_ref(x, L2_attn_w_q, L2_attn_w_kv, L2_attn_w_o, L2_attn_k_weights), axis=-1)
    x = _layernorm(x + _L2_xattn_ref(x, ctx_1024, ctx_1024, L2_xattn_Wq, L2_xattn_bq, L2_xattn_Wk, L2_xattn_bk, L2_xattn_Wv, L2_xattn_bv, L2_xattn_Wo, L2_xattn_bo), axis=-1)
    x = _layernorm(x + _L2_ffn_ref(x, L2_ffn_dw_kernel, L2_ffn_dw_bias, L2_ffn_pw_w, L2_ffn_pw_b, L2_ffn_router_w, L2_ffn_router_b, L2_ffn_expert_w, L2_ffn_expert_b, L2_ffn_out_w, L2_ffn_out_b, L2_ffn_norm_w, L2_ffn_ff_down_w, L2_ffn_ff_down_b, L2_ffn_ff_up_w, L2_ffn_ff_up_b), axis=-1)
    x = _layernorm(x + _L3_attn_ref(x, L3_attn_W_down, L3_attn_tokeys, L3_attn_toqueries, L3_attn_tovalues, L3_attn_W_unify, L3_attn_b_unify), axis=-1)
    x = _layernorm(x + _L3_xattn_ref(x, ctx_1024, ctx_1024, mask_Bx1xSxS2_bk1, L3_xattn_Wq, L3_xattn_Wk, L3_xattn_Wv, L3_xattn_Wo), axis=-1)
    x = _layernorm(x + _L3_ffn_ref(x, L3_ffn_shared_gate, L3_ffn_shared_up, L3_ffn_shared_down, L3_ffn_routed_gate, L3_ffn_routed_up, L3_ffn_routed_down, L3_ffn_Wr, L3_ffn_routing_bias), axis=-1)
    return x

_drawn_inputs = setup_inputs


def setup_inputs(seed=0):
    import zlib

    import numpy as np

    out = dict(_drawn_inputs(seed))
    spreads = {'L0_xattn_gamma': (1.0, 0.2),
     'L0_xattn_beta': (0.0, 0.1),
     'L1_attn_conv_b': (0.0, 0.473),
     'L1_attn_b_dt': (-4.600166320800781, 0.6),
     'L1_attn_D': (1.0, 0.2),
     'L1_xattn_bq': (0.0, 0.385),
     'L1_xattn_bk': (0.0, 0.8),
     'L1_xattn_bv': (0.0, 0.1),
     'L1_xattn_bo': (0.0, 0.1),
     'L2_ffn_dw_bias': (0.0, 0.8),
     'L2_ffn_pw_b': (0.0, 0.409),
     'L2_ffn_router_b': (0.0, 0.8),
     'L2_ffn_expert_b': (0.0, 0.8),
     'L2_ffn_out_b': (0.0, 0.1),
     'L2_ffn_norm_w': (1.0, 0.2),
     'L2_ffn_ff_down_b': (0.0, 0.8),
     'L2_ffn_ff_up_b': (0.0, 0.1)}
    factors = {'L0_attn_Wq': 8.0,
     'L0_attn_bq': 8.0,
     'L0_attn_Wk': 8.0,
     'L0_attn_bk': 8.0,
     'L0_attn_Wv': 8.0,
     'L0_attn_bv': 8.0,
     'L0_attn_Wo': 8.0,
     'L0_xattn_bq': 3.548,
     'L0_xattn_bk': 8.0,
     'L0_xattn_bv': 2.991,
     'L0_ffn_w1_w': 8.0,
     'L0_ffn_w1_s': 8.0,
     'L0_ffn_w2_w': 8.0,
     'L0_ffn_w2_s': 8.0,
     'L0_ffn_h1_w': 8.0,
     'L0_ffn_h1_s': 8.0,
     'L0_ffn_h2_w': 8.0,
     'L0_ffn_h2_s': 8.0,
     'L0_ffn_w3_w': 8.0,
     'L0_ffn_w3_s': 8.0,
     'L1_attn_W_dt': 5.003,
     'L1_attn_A_log': 3.616,
     'L1_ffn_w_q': 8.0,
     'L1_ffn_w_k': 8.0,
     'L1_ffn_w_gate': 8.0,
     'L1_ffn_value_experts': 8.0,
     'L1_ffn_output_experts': 8.0,
     'L2_attn_k_weights': 8.0,
     'L2_xattn_bq': 8.0,
     'L2_xattn_bk': 8.0,
     'L2_xattn_bv': 6.809,
     'L2_xattn_bo': 6.882,
     'L2_ffn_dw_kernel': 8.0,
     'L2_ffn_pw_w': 8.0,
     'L2_ffn_router_w': 8.0,
     'L2_ffn_expert_w': 7.731,
     'L2_ffn_out_w': 7.526,
     'L2_ffn_ff_down_w': 8.0,
     'L2_ffn_ff_up_w': 8.0,
     'L3_attn_W_down': 8.0,
     'L3_attn_tokeys': 8.0,
     'L3_attn_toqueries': 8.0,
     'L3_attn_tovalues': 8.0,
     'L3_attn_W_unify': 8.0,
     'L3_attn_b_unify': 3.445,
     'L3_ffn_shared_gate': 6.149,
     'L3_ffn_shared_up': 6.175,
     'L3_ffn_shared_down': 6.27,
     'L3_ffn_routed_gate': 8.0,
     'L3_ffn_routed_up': 8.0,
     'L3_ffn_routed_down': 8.0,
     'L3_ffn_Wr': 8.0,
     'L3_ffn_routing_bias': 8.0}
    for name, (base, spread) in spreads.items():
        noise = np.random.default_rng([zlib.crc32(name.encode()), seed]).standard_normal(out[name].shape)
        drawn = base * np.exp(spread * noise) if base else spread * noise
        out[name] = jnp.asarray(drawn.astype(out[name].dtype))
    for name, factor in factors.items():
        out[name] = (out[name] * factor).astype(out[name].dtype)
    return out
```

```python
from contextlib import ExitStack, contextmanager

import numpy as np
import concourse.bass as bass
from concourse import mybir

F32 = mybir.dt.float32
BF16 = mybir.dt.bfloat16
I32 = mybir.dt.int32
U8 = mybir.dt.uint8
ACT = mybir.ActivationFunctionType
ALU = mybir.AluOpType
AX = mybir.AxisListType

P = 128
BATCH, SEQ, CTX, D = 4, 512, 154, 128
NT = SEQ // P
KT2 = CTX // 2
H, DH = 16, 8
PARTS = 3
TERMS = PARTS * PARTS
ROWS = TERMS * DH
MASKED = -float(2 ** 40)
EPS = 1e-5
PB = 3


SMALL = ["wq", "wk", "wv", "wo", "bv", "bo", "bq", "bk"]
RESIDENT = {}
for _a in ("L0a", "L0x", "L1x", "L2x", "L3a", "L3x"):
    RESIDENT[_a] = [(n, 1 if n in ("bq", "bk") else D) for n in SMALL]
RESIDENT["L0a"] += [("cos", SEQ), ("sin", SEQ), ("rot", D)]
RESIDENT["L0x"] += [("gamma", D), ("beta", D)]
RESIDENT["L1m"] = [("w_in", 512), ("w_x", 80), ("w_dt", 256), ("w_out", 256), ("conv", 8), ("cb", 2), ("bdt", 2),
                   ("alog", 32), ("dskip", 2)]
RESIDENT["L1g"] = [("wq", 512), ("wk", 512), ("gate", 64)]
RESIDENT["L2a"] = [("wq", 1024), ("wkv", 1024), ("wo", 1024), ("kw", 8)]
RESIDENT["L2f"] = [("conv", 3), ("cb", 1), ("pw", D), ("pwb", 1), ("router", 8), ("rb", 8), ("experts", 1024),
                   ("eb", 1024), ("out", D), ("ob", D), ("norm", D), ("down", 32), ("downb", 1), ("up", D), ("upb", D)]
RESIDENT["L3a"] += [("down", D)]
RESIDENT["L3f"] = [("wr", 7), ("rb", 7)]
HID = 352
HID_TILES = [(0, 128), (128, 128), (256, 96)]
EXPERTS3 = 8
STREAMED = {"L0f": [("w1", 512), ("w2", 512), ("h1", 2048), ("h2", 2048), ("w3", 512), ("s3", D),
                    ("s1", 4), ("s2", 4), ("t1", 4), ("t2", 4)],
            "L1e": [("value", 4096), ("output", 4096)],
            "L3e": [("gate", 8 * HID), ("up", 8 * HID), ("down", 8 * 3 * D)]}
CONSTS = [("ident", P), ("desc", 8), ("half", 8), ("one", P)]


def columns(groups):
    at, out = 0, {}
    for g, items in groups.items():
        for n, c in items:
            out[g, n] = (at, c)
            at += c
    return out, at


R_AT, R_N = columns({"const": CONSTS} | RESIDENT)
S_AT = {g: columns({g: items}) for g, items in STREAMED.items()}
S_N = max(n for _, n in S_AT.values())
GROUPS = ["const"] + list(RESIDENT)
B_CONSTS = [("ident", P), ("tri", P), ("triT", P), ("sel", 4 * P), ("selhe", 4 * 8 * P)]
B_AT, B_N = columns({"b": B_CONSTS})


@contextmanager
def phase(k, *names):
    nc = k.nc

    assert len(names) <= len(k.pool), (len(names), len(k.pool))
    s = dict(zip(names, k.pool))
    with nc.Block() as block:
        yield block, s
    used = k.pool[:len(names)]
    nc.sync.sem_clear(range(used[0].num, used[-1].num + 1))
    nc.all_engine_barrier()


class Chain:

    def __init__(self, eng, sem):
        self.eng, self.sem, self.n = eng, sem, 0

    def __call__(self, ins):
        ins.then_inc(self.sem, 1)
        self.n += 1
        self.eng.wait_ge(self.sem, self.n)


def w(k, group, name, rows=P):
    at, n = R_AT[group, name]
    return k.weights[0:rows, at:at + n]


def ws(k, group, name, rows=P):
    at, n = S_AT[group][0][group, name]
    return k.stream[0:rows, at:at + n]


def wb(k, name, rows=P):
    at, n = B_AT["b", name]
    return k.bconst[0:rows, at:at + n]


def norm_vector(k, dve, chain, s, y, bias=None):
    chain(dve.tensor_tensor(k.resid[:, :, :], y, k.x[:, :, :], ALU.add))
    norm_stats(k, dve, chain, s["var_ready"], s["rstd_ready"], 1)
    for t in range(NT):
        last = dve.tensor_scalar(k.x[:, t, :], k.resid[:, t, :], k.mv[:, t, 0:1], k.rstd[:, t:t + 1],
                                 ALU.subtract, ALU.mult)
    last.then_inc(s["x_ready"], 1)


def norm_stats(k, dve, chain, var_ready, rstd_ready, n):
    for t in range(NT):
        last = dve.bn_stats(k.stats[:, t, :], k.resid[:, t, :])
    chain(last)
    for t in range(NT):
        last = dve.bn_aggr(k.mv[:, t, :], k.stats[:, t, :])
    last.then_inc(var_ready, 1)
    dve.wait_ge(rstd_ready, n)


def norm_gpsimd(k, pool, s, n=1, eps=EPS):
    pool.wait_ge(s["var_ready"], n)
    pool.tensor_scalar(k.vareps[:, :], k.mv[:, :, 1], eps, None, ALU.add).then_inc(s["eps_added"], 1)
    pool.wait_ge(s["eps_added"], n)
    pool.tensor_tensor(k.rstd[:, :], k.vareps[:, :], k.minus_half, ALU.pow).then_inc(s["rstd_ready"], 1)


def norm_tensor(k, pe, s, bank):
    pe.wait_ge(s["x_ready"], 1)
    for t in range(NT):
        last = pe.transpose(k.ps[:, bank, t * P:(t + 1) * P], k.x[:, t, :], k.ident)
    last.then_inc(s["xT_ready"], 1)


def norm_scalar(k, act, s, bank):
    act.wait_ge(s["xT_ready"], 1)
    act.copy(k.xT[:, :], k.ps[:, bank, :])


NORM_SEMS = ("var_ready", "eps_added", "rstd_ready", "x_ready", "xT_ready")


def small_attention(k, name, scale, keys, kv_rows, q_src, kv_src, biased=True, v_biased=True, masks=None,
                    scrambled=False, feed=None):
    nc, ps = k.nc, k.ps
    NK = keys // kv_rows
    self_ = keys == SEQ
    with ExitStack() as ctx:
        def sb(n, shape, dt):
            return ctx.enter_context(nc.sbuf_tensor(f"{name}_{n}", shape, dt))

        qs = sb("qs", [ROWS + PARTS, H, SEQ], BF16)
        ks = sb("ks", [ROWS + PARTS, H, keys], BF16)
        v = sb("v", [P, NK, H, DH + 1], F32)
        z = sb("z", [P, NT, H, DH + 1], F32)
        probs = sb("probs", [P, PB, NK, SEQ], F32)
        if masks:
            mask_q = sb("mask_q", [P, NT, CTX], BF16)
            mask_k = sb("mask_k", [KT2, 2, SEQ], BF16)

        with ExitStack() as inner:
            def sbi(n, shape, dt):
                return inner.enter_context(nc.sbuf_tensor(f"{name}_{n}", shape, dt))

            qf = sbi("qf", [P, SEQ], F32)
            kf = sbi("kf", [P, keys], F32)
            rq = sbi("rq", [P, SEQ], F32)
            rk = sbi("rk", [P, keys], F32)
            qp = sbi("qp", [P, PARTS, SEQ], BF16)
            kp = sbi("kp", [P, PARTS, keys], BF16)
            if masks:
                wide_q = sbi("raw_q", [P, masks[0].shape[2]], I32)
                wide_k = sbi("raw_k", [KT2, masks[1].shape[2]], I32)
                raw_q, raw_k = wide_q[:, :], wide_k[:, :]
                if masks[0].shape[2] != NT * CTX:
                    raw_q, raw_k = raw_q.bitcast(U8), raw_k.bitcast(U8)
                raw_q = raw_q.rearrange("p (t k) -> p t k", t=NT)
                raw_k = raw_k.rearrange("p (t q) -> p t q", t=2)
            if feed:
                feed(k, sbi)

            with phase(k, "chain", "q_proj", "k_proj", "v_proj", "q_sb", "k_sb", "q_parts", "k_parts", "stacked",
                       "ones", "masks_in", "source", "rot") as (block, s):
                @block.tensor
                def _(pe):
                    if name == "L0a":
                        pe.matmul(ps[:, 7, :], w(k, name, "rot"), k.xT[:, :], start=True, stop=True).then_inc(s["rot"], 1)
                        pe.wait_ge(s["source"], 1)
                    if name == "L3a":
                        pe.matmul(ps[:, 7, :], w(k, name, "down"), k.xT[:, :], start=True, stop=True).then_inc(s["rot"], 1)
                        pe.wait_ge(s["source"], 1)
                    pe.matmul(ps[:, 0, :], w(k, name, "wq"), q_src[:, :], start=True, stop=True).then_inc(s["q_proj"], 1)
                    pe.matmul(ps[:, 1, 0:keys], w(k, name, "wk"), kv_src[:, :], start=True, stop=True
                              ).then_inc(s["k_proj"], 1)
                    for t in range(NK):
                        last = pe.matmul(ps[0:kv_rows, 2, t * D:(t + 1) * D], kv_src[:, t * kv_rows:(t + 1) * kv_rows],
                                         w(k, name, "wv"), start=True, stop=True)
                    last.then_inc(s["v_proj"], 1)

                @block.scalar
                def _(act):
                    if name == "L3a":
                        act.wait_ge(s["rot"], 1)
                        act.copy(k.src[:, :], ps[:, 7, :]).then_inc(s["source"], 1)
                    act.wait_ge(s["q_proj"], 1)
                    qin, qout = ps[:, 0, :], qf[:, :]
                    if scrambled:
                        qin = ps[:, 0, :].rearrange("p (hi lo) -> p lo hi", lo=16)
                        qout = qf[:, :].rearrange("p (lo hi) -> p lo hi", lo=16)
                    act.activation(qout, qin, ACT.Identity, bias=w(k, name, "bq") if biased else 0.0
                                   ).then_inc(s["q_sb"], 1)
                    act.wait_ge(s["k_proj"], 1)
                    act.activation(kf[:, :], ps[:, 1, 0:keys], ACT.Identity, bias=w(k, name, "bk") if biased else 0.0
                                   ).then_inc(s["k_sb"], 1)

                @block.vector
                def _(dve):
                    chain = Chain(dve, s["chain"])
                    if name == "L0a":
                        chain(dve.tensor_tensor(rq[:, :], k.xT[:, :], w(k, name, "cos"), ALU.mult))
                        dve.wait_ge(s["rot"], 1)
                        chain(dve.tensor_tensor(qf[:, :], ps[:, 7, :], w(k, name, "sin"), ALU.mult))
                        chain(dve.tensor_tensor(k.src[:, :], rq[:, :], qf[:, :], ALU.add))
                        dve.memset(v[:, :, :, DH:DH + 1], 1.0).then_inc(s["source"], 1)
                    else:
                        dve.memset(v[:, :, :, DH:DH + 1], 1.0)
                    for full, rest, parts, ready, done in ((qf, rq, qp, s["q_sb"], s["q_parts"]),
                                                           (kf, rk, kp, s["k_sb"], s["k_parts"])):
                        dve.wait_ge(ready, 1)
                        chain(dve.tensor_copy(parts[:, 0, :], full[:, :]))
                        chain(dve.tensor_tensor(rest[:, :], full[:, :], parts[:, 0, :], ALU.subtract))
                        chain(dve.tensor_copy(parts[:, 1, :], rest[:, :]))
                        dve.tensor_tensor(parts[:, 2, :], rest[:, :], parts[:, 1, :], ALU.subtract).then_inc(done, 1)
                    dve.wait_ge(s["v_proj"], 1)
                    for t in range(NK):
                        out = v[0:kv_rows, t, :, 0:DH]
                        pv = ps[0:kv_rows, 2, t * D:(t + 1) * D].rearrange("p (h d) -> p h d", h=H)
                        if v_biased:
                            dve.tensor_tensor(out, pv, w(k, name, "bv", kv_rows).rearrange("p (h d) -> p h d", h=H),
                                              ALU.add)
                        else:
                            dve.tensor_copy(out, pv)
                    if masks:
                        dve.wait_ge(s["masks_in"], 32)
                        dve.tensor_scalar(mask_q[:, :, :], raw_q, 0.0, MASKED, masks[2], ALU.mult)
                        dve.tensor_scalar(mask_k[:, :, :], raw_k, 0.0, MASKED, masks[2], ALU.mult)

                @block.gpsimd
                def _(pool):
                    pool.memset(ks[64:ROWS + PARTS, :, :], 1.0).then_inc(s["ones"], 1)

                @block.sync
                def _(sp):
                    if masks:
                        sp.dma_start(wide_q[:, :], masks[0][bass.ds(k.b, 1)].rearrange("o p k -> p (o k)")
                                     ).then_inc(s["masks_in"], 16)
                        sp.dma_start(wide_k[:, :], masks[1][bass.ds(k.b, 1)].rearrange("o p q -> p (o q)")
                                     ).then_inc(s["masks_in"], 16)
                    sp.wait_ge(s["q_parts"], 1)
                    for t in range(TERMS):
                        sp.dma_start(qs[DH * t:DH * (t + 1), :, :], qp[:, t // PARTS, :]).then_inc(s["stacked"], 16)
                    sp.wait_ge(s["k_parts"], 1)
                    sp.wait_ge(s["ones"], 1)
                    for t in range(TERMS):
                        sp.dma_start(ks[DH * t:DH * (t + 1), :, :], kp[:, t % PARTS, :]).then_inc(s["stacked"], 16)
                    sp.wait_ge(s["stacked"], 16 * 2 * TERMS)

        attend(k, name, scale, keys, kv_rows, NK, self_, qs, ks, v, z, probs,
               (mask_q, mask_k) if masks else None, sb)
        small_output(k, name, z, scrambled, sb, biased=name not in ("L3x",))


def attend(k, name, scale, keys, kv_rows, NK, self_, qs, ks, v, z, probs, masks, sb):
    nc, ps = k.nc, k.ps
    G = 4
    LOOK = 6
    UNITS = 2 if self_ else 1
    negmax = sb("negmax", [P, NT, H], F32)
    rest = sb("rest", [P, H // G, 2, NT, G], F32)
    mparts = sb("mparts", [P, H // G, NT, PARTS, G], BF16)
    mt = sb("mt", [PARTS * G, H // G, SEQ], BF16)
    mt_ps = ps[:, 7, :].bitcast(BF16)

    def unit_banks(i):
        return 2 * (i % 2)

    with phase(k, "chain", "scores", "maxed", "split", "mt_ready", "mt_sb", "mt_row", "scoresT", "exped", "head_done",
               "z_out") as (block, s):
        @block.tensor
        def _(pe):
            def scores(h, qt):
                i, t = h * UNITS + qt * UNITS // NT, qt % (NT // UNITS)
                if t == 0 and i >= 2:
                    pe.wait_ge(s["maxed"], i - 1)
                bank, at = (t, 0) if self_ else (t // 2, 256 * (t % 2))
                out = ps[:, unit_banks(i) + bank, at:at + keys]
                last = pe.matmul(out, qs[0:ROWS, h, qt * P:(qt + 1) * P], ks[0:ROWS, h, :], start=True, stop=not masks)
                if masks:
                    last = pe.matmul(out, wb(k, "ident"), masks[0][:, qt, :], start=False, stop=True)
                if t == NT // UNITS - 1:
                    last.then_inc(s["scores"], 1)

            def turn_maxima(g):
                pe.wait_ge(s["split"], g + 1)
                if g:
                    pe.wait_ge(s["mt_sb"], g)
                for t in range(NT):
                    last = pe.transpose(mt_ps[0:PARTS * G, t * P:(t + 1) * P],
                                        mparts[:, g, t, :, :].rearrange("p a b -> p (a b)"), wb(k, "ident"))
                last.then_inc(s["mt_ready"], 1)

            def scores_turned(h, t):
                if h % G == 0 and t == 0:
                    pe.wait_ge(s["mt_row"], 16 * (h // G + 1))
                i = h * NK + t
                if i >= 2:
                    pe.wait_ge(s["exped"], i - 1)
                out = ps[0:kv_rows, 4 + i % 2, :]
                last = pe.matmul(out, ks[:, h, t * kv_rows:(t + 1) * kv_rows], qs[:, h, :], start=True, stop=not masks)
                if masks:
                    last = pe.matmul(out, wb(k, "ident")[0:KT2, 0:KT2], masks[1][:, t, :], start=False, stop=True)
                last.then_inc(s["scoresT"], 1)

            def weigh(h, qt):
                if qt == 0:
                    pe.wait_ge(s["exped"], (h + 1) * NK)
                    if h % G == 0 and h:
                        pe.wait_ge(s["z_out"], h // G)
                at = (qt * G + h % G) * (DH + 1)
                for t in range(NK):
                    last = pe.matmul(ps[:, 6, at:at + DH + 1], probs[0:kv_rows, h % PB, t, qt * P:(qt + 1) * P],
                                     v[0:kv_rows, t, h, :], start=t == 0, stop=t == NK - 1)
                if qt == NT - 1:
                    last.then_inc(s["head_done"], 1)

            for step in range(-LOOK, H + 2):
                if (step + LOOK) % G == 0 and 0 < step + LOOK <= H:
                    turn_maxima((step + LOOK) // G - 1)
                for t in range(NT):
                    if step + LOOK < H:
                        scores(step + LOOK, t)
                    if 0 <= step < H and t < NK:
                        scores_turned(step, t)
                    h, qt = (step - 1, t - 1) if t else (step - 2, NT - 1)
                    if 0 <= h < H:
                        weigh(h, qt)

        @block.vector
        def _(dve):
            chain = Chain(dve, s["chain"])

            def maxima(h):
                for u in range(UNITS):
                    i = h * UNITS + u
                    dve.wait_ge(s["scores"], i + 1)
                    b = unit_banks(i)
                    if self_:
                        src, out = ps[:, b:b + 2, 0:keys], negmax[:, 2 * u:2 * u + 2, h]
                    else:
                        src = ps[:, b:b + 2, :].rearrange("p b (t k) -> p b t k", t=2)[:, :, :, 0:keys]
                        out = negmax[:, :, h].rearrange("p (b t) -> p b t", t=2)
                    last = dve.tensor_reduce(out, src, AX.X, ALU.max, negate=True)
                    last.then_inc(s["maxed"], 1)

            def split(g):
                m = negmax[:, :, g * G:(g + 1) * G]
                dve.wait_ge(s["maxed"], (g + 1) * G * UNITS)
                chain(dve.tensor_copy(mparts[:, g, :, 0, :], m))
                chain(dve.tensor_tensor(rest[:, g, 0], m, mparts[:, g, :, 0, :], ALU.subtract))
                chain(dve.tensor_copy(mparts[:, g, :, 1, :], rest[:, g, 0]))
                dve.tensor_tensor(mparts[:, g, :, 2, :], rest[:, g, 0], mparts[:, g, :, 1, :], ALU.subtract
                                  ).then_inc(s["split"], 1)

            def copy_out(g):
                dve.wait_ge(s["head_done"], (g + 1) * G)
                dve.tensor_copy(z[:, :, g * G:(g + 1) * G, :],
                                ps[:, 6, 0:NT * G * (DH + 1)].rearrange("p (t h d) -> p t h d", t=NT, h=G)
                                ).then_inc(s["z_out"], 1)

            for step in range(-LOOK, H):
                h = step + LOOK
                if step >= 2 and (step - 2) % G == G - 1:
                    copy_out((step - 2) // G)
                if h < H:
                    maxima(h)
                    if h % G == G - 1:
                        split(h // G)
            copy_out(H // G - 1)

        @block.scalar
        def _(act):
            for step in range(-LOOK, H):
                if (step + LOOK) % G == 0 and 0 < step + LOOK <= H:
                    g = (step + LOOK) // G - 1
                    act.wait_ge(s["mt_ready"], g + 1)
                    act.copy(mt[:, g, :], mt_ps[0:PARTS * G, 0:SEQ]).then_inc(s["mt_sb"], 1)
                if step >= 0:
                    for t in range(NK):
                        i = step * NK + t
                        if step >= PB and t == 0:
                            act.wait_ge(s["head_done"], step - PB + 1)
                        act.wait_ge(s["scoresT"], i + 1)
                        act.activation(probs[0:kv_rows, step % PB, t, :], ps[0:kv_rows, 4 + i % 2, :], ACT.Exp,
                                       scale=scale).then_inc(s["exped"], 1)

        @block.sync
        def _(sp):
            for g in range(H // G):
                sp.wait_ge(s["mt_sb"], g + 1)
                sp.dma_start(qs[ROWS:ROWS + PARTS, g * G:(g + 1) * G, :], mt[:, g, :]).then_inc(s["mt_row"], 16)


def small_output(k, name, z, scrambled, sb, biased):
    nc, ps = k.nc, k.ps
    inv = sb("inv", [P, NT, H, 1], F32)
    zn = sb("zn", [P, NT, H, DH], F32)
    znT = sb("znT", [P, SEQ], F32)
    dec = sb("dec", [P, NT, D], F32)
    with phase(k, "chain", "zn_ready", "znT_ready", "znT_sb", "y_ready", *NORM_SEMS) as (block, s):
        @block.vector
        def _(dve):
            chain = Chain(dve, s["chain"])
            chain(dve.reciprocal(inv[:, :, :, :], z[:, :, :, DH:DH + 1]))
            last = dve.tensor_tensor(zn[:, :, :, :], z[:, :, :, 0:DH], inv[:, :, :, :].to_broadcast([P, NT, H, DH]),
                                     ALU.mult)
            last.then_inc(s["zn_ready"], 1)
            if not scrambled:
                dve.wait_ge(s["y_ready"], 1)
                norm_vector(k, dve, chain, s, ps[:, 1, :].rearrange("p (t d) -> p t d", t=NT))
                return
            dve.wait_ge(s["zn_ready"], 1)
            for a in range(4):
                for b in range(4):
                    src = zn[32 * a:32 * a + 32, :, b::4, :].rearrange("p j t d -> p t j d")
                    out = dec[32 * b:32 * b + 32, :, :].rearrange("p t (j a d) -> p t j a d", j=4, a=4)[:, :, :, a, :]
                    last = dve.tensor_copy(out, src)
            chain(last)
            chain(dve.tensor_tensor(k.resid[:, :, :], dec[:, :, :], k.x[:, :, :], ALU.add))
            norm_stats(k, dve, chain, s["var_ready"], s["rstd_ready"], 1)
            for t in range(NT):
                last = dve.tensor_scalar(dec[:, t, :], k.resid[:, t, :], k.mv[:, t, 0:1], k.rstd[:, t:t + 1],
                                         ALU.subtract, ALU.mult)
            chain(last)
            gamma = w(k, name, "gamma").unsqueeze(1).to_broadcast([P, NT, D])
            beta = w(k, name, "beta").unsqueeze(1).to_broadcast([P, NT, D])
            chain(dve.tensor_tensor(zn[:, :, :, :].rearrange("p t h d -> p t (h d)"), dec[:, :, :], gamma, ALU.mult))
            chain(dve.tensor_tensor(dec[:, :, :], zn[:, :, :, :].rearrange("p t h d -> p t (h d)"), beta, ALU.add))
            chain(dve.tensor_tensor(k.resid[:, :, :], dec[:, :, :], k.x[:, :, :], ALU.add))
            norm_stats(k, dve, chain, s["var_ready"], s["rstd_ready"], 2)
            for t in range(NT):
                last = dve.tensor_scalar(k.x[:, t, :], k.resid[:, t, :], k.mv[:, t, 0:1], k.rstd[:, t:t + 1],
                                         ALU.subtract, ALU.mult)
            last.then_inc(s["x_ready"], 1)

        @block.gpsimd
        def _(pool):
            norm_gpsimd(k, pool, s)
            if scrambled:
                norm_gpsimd(k, pool, s, 2)

        @block.tensor
        def _(pe):
            if not scrambled:
                pe.wait_ge(s["zn_ready"], 1)
                for t in range(NT):
                    last = pe.transpose(ps[:, 0, t * P:(t + 1) * P], zn[:, t, :, :].rearrange("p h d -> p (h d)"), k.ident)
                last.then_inc(s["znT_ready"], 1)
                pe.wait_ge(s["znT_sb"], 1)
                for t in range(NT):
                    last = pe.matmul(ps[:, 1, t * D:(t + 1) * D], znT[:, t * P:(t + 1) * P], w(k, name, "wo"),
                                     start=True, stop=not biased)
                    if biased:
                        last = pe.matmul(ps[:, 1, t * D:(t + 1) * D], w(k, "const", "one", 1), w(k, name, "bo", 1),
                                         start=False, stop=True)
                last.then_inc(s["y_ready"], 1)
            norm_tensor(k, pe, s, 2)

        @block.scalar
        def _(act):
            if not scrambled:
                act.wait_ge(s["znT_ready"], 1)
                act.copy(znT[:, :], ps[:, 0, :]).then_inc(s["znT_sb"], 1)
            norm_scalar(k, act, s, 2)


def gated_ffn(k, stream_loaded):
    nc, ps = k.nc, k.ps
    M = 4
    name = "L0f"
    w1, w2 = ws(k, name, "w1"), ws(k, name, "w2")
    h1w, h2w = (ws(k, name, n).rearrange("p (t o) -> p t o", t=M) for n in ("h1", "h2"))
    w3 = ws(k, name, "w3").rearrange("p (t o) -> p t o", t=M)
    with ExitStack() as ctx:
        a = ctx.enter_context(nc.sbuf_tensor("ffn_a", [P, M, SEQ], F32))
        g = ctx.enter_context(nc.sbuf_tensor("ffn_g", [P, M, SEQ], F32))
        y = ctx.enter_context(nc.sbuf_tensor("ffn_y", [P, NT, D], F32))
        with phase(k, "chain", "up_ready", "silu_ready", "prod_ready", "h1_ready", "h1_sb", "h2_ready", "h2_sb",
                   "y_ready", *NORM_SEMS) as (block, s):
            @block.tensor
            def _(pe):
                pe.wait_ge(stream_loaded, 16)
                for m in range(M):
                    if m >= 2:
                        pe.wait_ge(s["prod_ready"], m - 1)
                    b = 2 * (m % 2)
                    pe.matmul(ps[:, b, :], w1[:, m * P:(m + 1) * P], k.xT[:, :], start=True, stop=True)
                    pe.matmul(ps[:, b + 1, :], w2[:, m * P:(m + 1) * P], k.xT[:, :], start=True, stop=True
                              ).then_inc(s["up_ready"], 1)
                for src, wt, got, done, freed, b in ((a, h1w, s["prod_ready"], s["h1_ready"], s["h1_sb"], 4),
                                                     (g, h2w, s["h1_sb"], s["h2_ready"], s["h2_sb"], 6)):
                    for m in range(M):
                        if m >= 2:
                            pe.wait_ge(freed, m - 1)
                        for t in range(M):
                            if m == 0:
                                pe.wait_ge(got, t + 1)
                            last = pe.matmul(ps[:, b + m % 2, :], wt[:, t, m * P:(m + 1) * P], src[:, t, :],
                                             start=t == 0, stop=t == M - 1)
                        last.then_inc(done, 1)
                pe.wait_ge(s["h2_sb"], M)
                for t in range(NT):
                    for m in range(M):
                        last = pe.matmul(ps[:, 0, t * D:(t + 1) * D], a[:, m, t * P:(t + 1) * P], w3[:, m, :],
                                         start=m == 0, stop=m == M - 1)
                last.then_inc(s["y_ready"], 1)
                norm_tensor(k, pe, s, 1)

            @block.scalar
            def _(act):
                for m in range(M):
                    act.wait_ge(s["up_ready"], m + 1)
                    act.activation(g[:, m, :], ps[:, 2 * (m % 2), :], ACT.Silu, scale=ws(k, name, "s1")[:, m:m + 1]
                                   ).then_inc(s["silu_ready"], 1)
                for m in range(M):
                    act.wait_ge(s["h1_ready"], m + 1)
                    act.activation(g[:, m, :], ps[:, 4 + m % 2, :], ACT.Gelu, scale=ws(k, name, "t1")[:, m:m + 1]
                                   ).then_inc(s["h1_sb"], 1)
                for m in range(M):
                    act.wait_ge(s["h2_ready"], m + 1)
                    act.activation(a[:, m, :], ps[:, 6 + m % 2, :], ACT.Gelu, scale=ws(k, name, "t2")[:, m:m + 1]
                                   ).then_inc(s["h2_sb"], 1)
                norm_scalar(k, act, s, 1)

            @block.vector
            def _(dve):
                chain = Chain(dve, s["chain"])
                for m in range(M):
                    dve.wait_ge(s["silu_ready"], m + 1)
                    dve.scalar_tensor_tensor(out=a[:, m, :], in0=ps[:, 2 * (m % 2) + 1, :],
                                             scalar=ws(k, name, "s2")[:, m:m + 1], in1=g[:, m, :],
                                             op0=ALU.mult, op1=ALU.mult).then_inc(s["prod_ready"], 1)
                dve.wait_ge(s["y_ready"], 1)
                chain(dve.tensor_tensor(y[:, :, :], ps[:, 0, :].rearrange("p (t d) -> p t d", t=NT),
                                        ws(k, name, "s3").unsqueeze(1).to_broadcast([P, NT, D]), ALU.mult))
                norm_vector(k, dve, chain, s, y[:, :, :])

            @block.gpsimd
            def _(pool):
                norm_gpsimd(k, pool, s)


def mamba(k, next_stream):
    nc, ps = k.nc, k.ps
    name, J, N, R = "L1m", 2, 16, 8
    XD = R + 2 * N
    TAPS = 4
    conv = w(k, name, "conv").rearrange("p (j t) -> p j t", j=J)
    w_x = w(k, name, "w_x").rearrange("p (j n) -> p j n", j=J)
    w_dt = w(k, name, "w_dt", R)
    w_out = w(k, name, "w_out").rearrange("p (j n) -> p j n", j=J)
    with ExitStack() as ctx:
        def sb(n, shape, dt=F32):
            return ctx.enter_context(nc.sbuf_tensor(f"mamba_{n}", shape, dt))

        xc = sb("xc", [P, J, SEQ])
        sz = sb("sz", [P, J, SEQ])
        delta = sb("delta", [P, J, SEQ])
        du = sb("du", [P, J, SEQ])
        xd = sb("xd", [XD, SEQ])
        aneg = sb("aneg", [P, J * N])
        with ExitStack() as inner:
            def sbi(n, shape):
                return inner.enter_context(nc.sbuf_tensor(f"mamba_{n}", shape, F32))

            xpad = sbi("xpad", [P, J, SEQ + TAPS - 1])
            acc = sbi("acc", [P, J, SEQ])
            vv = sbi("v", [P, J, SEQ])
            low = sbi("low", [P, J, SEQ])
            u = sbi("u", [P, J, SEQ])
            w1 = sbi("w1", [P, J, SEQ])
            ln = sbi("ln", [P, J, SEQ])
            with phase(k, "chain", "xz", "xi_sb", "conv_done", "xc_sb", "xd_ready", "xd_sb", "dt_ready", "low_ready",
                       "u_ready", "w1_ready", "ln_ready", "a_ready", "padded") as (block, s):
                @block.sync
                def _(sp):
                    next_stream(sp)

                @block.tensor
                def _(pe):
                    for m in range(2 * J):
                        pe.matmul(ps[:, m, :], w(k, name, "w_in")[:, m * P:(m + 1) * P], k.xT[:, :], start=True,
                                  stop=True).then_inc(s["xz"], 1)
                    pe.wait_ge(s["xc_sb"], J)
                    for j in range(J):
                        last = pe.matmul(ps[0:XD, 4, :], w_x[:, j, :], xc[:, j, :], start=j == 0, stop=j == J - 1)
                    last.then_inc(s["xd_ready"], 1)
                    pe.wait_ge(s["xd_sb"], 1)
                    for j in range(J):
                        last = pe.matmul(ps[:, 5 + j, :], w_dt[:, j * P:(j + 1) * P], xd[0:R, :], start=True, stop=True)
                    last.then_inc(s["dt_ready"], 1)

                @block.scalar
                def _(act):
                    for j in range(J):
                        act.wait_ge(s["xz"], j + 1)
                        act.copy(xpad[:, j, TAPS - 1:], ps[:, j, :]).then_inc(s["xi_sb"], 1)
                    for j in range(J):
                        act.wait_ge(s["xz"], J + j + 1)
                        act.activation(sz[:, j, :], ps[:, J + j, :], ACT.Silu)
                    for j in range(J):
                        act.wait_ge(s["conv_done"], j + 1)
                        act.activation(xc[:, j, :], acc[:, j, :], ACT.Silu, bias=w(k, name, "cb")[:, j:j + 1]
                                       ).then_inc(s["xc_sb"], 1)
                    act.activation(aneg[:, :], w(k, name, "alog"), ACT.Exp).then_inc(s["a_ready"], 1)
                    act.wait_ge(s["xd_ready"], 1)
                    act.copy(xd[:, :], ps[0:XD, 4, :]).then_inc(s["xd_sb"], 1)
                    act.wait_ge(s["low_ready"], 1)
                    act.activation(u[:, :, :], low[:, :, :], ACT.Exp).then_inc(s["u_ready"], 1)
                    act.wait_ge(s["w1_ready"], 1)
                    act.activation(ln[:, :, :], w1[:, :, :], ACT.Ln).then_inc(s["ln_ready"], 1)

                @block.gpsimd
                def _(pool):
                    pool.memset(xpad[:, :, 0:TAPS - 1], 0.0).then_inc(s["padded"], 1)

                @block.vector
                def _(dve):
                    chain = Chain(dve, s["chain"])
                    dve.wait_ge(s["padded"], 1)
                    for j in range(J):
                        dve.wait_ge(s["xi_sb"], j + 1)
                        chain(dve.tensor_scalar(acc[:, j, :], xpad[:, j, 0:SEQ], conv[:, j, 0:1], None, ALU.mult))
                        for t in range(1, TAPS):
                            last = dve.scalar_tensor_tensor(out=acc[:, j, :], in0=xpad[:, j, t:t + SEQ],
                                                            scalar=conv[:, j, t:t + 1], in1=acc[:, j, :],
                                                            op0=ALU.mult, op1=ALU.add)
                            if t < TAPS - 1:
                                chain(last)
                        last.then_inc(s["conv_done"], 1)
                    dve.wait_ge(s["a_ready"], 1)
                    chain(dve.tensor_scalar(aneg[:, :], aneg[:, :], -1.0, None, ALU.mult))
                    dve.wait_ge(s["dt_ready"], 1)
                    for j in range(J):
                        last = dve.tensor_scalar(vv[:, j, :], ps[:, 5 + j, :], w(k, name, "bdt")[:, j:j + 1], None, ALU.add)
                    chain(last)
                    dve.scalar_tensor_tensor(out=low[:, :, :], in0=vv[:, :, :], scalar=-1.0, in1=vv[:, :, :],
                                             op0=ALU.mult, op1=ALU.min).then_inc(s["low_ready"], 1)
                    dve.wait_ge(s["u_ready"], 1)
                    dve.tensor_scalar(w1[:, :, :], u[:, :, :], 1.0, None, ALU.add).then_inc(s["w1_ready"], 1)
                    dve.wait_ge(s["w1_ready"], 1)
                    chain(dve.scalar_tensor_tensor(out=low[:, :, :], in0=w1[:, :, :], scalar=-1.0, in1=u[:, :, :],
                                                   op0=ALU.add, op1=ALU.subtract))
                    dve.wait_ge(s["ln_ready"], 1)
                    chain(dve.scalar_tensor_tensor(out=vv[:, :, :], in0=vv[:, :, :], scalar=0.0, in1=ln[:, :, :],
                                                   op0=ALU.max, op1=ALU.add))
                    chain(dve.tensor_tensor(delta[:, :, :], vv[:, :, :], low[:, :, :], ALU.subtract))
                    chain(dve.tensor_tensor(du[:, :, :], delta[:, :, :], xc[:, :, :], ALU.mult))

        RING = 4
        bsb = sb("b", [P, 2, SEQ])
        da = sb("da", [P, RING, SEQ])
        dbu = sb("dbu", [P, RING, SEQ])
        hs = sb("h", [P, 2, SEQ])
        hc = sb("hc", [P, RING, SEQ])
        y = sb("y", [P, J, SEQ])
        with phase(k, "chain", "bc_ready", "b_sb", "da_ready", "dbu_ready", "scanned", "hc_ready", "summed", "y_in",
                   "y_ready", *NORM_SEMS) as (block, s):
            @block.tensor
            def _(pe):
                def spread(n):
                    if n >= 2:
                        pe.wait_ge(s["b_sb"], n - 1)
                        pe.wait_ge(s["hc_ready"], J * (n - 1))
                    for c in range(2):
                        r = R + c * N + n
                        last = pe.matmul(ps[:, 2 * (n % 2) + c, :], k.ident[0:XD, r:r + 1].to_broadcast([XD, P]),
                                         xd[:, :], start=True, stop=True)
                    last.then_inc(s["bc_ready"], 1)

                spread(0)
                for n in range(N):
                    if n + 1 < N:
                        spread(n + 1)
                    for j in range(J):
                        pe.wait_ge(s["hc_ready"], J * n + j + 1)
                        pe.matmul(ps[:, 4 + j, :], k.ident, hc[:, (J * n + j) % RING, :], start=n == 0, stop=n == N - 1
                                  ).then_inc(s["summed"], 1)
                pe.wait_ge(s["y_in"], 1)
                for t in range(NT):
                    for j in range(J):
                        last = pe.matmul(ps[:, 0, t * D:(t + 1) * D], y[:, j, t * P:(t + 1) * P], w_out[:, j, :],
                                         start=j == 0, stop=j == J - 1)
                last.then_inc(s["y_ready"], 1)
                norm_tensor(k, pe, s, 1)

            @block.scalar
            def _(act):
                for n in range(N):
                    act.wait_ge(s["bc_ready"], n + 1)
                    if n >= 2:
                        act.wait_ge(s["dbu_ready"], J * (n - 1))
                    act.copy(bsb[:, n % 2, :], ps[:, 2 * (n % 2), :]).then_inc(s["b_sb"], 1)
                    for j in range(J):
                        i = J * n + j
                        if i >= RING:
                            act.wait_ge(s["scanned"], i - RING + 1)
                        act.activation(da[:, i % RING, :], delta[:, j, :], ACT.Exp, scale=aneg[:, j * N + n:j * N + n + 1]
                                       ).then_inc(s["da_ready"], 1)
                norm_scalar(k, act, s, 1)

            @block.gpsimd
            def _(pool):
                for n in range(N):
                    pool.wait_ge(s["b_sb"], n + 1)
                    for j in range(J):
                        i = J * n + j
                        if i >= RING:
                            pool.wait_ge(s["scanned"], i - RING + 1)
                        pool.tensor_tensor(dbu[:, i % RING, :], du[:, j, :], bsb[:, n % 2, :], ALU.mult
                                           ).then_inc(s["dbu_ready"], 1)
                norm_gpsimd(k, pool, s)

            @block.vector
            def _(dve):
                chain = Chain(dve, s["chain"])
                for n in range(N):
                    for j in range(J):
                        i = J * n + j
                        dve.wait_ge(s["da_ready"], i + 1)
                        dve.wait_ge(s["dbu_ready"], i + 1)
                        dve.tensor_tensor_scan(out=hs[:, i % 2, :], data0=da[:, i % RING, :], data1=dbu[:, i % RING, :],
                                               initial=0.0, op0=ALU.mult, op1=ALU.add).then_inc(s["scanned"], 1)
                        dve.wait_ge(s["scanned"], i + 1)
                        if i >= RING:
                            dve.wait_ge(s["summed"], i - RING + 1)
                        dve.tensor_tensor(hc[:, i % RING, :], hs[:, i % 2, :], ps[:, 2 * (n % 2) + 1, :], ALU.mult
                                          ).then_inc(s["hc_ready"], 1)
                dve.wait_ge(s["summed"], J * N)
                for j in range(J):
                    last = dve.scalar_tensor_tensor(out=y[:, j, :], in0=xc[:, j, :], scalar=w(k, name, "dskip")[:, j:j + 1],
                                                    in1=ps[:, 4 + j, :], op0=ALU.mult, op1=ALU.add)
                chain(last)
                dve.tensor_tensor(y[:, :, :], y[:, :, :], sz[:, :, :], ALU.mult).then_inc(s["y_in"], 1)
                dve.wait_ge(s["y_ready"], 1)
                norm_vector(k, dve, chain, s, ps[:, 0, :].rearrange("p (t d) -> p t d", t=NT))


WD = 64


def wide_attend(k, name, heads, scale, qT, kT, v, zn, sb):
    nc, ps = k.nc, k.ps
    G, LOOK, UNITS = 4, 6, 2
    negmax = sb("negmax", [P, NT, heads], F32)
    rest = sb("rest", [P, heads // G, NT, G], F32)
    mparts = sb("mparts", [P, heads // G, NT, PARTS, G], BF16)
    mt = sb("mt", [PARTS * G, 2, SEQ], BF16)
    probs = sb("probs", [P, PB, NT, SEQ], F32)
    inv = sb("inv", [P, 2, NT, 1], F32)
    mt_ps = ps[:, 7, :].bitcast(BF16)
    sel = wb(k, "sel", PARTS * G).rearrange("p (g n) -> p g n", g=G)
    with phase(k, "chain", "scores", "maxed", "split", "mt_ready", "mt_sb", "scoresT", "exped", "head_done",
               "z_out") as (block, s):
        @block.tensor
        def _(pe):
            def scores(h, qt):
                o = WD * (h % 2)
                i, t = h * UNITS + qt // 2, qt % 2
                if t == 0 and i >= 2:
                    pe.wait_ge(s["maxed"], i - 1)
                n = (qt + 1) * P
                bank = 2 * (i % 2) + t
                pe.matmul(ps[:, bank, 0:n], qT[o:o + WD, h // 2, qt * P:n], kT[o:o + WD, h // 2, 0:n],
                          start=True, stop=True)
                last = pe.matmul(ps[:, bank, qt * P:n], wb(k, "ident"), wb(k, "tri"), start=False, stop=True,
                                 skip_group_check=True)
                if t == 1:
                    last.then_inc(s["scores"], 1)

            def turn_maxima(g):
                pe.wait_ge(s["split"], g + 1)
                if g:
                    pe.wait_ge(s["mt_sb"], g)
                for t in range(NT):
                    last = pe.transpose(mt_ps[0:PARTS * G, t * P:(t + 1) * P],
                                        mparts[:, g, t, :, :].rearrange("p a b -> p (a b)"), wb(k, "ident"))
                last.then_inc(s["mt_ready"], 1)

            def scores_turned(h, t):
                o = WD * (h % 2)
                if h % G == 0 and t == 0:
                    pe.wait_ge(s["mt_sb"], h // G + 1)
                i = h * NT + t
                if i >= 2:
                    pe.wait_ge(s["exped"], i - 1)
                q0 = t * P
                bank = 4 + i % 2
                pe.matmul(ps[:, bank, q0:], kT[o:o + WD, h // 2, q0:q0 + P], qT[o:o + WD, h // 2, q0:],
                          start=True, stop=False)
                pe.matmul(ps[:, bank, q0:q0 + P], wb(k, "ident"), wb(k, "triT"), start=False, stop=False,
                          skip_group_check=True)
                pe.matmul(ps[:, bank, q0:], sel[:, h % G, :], mt[:, h // G % 2, q0:], start=False, stop=True
                          ).then_inc(s["scoresT"], 1)

            def weigh(h, qt):
                if qt == 0:
                    pe.wait_ge(s["exped"], (h + 1) * NT)
                    if h:
                        pe.wait_ge(s["z_out"], h)
                at = qt * (WD + 1)
                for t in range(qt + 1):
                    last = pe.matmul(ps[:, 6, at:at + WD + 1], probs[:, h % PB, t, qt * P:(qt + 1) * P], v[:, t, h, :],
                                     start=t == 0, stop=t == qt)
                if qt == NT - 1:
                    last.then_inc(s["head_done"], 1)

            for step in range(-LOOK, heads + 2):
                if (step + LOOK) % G == 0 and 0 < step + LOOK <= heads:
                    turn_maxima((step + LOOK) // G - 1)
                for t in range(NT):
                    if step + LOOK < heads:
                        scores(step + LOOK, t)
                    if 0 <= step < heads:
                        scores_turned(step, t)
                    h, qt = (step - 1, t - 1) if t else (step - 2, NT - 1)
                    if 0 <= h < heads:
                        weigh(h, qt)

        @block.vector
        def _(dve):
            chain = Chain(dve, s["chain"])

            def maxima(h):
                for u in range(UNITS):
                    i = h * UNITS + u
                    dve.wait_ge(s["scores"], i + 1)
                    for t in range(2):
                        qt = 2 * u + t
                        last = dve.tensor_reduce(negmax[:, qt, h:h + 1], ps[:, 2 * (i % 2) + t, 0:(qt + 1) * P], AX.X,
                                                 ALU.max, negate=True)
                    last.then_inc(s["maxed"], 1)

            def split(g):
                m = negmax[:, :, g * G:(g + 1) * G]
                dve.wait_ge(s["maxed"], (g + 1) * G * UNITS)
                chain(dve.tensor_copy(mparts[:, g, :, 0, :], m))
                chain(dve.tensor_tensor(rest[:, g], m, mparts[:, g, :, 0, :], ALU.subtract))
                chain(dve.tensor_copy(mparts[:, g, :, 1, :], rest[:, g]))
                dve.tensor_tensor(mparts[:, g, :, 2, :], rest[:, g], mparts[:, g, :, 1, :], ALU.subtract
                                  ).then_inc(s["split"], 1)

            def normalize(h):
                dve.wait_ge(s["head_done"], h + 1)
                out = ps[:, 6, 0:NT * (WD + 1)].rearrange("p (t d) -> p t d", t=NT)
                chain(dve.reciprocal(inv[:, h % 2], out[:, :, WD:WD + 1]))
                dve.tensor_tensor(zn[:, :, h, :], out[:, :, 0:WD], inv[:, h % 2].to_broadcast([P, NT, WD]), ALU.mult
                                  ).then_inc(s["z_out"], 1)

            for step in range(-LOOK, heads):
                h = step + LOOK
                if step >= 2:
                    normalize(step - 2)
                if h < heads:
                    maxima(h)
                    if h % G == G - 1:
                        split(h // G)
            normalize(heads - 2)
            normalize(heads - 1)

        @block.scalar
        def _(act):
            for step in range(-LOOK, heads):
                if (step + LOOK) % G == 0 and 0 < step + LOOK <= heads:
                    g = (step + LOOK) // G - 1
                    act.wait_ge(s["mt_ready"], g + 1)
                    if g >= 2:
                        act.wait_ge(s["scoresT"], (g - 1) * G * NT)
                    act.copy(mt[:, g % 2, :], mt_ps[0:PARTS * G, 0:SEQ]).then_inc(s["mt_sb"], 1)
                if step >= 0:
                    for t in range(NT):
                        i = step * NT + t
                        if step >= PB and t == 0:
                            act.wait_ge(s["head_done"], step - PB + 1)
                        act.wait_ge(s["scoresT"], i + 1)
                        act.activation(probs[:, step % PB, t, t * P:], ps[:, 4 + i % 2, t * P:], ACT.Exp, scale=scale
                                       ).then_inc(s["exped"], 1)


def top_one(k, dve, chain, values, key, best, picked, E):
    S4 = list(values.shape)
    chain(dve.tensor_reduce(best, values, AX.X, ALU.max))
    bc = lambda a: a.to_broadcast(S4)
    chain(dve.tensor_tensor(key, values, bc(best), ALU.is_equal))
    desc = w(k, "const", "desc")[:, 0:E].unsqueeze(1).to_broadcast([P, S4[1], E])
    chain(dve.tensor_tensor(key, key, desc, ALU.mult))
    return key


def expert_attention(k, stream_loaded):
    nc, ps = k.nc, k.ps
    name, HE, E = "L1g", 8, 8
    PAIRS = HE // 2
    at, _ = S_AT["L1e"]
    value = k.stream[:, 0:4096].rearrange("p (e n) -> p e n", e=E)
    output = k.stream[:, 4096:8192].rearrange("p (e r d) -> p e r d", e=E, r=PAIRS)
    with ExitStack() as ctx:
        def sb(n, shape, dt=F32):
            return ctx.enter_context(nc.sbuf_tensor(f"moa_{n}", shape, dt))

        zn = sb("zn", [P, NT, HE, WD])
        gate = sb("gate", [P, NT * HE, 1])
        picked_b = sb("picked_b", [P, NT, HE * E], BF16)
        with ExitStack() as inner:
            def sbi(n, shape, dt=F32):
                return inner.enter_context(nc.sbuf_tensor(f"moa_{n}", shape, dt))

            qT = sbi("qT", [P, PAIRS, SEQ])
            kT = sbi("kT", [P, PAIRS, SEQ])
            v = sbi("v", [P, NT, HE, WD + 1])
            gates = sbi("gates", [P, NT * HE, E])
            key = sbi("key", [P, NT * HE, E])
            kmax = sbi("kmax", [P, NT * HE, 1])
            picked = sbi("picked", [P, NT, HE, E], I32)
            with phase(k, "chain", "qk", "qk_sb", "logits", "gates", "picked", "values", "chosen") as (block, s):
                @block.tensor
                def _(pe):
                    for t in range(NT):
                        last = pe.matmul(ps[:, 2, t * 64:(t + 1) * 64], k.xT[:, t * P:(t + 1) * P], w(k, name, "gate"),
                                         start=True, stop=True)
                    last.then_inc(s["logits"], 1)
                    for m in range(2 * PAIRS):
                        if m >= 2:
                            pe.wait_ge(s["qk_sb"], m - 1)
                        wt = w(k, name, "wq" if m % 2 == 0 else "wk")
                        pe.matmul(ps[:, m % 2, :], wt[:, m // 2 * P:(m // 2 + 1) * P], k.xT[:, :], start=True, stop=True
                                  ).then_inc(s["qk"], 1)
                    pe.wait_ge(stream_loaded, 16)
                    for e in range(E):
                        for t in range(NT):
                            i = e * NT + t
                            if i >= 4:
                                pe.wait_ge(s["chosen"], i - 3)
                            pe.matmul(ps[:, 4 + i % 4, :], k.xT[:, t * P:(t + 1) * P], value[:, e, :], start=True,
                                      stop=True).then_inc(s["values"], 1)

                @block.scalar
                def _(act):
                    act.wait_ge(s["logits"], 1)
                    act.activation(gates[:, :, :], ps[:, 2, 0:256].rearrange("p (a e) -> p a e", e=E), ACT.Sigmoid
                                   ).then_inc(s["gates"], 1)
                    for m in range(2 * PAIRS):
                        act.wait_ge(s["qk"], m + 1)
                        act.copy((qT if m % 2 == 0 else kT)[:, m // 2, :], ps[:, m % 2, :]).then_inc(s["qk_sb"], 1)

                @block.vector
                def _(dve):
                    chain = Chain(dve, s["chain"])
                    chain(dve.memset(v[:, :, :, :], 1.0))
                    dve.wait_ge(s["gates"], 1)
                    S3 = [P, NT * HE, E]
                    top_one(k, dve, chain, gates[:, :, :], key[:, :, :], gate[:, :, :], None, E)
                    chain(dve.tensor_reduce(kmax[:, :, :], key[:, :, :], AX.X, ALU.max))
                    pk = picked[:, :, :, :].rearrange("p t h e -> p (t h) e")
                    chain(dve.tensor_tensor(pk, key[:, :, :], kmax[:, :, :].to_broadcast(S3), ALU.is_equal))
                    chain(dve.tensor_copy(picked_b[:, :, :].rearrange("p t (h e) -> p (t h) e", e=E), pk))
                    for e in range(E):
                        for t in range(NT):
                            i = e * NT + t
                            dve.wait_ge(s["values"], i + 1)
                            if e:
                                dve.wait_ge(s["chosen"], i - NT + 1)
                            dve.copy_predicated(v[:, t, :, 0:WD], picked[:, t, :, e:e + 1].to_broadcast([P, HE, WD]),
                                                ps[:, 4 + i % 4, :].rearrange("p (h d) -> p h d", h=HE)
                                                ).then_inc(s["chosen"], 1)
                    dve.wait_ge(s["chosen"], NT * E)
                    for t in range(NT):
                        g = gate[:, t * HE:(t + 1) * HE, :].to_broadcast([P, HE, WD])
                        dve.tensor_tensor(v[:, t, :, 0:WD], v[:, t, :, 0:WD], g, ALU.mult)

            wide_attend(k, "L1g", HE, WD ** -0.5, qT, kT, v, zn,
                        lambda n, sh, dt: inner.enter_context(nc.sbuf_tensor(f"moa_{n}", sh, dt)))

        zT = sb("zT", [P, PAIRS, SEQ])
        pT = sb("pT", [HE * E, SEQ], BF16)
        RING = 4
        xm = sb("xm", [P, RING, SEQ])
        pT_ps = ps[:, 2, :].bitcast(BF16)
        with phase(k, "chain", "scaled", "zT_ready", "zT_sb", "pT_ready", "pT_sb", "spread", "masked", "used",
                   "y_ready", *NORM_SEMS) as (block, s):
            @block.tensor
            def _(pe):
                for t in range(NT):
                    last = pe.transpose(pT_ps[0:HE * E, t * P:(t + 1) * P], picked_b[:, t, :], wb(k, "ident"))
                last.then_inc(s["pT_ready"], 1)
                pe.wait_ge(s["scaled"], 1)
                for r in range(PAIRS):
                    if r >= 2:
                        pe.wait_ge(s["zT_sb"], r - 1)
                    for t in range(NT):
                        last = pe.transpose(ps[:, r % 2, t * P:(t + 1) * P],
                                            zn[:, t, 2 * r:2 * r + 2, :].rearrange("p h d -> p (h d)"), k.ident)
                    last.then_inc(s["zT_ready"], 1)
                pe.wait_ge(s["pT_sb"], 1)

                def spread(i):
                    if i >= 2:
                        pe.wait_ge(s["masked"], i - 1)
                    pe.matmul(ps[:, 2 + i % 2, :], wb(k, "selhe", HE * E)[:, i * P:(i + 1) * P], pT[:, :],
                              start=True, stop=True).then_inc(s["spread"], 1)

                spread(0)
                for i in range(PAIRS * E):
                    if i + 1 < PAIRS * E:
                        spread(i + 1)
                    pe.wait_ge(s["masked"], i + 1)
                    for t in range(NT):
                        last = pe.matmul(ps[:, 4 + t, 0:D], xm[:, i % RING, t * P:(t + 1) * P], output[:, i % E, i // E, :],
                                         start=i == 0, stop=i == PAIRS * E - 1)
                    last.then_inc(s["used"], 1)
                norm_tensor(k, pe, s, 0)

            @block.scalar
            def _(act):
                act.wait_ge(s["pT_ready"], 1)
                act.copy(pT[:, :], pT_ps[0:HE * E, 0:SEQ]).then_inc(s["pT_sb"], 1)
                for r in range(PAIRS):
                    act.wait_ge(s["zT_ready"], r + 1)
                    act.copy(zT[:, r, :], ps[:, r % 2, :]).then_inc(s["zT_sb"], 1)
                norm_scalar(k, act, s, 0)

            @block.gpsimd
            def _(pool):
                norm_gpsimd(k, pool, s)

            @block.vector
            def _(dve):
                chain = Chain(dve, s["chain"])
                for t in range(NT):
                    last = dve.tensor_tensor(zn[:, t, :, :], zn[:, t, :, :],
                                             gate[:, t * HE:(t + 1) * HE, :].to_broadcast([P, HE, WD]), ALU.mult)
                last.then_inc(s["scaled"], 1)
                for i in range(PAIRS * E):
                    if i % E == 0:
                        dve.wait_ge(s["zT_sb"], i // E + 1)
                    dve.wait_ge(s["spread"], i + 1)
                    if i >= RING:
                        dve.wait_ge(s["used"], i - RING + 1)
                    dve.tensor_tensor(xm[:, i % RING, :], zT[:, i // E, :], ps[:, 2 + i % 2, :], ALU.mult
                                      ).then_inc(s["masked"], 1)
                dve.wait_ge(s["used"], PAIRS * E)
                norm_vector(k, dve, chain, s, ps[:, 4:8, 0:D])


def shared_kv_attention(k, next_stream):
    nc, ps = k.nc, k.ps
    name, HW = "L2a", 16
    PAIRS = HW // 2
    with ExitStack() as ctx:
        def sb(n, shape, dt=F32):
            return ctx.enter_context(nc.sbuf_tensor(f"skv_{n}", shape, dt))

        zn = sb("zn", [P, NT, HW, WD])
        with ExitStack() as inner:
            def sbi(n, shape, dt=F32):
                return inner.enter_context(nc.sbuf_tensor(f"skv_{n}", shape, dt))

            qT = sbi("qT", [P, PAIRS, SEQ])
            kT = sbi("kT", [P, PAIRS, SEQ])
            v = sbi("v", [P, NT, HW, WD + 1])
            kw1 = sbi("kw1", [P, PAIRS])
            with phase(k, "chain", "q_ready", "k_ready", "v_ready", "q_sb", "k_sb", "v_sb") as (block, s):
                @block.sync
                def _(sp):
                    next_stream(sp)

                @block.tensor
                def _(pe):
                    for m in range(PAIRS):
                        if m >= 2:
                            pe.wait_ge(s["q_sb"], m - 1)
                        pe.matmul(ps[:, m % 2, :], w(k, name, "wq")[:, m * P:(m + 1) * P], k.xT[:, :], start=True,
                                  stop=True).then_inc(s["q_ready"], 1)
                        if m >= 2:
                            pe.wait_ge(s["k_sb"], m - 1)
                        pe.matmul(ps[:, 2 + m % 2, :], w(k, name, "wkv")[:, m * P:(m + 1) * P], k.xT[:, :], start=True,
                                  stop=True).then_inc(s["k_ready"], 1)
                        if m >= 2:
                            pe.wait_ge(s["v_sb"], m - 1)
                        t = m // 2
                        pe.matmul(ps[:, 4 + m % 2, :], k.xT[:, t * P:(t + 1) * P],
                                  w(k, name, "wkv")[:, m % 2 * 512:(m % 2 + 1) * 512], start=True, stop=True
                                  ).then_inc(s["v_ready"], 1)

                @block.scalar
                def _(act):
                    for m in range(PAIRS):
                        act.wait_ge(s["q_ready"], m + 1)
                        act.copy(qT[:, m, :], ps[:, m % 2, :]).then_inc(s["q_sb"], 1)

                @block.vector
                def _(dve):
                    chain = Chain(dve, s["chain"])
                    dve.memset(v[:, :, :, WD:WD + 1], 1.0)
                    chain(dve.tensor_scalar(kw1[:, :], w(k, name, "kw"), 1.0, None, ALU.add))
                    for m in range(PAIRS):
                        dve.wait_ge(s["k_ready"], m + 1)
                        dve.tensor_scalar(kT[:, m, :], ps[:, 2 + m % 2, :], kw1[:, m:m + 1], None, ALU.mult
                                          ).then_inc(s["k_sb"], 1)
                        dve.wait_ge(s["v_ready"], m + 1)
                        h0 = m % 2 * 8
                        dve.tensor_copy(v[:, m // 2, h0:h0 + 8, 0:WD],
                                        ps[:, 4 + m % 2, :].rearrange("p (h d) -> p h d", h=8)).then_inc(s["v_sb"], 1)

            wide_attend(k, name, HW, D ** -0.5, qT, kT, v, zn,
                        lambda n, sh, dt: inner.enter_context(nc.sbuf_tensor(f"skv_{n}", sh, dt)))

        zT = sb("zT", [P, PAIRS, SEQ])
        wo = w(k, name, "wo").rearrange("p (r d) -> p r d", r=PAIRS)
        with phase(k, "chain", "zT_ready", "zT_sb", "y_ready", *NORM_SEMS) as (block, s):
            @block.tensor
            def _(pe):
                def turn(r):
                    if r >= 2:
                        pe.wait_ge(s["zT_sb"], r - 1)
                    for t in range(NT):
                        last = pe.transpose(ps[:, r % 2, t * P:(t + 1) * P],
                                            zn[:, t, 2 * r:2 * r + 2, :].rearrange("p h d -> p (h d)"), k.ident)
                    last.then_inc(s["zT_ready"], 1)

                turn(0)
                for r in range(PAIRS):
                    if r + 1 < PAIRS:
                        turn(r + 1)
                    pe.wait_ge(s["zT_sb"], r + 1)
                    for t in range(NT):
                        last = pe.matmul(ps[:, 4 + t, 0:D], zT[:, r, t * P:(t + 1) * P], wo[:, r, :], start=r == 0,
                                         stop=r == PAIRS - 1)
                last.then_inc(s["y_ready"], 1)
                norm_tensor(k, pe, s, 2)

            @block.scalar
            def _(act):
                for r in range(PAIRS):
                    act.wait_ge(s["zT_ready"], r + 1)
                    act.copy(zT[:, r, :], ps[:, r % 2, :]).then_inc(s["zT_sb"], 1)
                norm_scalar(k, act, s, 2)

            @block.gpsimd
            def _(pool):
                norm_gpsimd(k, pool, s)

            @block.vector
            def _(dve):
                chain = Chain(dve, s["chain"])
                dve.wait_ge(s["y_ready"], 1)
                norm_vector(k, dve, chain, s, ps[:, 4:8, 0:D])


def top_two(k, dve, chain, vals, E, b):
    S3 = [P, NT, E]
    top_one(k, dve, chain, vals, b.key[:, :, 0:E], b.best[:, :, :], None, E)
    chain(dve.tensor_reduce(b.kmax[:, :, :], b.key[:, :, 0:E], AX.X, ALU.max))
    chain(dve.tensor_tensor(b.first[:, :, 0:E], b.key[:, :, 0:E], b.kmax[:, :, :].to_broadcast(S3), ALU.is_equal))
    chain(dve.scalar_tensor_tensor(out=b.rest[:, :, 0:E], in0=b.first[:, :, 0:E], scalar=-1e30, in1=vals,
                                   op0=ALU.mult, op1=ALU.add))
    top_one(k, dve, chain, b.rest[:, :, 0:E], b.key[:, :, 0:E], b.second[:, :, :], None, E)
    chain(dve.tensor_reduce(b.kmax[:, :, :], b.key[:, :, 0:E], AX.X, ALU.max))
    chain(dve.tensor_tensor(b.next[:, :, 0:E], b.key[:, :, 0:E], b.kmax[:, :, :].to_broadcast(S3), ALU.is_equal))


class RouterBuffers:
    def __init__(self, sb):
        def wide(n):
            return sb(n, [P, NT, 8])

        def one(n):
            return sb(n, [P, NT, 1])

        self.vals, self.key, self.first, self.next, self.rest = (
            wide("vals"), wide("key"), wide("first"), wide("next"), wide("rest"))
        self.best, self.second, self.kmax, self.e2, self.w1, self.w2 = (
            one("best"), one("second"), one("kmax"), one("e2"), one("w1"), one("w2"))


def conv_experts(k):
    nc, ps = k.nc, k.ps
    name, E, TAPS, HID2, RMS_EPS = "L2f", 8, 3, 32, 1e-6
    W = lambda n, r=P: w(k, name, n, r)
    bc = lambda n, c=D: W(n).unsqueeze(1).to_broadcast([P, NT, c])
    with ExitStack() as ctx:
        def sb(n, shape, dt=F32):
            return ctx.enter_context(nc.sbuf_tensor(f"conv_{n}", shape, dt))

        xpad = sb("xpad", [P, SEQ + TAPS - 1])
        acc = sb("acc", [P, SEQ])
        pw = sb("pw", [P, SEQ])
        x1T = sb("x1T", [P, SEQ])
        x1 = sb("x1", [P, NT, D])
        rw = sb("rw", [P, NT, E])
        yb = sb("yb", [P, NT, 2, SEQ])
        comb = sb("comb", [P, NT, D])
        combT = sb("combT", [P, SEQ])
        r = sb("r", [P, NT, D])
        sq = sb("sq", [P, NT, D])
        h = sb("h", [P, NT, D])
        hT = sb("hT", [P, SEQ])
        g = sb("g", [HID2, SEQ])
        b = RouterBuffers(sb)
        tok = lambda bank: ps[:, bank, :].rearrange("p (t d) -> p t d", t=NT)
        with phase(k, "chain", "conv_done", "pw_ready", "pw_sb", "x1T_done", "turned", "logits", "x1_sb", "e_in", "e_out", "ye_in",
                   "ye_out", "comb_ready") as (block, s):
            @block.tensor
            def _(pe):
                pe.wait_ge(s["conv_done"], 1)
                pe.matmul(ps[:, 0, :], W("pw"), acc[:, :], start=True, stop=True).then_inc(s["pw_ready"], 1)
                pe.wait_ge(s["x1T_done"], 1)
                for t in range(NT):
                    last = pe.matmul(ps[:, 2, t * E:(t + 1) * E], x1T[:, t * P:(t + 1) * P], W("router"), start=True, stop=True)
                last.then_inc(s["logits"], 1)
                for t in range(NT):
                    last = pe.transpose(ps[:, 1, t * P:(t + 1) * P], x1T[:, t * P:(t + 1) * P], k.ident)
                last.then_inc(s["turned"], 1)
                for t in range(NT):
                    for c in range(2):
                        i = 2 * t + c
                        if i >= 4:
                            pe.wait_ge(s["ye_in"], i - 3)
                        pe.matmul(ps[:, 4 + i % 4, :], x1T[:, t * P:(t + 1) * P], W("experts")[:, c * 512:(c + 1) * 512],
                                  start=True, stop=True).then_inc(s["e_in"], 1)

            @block.scalar
            def _(act):
                act.wait_ge(s["pw_ready"], 1)
                act.activation(pw[:, :], ps[:, 0, :], ACT.Silu, bias=W("pwb")).then_inc(s["pw_sb"], 1)
                act.wait_ge(s["turned"], 1)
                act.copy(x1[:, :, :], tok(1))
                for i in range(2 * NT):
                    act.wait_ge(s["ye_in"], i + 1)
                    act.activation(yb[:, i // 2, i % 2, :], yb[:, i // 2, i % 2, :], ACT.Silu).then_inc(s["ye_out"], 1)
                act.wait_ge(s["e_out"], 1)
                act.activation(b.e2[:, :, :], b.e2[:, :, :], ACT.Exp).then_inc(s["x1_sb"], 1)

            @block.vector
            def _(dve):
                chain = Chain(dve, s["chain"])
                dve.memset(xpad[:, 0:TAPS - 1], 0.0)
                chain(dve.tensor_copy(xpad[:, TAPS - 1:], k.xT[:, :]))
                chain(dve.tensor_scalar(acc[:, :], xpad[:, 0:SEQ], W("conv")[:, 0:1], W("cb"), ALU.mult, ALU.add))
                for t in range(1, TAPS):
                    last = dve.scalar_tensor_tensor(out=acc[:, :], in0=xpad[:, t:t + SEQ], scalar=W("conv")[:, t:t + 1],
                                                    in1=acc[:, :], op0=ALU.mult, op1=ALU.add)
                    if t < TAPS - 1:
                        chain(last)
                last.then_inc(s["conv_done"], 1)
                dve.wait_ge(s["pw_sb"], 1)
                dve.tensor_tensor(x1T[:, :], k.xT[:, :], pw[:, :], ALU.add).then_inc(s["x1T_done"], 1)
                dve.wait_ge(s["logits"], 1)
                chain(dve.tensor_tensor(b.vals[:, :, :], ps[:, 2, 0:NT * E].rearrange("p (t e) -> p t e", t=NT),
                                        bc("rb", E), ALU.add))
                top_two(k, dve, chain, b.vals[:, :, :], E, b)
                dve.tensor_tensor(b.e2[:, :, :], b.second[:, :, :], b.best[:, :, :], ALU.subtract).then_inc(s["e_out"], 1)
                for i in range(2 * NT):
                    dve.wait_ge(s["e_in"], i + 1)
                    dve.tensor_tensor(yb[:, i // 2, i % 2, :], ps[:, 4 + i % 4, :],
                                      W("eb")[:, i % 2 * 512:(i % 2 + 1) * 512], ALU.add).then_inc(s["ye_in"], 1)
                dve.wait_ge(s["x1_sb"], 1)
                chain(dve.tensor_scalar(b.w1[:, :, :], b.e2[:, :, :], 1.0, None, ALU.add))
                chain(dve.reciprocal(b.w1[:, :, :], b.w1[:, :, :]))
                chain(dve.tensor_tensor(b.w2[:, :, :], b.e2[:, :, :], b.w1[:, :, :], ALU.mult))
                mix(dve, chain, b, rw[:, :, :], E)
                ye = yb[:, :, :, :].rearrange("p t c (e d) -> p t (c e) d", e=4)
                for e in range(E):
                    for t in range(NT):
                        if e == 0:
                            dve.wait_ge(s["ye_out"], 2 * t + 2)
                            last = dve.tensor_scalar(comb[:, t, :], ye[:, t, e, :], rw[:, t, e:e + 1], None, ALU.mult)
                        else:
                            last = dve.scalar_tensor_tensor(out=comb[:, t, :], in0=ye[:, t, e, :], scalar=rw[:, t, e:e + 1],
                                                            in1=comb[:, t, :], op0=ALU.mult, op1=ALU.add)
                    chain(last)

        with phase(k, "chain", "turned", "turned_sb", "moe_ready", "h_ready", "hT_ready", "hT_sb", "down_ready", "g_ready", "up_ready",
                   "ms_ready", "ms_eps", "rms_ready", *NORM_SEMS) as (block, s):
            @block.tensor
            def _(pe):
                for t in range(NT):
                    last = pe.transpose(ps[:, 0, t * P:(t + 1) * P], comb[:, t, :], k.ident)
                last.then_inc(s["turned"], 1)
                pe.wait_ge(s["turned_sb"], 1)
                for t in range(NT):
                    last = pe.matmul(ps[:, 1, t * D:(t + 1) * D], combT[:, t * P:(t + 1) * P], W("out"), start=True, stop=True)
                last.then_inc(s["moe_ready"], 1)
                pe.wait_ge(s["h_ready"], 1)
                for t in range(NT):
                    last = pe.transpose(ps[:, 2, t * P:(t + 1) * P], h[:, t, :], k.ident)
                last.then_inc(s["hT_ready"], 1)
                pe.wait_ge(s["hT_sb"], 1)
                pe.matmul(ps[0:HID2, 3, :], W("down"), hT[:, :], start=True, stop=True).then_inc(s["down_ready"], 1)
                pe.wait_ge(s["g_ready"], 1)
                for t in range(NT):
                    last = pe.matmul(ps[:, 4, t * D:(t + 1) * D], g[:, t * P:(t + 1) * P], W("up", HID2), start=True, stop=True)
                last.then_inc(s["up_ready"], 1)
                norm_tensor(k, pe, s, 5)

            @block.scalar
            def _(act):
                act.wait_ge(s["turned"], 1)
                act.copy(combT[:, :], ps[:, 0, :]).then_inc(s["turned_sb"], 1)
                act.wait_ge(s["hT_ready"], 1)
                act.copy(hT[:, :], ps[:, 2, :]).then_inc(s["hT_sb"], 1)
                act.wait_ge(s["down_ready"], 1)
                act.activation(g[:, :], ps[0:HID2, 3, :], ACT.Gelu, bias=W("downb", HID2)).then_inc(s["g_ready"], 1)
                norm_scalar(k, act, s, 5)

            @block.gpsimd
            def _(pool):
                pool.wait_ge(s["ms_ready"], 1)
                pool.tensor_scalar(k.vareps[:, :], b.e2[:, :, 0], 1.0 / D, RMS_EPS, ALU.mult, ALU.add).then_inc(s["ms_eps"], 1)
                pool.wait_ge(s["ms_eps"], 1)
                pool.tensor_tensor(k.rstd[:, :], k.vareps[:, :], k.minus_half, ALU.pow).then_inc(s["rms_ready"], 1)
                norm_gpsimd(k, pool, s)

            @block.vector
            def _(dve):
                chain = Chain(dve, s["chain"])
                chain(dve.tensor_tensor(x1[:, :, :], x1[:, :, :], bc("ob"), ALU.add))
                dve.wait_ge(s["moe_ready"], 1)
                chain(dve.tensor_tensor(r[:, :, :], tok(1), x1[:, :, :], ALU.add))
                chain(dve.tensor_tensor(sq[:, :, :], r[:, :, :], r[:, :, :], ALU.mult))
                dve.tensor_reduce(b.e2[:, :, :], sq[:, :, :], AX.X, ALU.add).then_inc(s["ms_ready"], 1)
                dve.wait_ge(s["rms_ready"], 1)
                for t in range(NT):
                    last = dve.scalar_tensor_tensor(out=h[:, t, :], in0=r[:, t, :], scalar=k.rstd[:, t:t + 1],
                                                    in1=W("norm"), op0=ALU.mult, op1=ALU.mult)
                last.then_inc(s["h_ready"], 1)
                dve.wait_ge(s["h_ready"], 1)
                chain(dve.tensor_tensor(r[:, :, :], h[:, :, :], bc("upb"), ALU.add))
                dve.wait_ge(s["up_ready"], 1)
                chain(dve.tensor_tensor(h[:, :, :], tok(4), r[:, :, :], ALU.add))
                norm_vector(k, dve, chain, s, h[:, :, :])


def mix(dve, chain, b, rw, E):
    S3 = [P, NT, E]
    chain(dve.tensor_tensor(b.first[:, :, 0:E], b.first[:, :, 0:E], b.w1[:, :, :].to_broadcast(S3), ALU.mult))
    chain(dve.tensor_tensor(b.next[:, :, 0:E], b.next[:, :, 0:E], b.w2[:, :, :].to_broadcast(S3), ALU.mult))
    chain(dve.tensor_tensor(rw, b.first[:, :, 0:E], b.next[:, :, 0:E], ALU.add))


def routed_ffn(k, stream_loaded):
    nc, ps = k.nc, k.ps
    name, E = "L3f", EXPERTS3 - 1
    at, _ = S_AT["L3e"]
    part = lambda n: k.stream[:, at["L3e", n][0]:sum(at["L3e", n])]
    gate, up = (part(n).rearrange("p (e f) -> p e f", e=EXPERTS3) for n in ("gate", "up"))
    down = part("down").rearrange("p (e t d) -> p e t d", e=EXPERTS3, t=3)
    HT = len(HID_TILES)
    with ExitStack() as ctx:
        def sb(n, shape, dt=F32):
            return ctx.enter_context(nc.sbuf_tensor(f"rffn_{n}", shape, dt))

        b = RouterBuffers(sb)
        rw = sb("rw", [P, NT, EXPERTS3])
        sg = sb("sg", [P, 2, SEQ])
        hid = sb("hid", [P, 2, HT, SEQ])
        acc = sb("acc", [P, NT, D])
        with phase(k, "chain", "logits", "scaled", "probs", "up_ready", "silu_ready", "hid_ready", "down_ready", "added",
                   *NORM_SEMS) as (block, s):
            @block.tensor
            def _(pe):
                for t in range(NT):
                    last = pe.matmul(ps[:, 6, t * E:(t + 1) * E], k.xT[:, t * P:(t + 1) * P], w(k, name, "wr"), start=True,
                                     stop=True)
                last.then_inc(s["logits"], 1)
                pe.wait_ge(stream_loaded, 16)

                def gate_up(e):
                    for t, (a0, nr) in enumerate(HID_TILES):
                        i = e * HT + t
                        if i >= 2:
                            pe.wait_ge(s["hid_ready"], i - 1)
                        bk = 2 * (i % 2)
                        pe.matmul(ps[0:nr, bk, :], gate[:, e, a0:a0 + nr], k.xT[:, :], start=True, stop=True)
                        pe.matmul(ps[0:nr, bk + 1, :], up[:, e, a0:a0 + nr], k.xT[:, :], start=True, stop=True
                                  ).then_inc(s["up_ready"], 1)

                gate_up(0)
                for e in range(EXPERTS3):
                    if e + 1 < EXPERTS3:
                        gate_up(e + 1)
                    pe.wait_ge(s["hid_ready"], (e + 1) * HT)
                    if e >= 2:
                        pe.wait_ge(s["added"], e - 1)
                    for tt in range(NT):
                        for t, (a0, nr) in enumerate(HID_TILES):
                            last = pe.matmul(ps[:, 4 + e % 2, tt * D:(tt + 1) * D], hid[0:nr, e % 2, t, tt * P:(tt + 1) * P],
                                             down[0:nr, e, t, :], start=t == 0, stop=t == HT - 1)
                    last.then_inc(s["down_ready"], 1)
                norm_tensor(k, pe, s, 7)

            @block.scalar
            def _(act):
                act.wait_ge(s["scaled"], 1)
                act.activation(b.vals[:, :, 0:E], b.vals[:, :, 0:E], ACT.Sigmoid).then_inc(s["probs"], 1)
                for e in range(EXPERTS3):
                    for t, (a0, nr) in enumerate(HID_TILES):
                        i = e * HT + t
                        act.wait_ge(s["up_ready"], i + 1)
                        if i >= 2:
                            act.wait_ge(s["hid_ready"], i - 1)
                        act.activation(sg[0:nr, i % 2, :], ps[0:nr, 2 * (i % 2), :], ACT.Silu).then_inc(s["silu_ready"], 1)
                norm_scalar(k, act, s, 7)

            @block.gpsimd
            def _(pool):
                norm_gpsimd(k, pool, s)

            @block.vector
            def _(dve):
                chain = Chain(dve, s["chain"])
                S3 = [P, NT, E]

                def route():
                    top_two(k, dve, chain, b.vals[:, :, 0:E], E, b)
                    chain(dve.tensor_tensor(b.e2[:, :, :], b.best[:, :, :], b.second[:, :, :], ALU.add))
                    chain(dve.reciprocal(b.e2[:, :, :], b.e2[:, :, :]))
                    chain(dve.tensor_tensor(b.w1[:, :, :], b.best[:, :, :], b.e2[:, :, :], ALU.mult))
                    chain(dve.tensor_tensor(b.w2[:, :, :], b.second[:, :, :], b.e2[:, :, :], ALU.mult))
                    chain(dve.memset(rw[:, :, 0:1], 1.0))
                    mix(dve, chain, b, rw[:, :, 1:EXPERTS3], E)

                def add(e):
                    dve.wait_ge(s["down_ready"], e + 1)
                    for t in range(NT):
                        y = ps[:, 4 + e % 2, t * D:(t + 1) * D]
                        if e == 0:
                            last = dve.tensor_scalar(acc[:, t, :], y, rw[:, t, 0:1], None, ALU.mult)
                        else:
                            last = dve.scalar_tensor_tensor(out=acc[:, t, :], in0=y, scalar=rw[:, t, e:e + 1],
                                                            in1=acc[:, t, :], op0=ALU.mult, op1=ALU.add)
                    last.then_inc(s["added"], 1)
                    dve.wait_ge(s["added"], e + 1)

                dve.wait_ge(s["logits"], 1)
                chain(dve.tensor_tensor(b.vals[:, :, 0:E], ps[:, 6, 0:NT * E].rearrange("p (t e) -> p t e", t=NT),
                                        w(k, name, "rb").unsqueeze(1).to_broadcast(S3), ALU.mult))
                dve.memset(b.w1[:, :, :], 0.0).then_inc(s["scaled"], 1)
                dve.wait_ge(s["probs"], 1)
                route()
                for e in range(EXPERTS3):
                    for t, (a0, nr) in enumerate(HID_TILES):
                        i = e * HT + t
                        dve.wait_ge(s["silu_ready"], i + 1)
                        if e >= 2 and t == 0:
                            dve.wait_ge(s["down_ready"], e - 1)
                        dve.tensor_tensor(hid[0:nr, e % 2, t, :], sg[0:nr, i % 2, :], ps[0:nr, 2 * (i % 2) + 1, :], ALU.mult
                                          ).then_inc(s["hid_ready"], 1)
                    if e >= 1:
                        add(e - 1)
                add(EXPERTS3 - 1)
                norm_vector(k, dve, chain, s, acc[:, :, :])


UPTO = 12


class Kernel:
    pass


def build(nc, xin, xTin, ctxT, m1q, m1k, m3q, m3k, wres, wstr0, wstr1, wstr3, bc, out):
    k = Kernel()
    k.nc = nc
    with ExitStack() as ctx:
        def sb(n, shape, dt=F32):
            return ctx.enter_context(nc.sbuf_tensor(n, shape, dt))

        k.weights = sb("weights", [P, R_N])
        k.stream = sb("stream", [P, S_N])
        k.bconst = sb("bconst", [P, B_N], BF16)
        k.x = sb("x_tok", [P, NT, D])
        k.xT = sb("xT", [P, SEQ])
        k.src = sb("src", [P, SEQ])
        k.ctxT = sb("ctxT", [P, CTX])
        k.resid = sb("resid", [P, NT, D])
        k.stats = sb("stats", [P, NT, 6])
        k.mv = sb("mv", [P, NT, 2])
        k.vareps = sb("vareps", [P, NT])
        k.rstd = sb("rstd", [P, NT])
        k.ps = ctx.enter_context(nc.psum_tensor("ps", [P, 8, 512], F32))
        k.ident = w(k, "const", "ident")
        k.minus_half = w(k, "const", "half")[:, 0:NT]
        loaded = {g: ctx.enter_context(nc.semaphore(f"loaded_{g}")) for g in GROUPS}
        bloaded = ctx.enter_context(nc.semaphore("bloaded"))
        stream_loaded = ctx.enter_context(nc.semaphore("stream_loaded"))
        stored = ctx.enter_context(nc.semaphore("stored"))
        k.pool = [ctx.enter_context(nc.semaphore(f"stage_{i}")) for i in range(18)]

        with nc.Block() as block:
            @block.sync
            def _(sp):
                sp.dma_start(k.bconst[:, :], bc[:, :]).then_inc(bloaded, 16)
                for g in GROUPS:
                    a = min(R_AT[x][0] for x in R_AT if x[0] == g)
                    z = max(sum(R_AT[x]) for x in R_AT if x[0] == g)
                    sp.dma_start(k.weights[:, a:z], wres[:, a:z]).then_inc(loaded[g], 16)
                for g in GROUPS:
                    sp.wait_ge(loaded[g], 16)
                sp.wait_ge(bloaded, 16)

        def stream_in(sp, src):
            sp.sem_clear(stream_loaded)
            sp.dma_start(k.stream[:, 0:src.shape[1]], src[:, :]).then_inc(stream_loaded, 16)

        with nc.Fori(0, BATCH) as b:
            k.b = b
            with phase(k, "x_in") as (block, s):
                @block.sync
                def _(sp):
                    sp.dma_start(k.x[:, :, :], xin[bass.ds(b, 1)].rearrange("o (t p) d -> p (o t) d", p=P)
                                 ).then_inc(s["x_in"], 16)
                    sp.dma_start(k.xT[:, :], xTin[bass.ds(b, 1)].rearrange("o p t -> p (o t)")).then_inc(s["x_in"], 16)
                    sp.dma_start(k.ctxT[:, :], ctxT[bass.ds(b, 1)].rearrange("o p t -> p (o t)")).then_inc(s["x_in"], 16)
                    stream_in(sp, wstr0)
                    sp.wait_ge(s["x_in"], 48)

            R8 = DH ** -0.5
            stages = [
                lambda: small_attention(k, "L0a", R8, SEQ, P, k.src, k.src),
                lambda: small_attention(k, "L0x", 1.0, CTX, KT2, k.xT, k.ctxT, scrambled=True),
                lambda: gated_ffn(k, stream_loaded),
                lambda: mamba(k, lambda sp: stream_in(sp, wstr1)),
                lambda: small_attention(k, "L1x", R8, CTX, KT2, k.xT, k.ctxT, masks=(m1q, m1k, ALU.is_equal)),
                lambda: expert_attention(k, stream_loaded),
                lambda: shared_kv_attention(k, lambda sp: stream_in(sp, wstr3)),
                lambda: small_attention(k, "L2x", R8, CTX, KT2, k.xT, k.ctxT),
                lambda: conv_experts(k),
                lambda: small_attention(k, "L3a", R8, SEQ, P, k.src, k.src, biased=False, v_biased=False),
                lambda: small_attention(k, "L3x", R8, CTX, KT2, k.xT, k.ctxT, biased=False, v_biased=False,
                                        masks=(m3q, m3k, ALU.not_equal)),
                lambda: routed_ffn(k, stream_loaded),
            ]
            for st in stages[START:UPTO]:
                st()
            with phase(k, "x_out") as (block, s):
                @block.sync
                def _(sp):
                    sp.dma_start(out[bass.ds(b, 1)].rearrange("o (t p) d -> p (o t) d", p=P), k.x[:, :, :]
                                 ).then_inc(s["x_out"], 16)
                    sp.wait_ge(s["x_out"], 16)


START = 0


def block_diagonal(m):
    h, i, j = m.shape
    out = np.zeros((h, j, h, i), m.dtype)
    for n in range(h):
        out[n, :, n, :] = m[n].T
    return out.reshape(h * j, h * i)


def by_dim(m):
    return m.reshape(m.shape[0], H, DH).transpose(0, 2, 1).reshape(m.shape[0], H * DH)


def rows(v):
    return np.broadcast_to(v.reshape(1, -1), (P, v.size))


def tiles(m):
    return m.reshape(-1, P, m.shape[1]).transpose(1, 0, 2).reshape(P, -1)


def pack(at, n, blocks):
    out = np.zeros((P, n), np.float32)
    for key, m in blocks.items():
        c, cols = at[key]
        assert m.ndim == 2 and m.shape[1] == cols and m.shape[0] <= P, (key, m.shape, cols)
        out[:m.shape[0], c:c + cols] = m
    return out


def lay_out(i):
    B = {}
    col = lambda v: v.reshape(-1, 1)
    for a, key, t in (("L0a", "L0_attn_", True), ("L0x", "L0_xattn_", True), ("L1x", "L1_xattn_", True),
                      ("L2x", "L2_xattn_", True), ("L3x", "L3_xattn_", True)):
        g = lambda n: (i[key + n].T if t else i[key + n])
        B[a, "wq"], B[a, "wk"], B[a, "wv"] = by_dim(g("Wq")), by_dim(g("Wk")), g("Wv")
        if key + "Wo" in i:
            B[a, "wo"] = g("Wo")
        if key + "bq" in i:
            B[a, "bq"], B[a, "bk"] = (by_dim(i[key + n].reshape(1, -1)).T for n in ("bq", "bk"))
            B[a, "bv"] = rows(i[key + "bv"])
        if key + "bo" in i:
            B[a, "bo"] = rows(i[key + "bo"])
    B["L0x", "gamma"], B["L0x", "beta"] = rows(i["L0_xattn_gamma"]), rows(i["L0_xattn_beta"])
    B["L3a", "down"] = i["L3_attn_W_down"]
    B["L3a", "wq"] = by_dim(block_diagonal(i["L3_attn_toqueries"]))
    B["L3a", "wk"] = by_dim(block_diagonal(i["L3_attn_tokeys"]))
    B["L3a", "wv"] = block_diagonal(i["L3_attn_tovalues"])
    B["L3a", "wo"], B["L3a", "bo"] = i["L3_attn_W_unify"], rows(i["L3_attn_b_unify"])
    freq = np.exp(np.arange(0, D, 2, dtype=np.float32) * np.float32(-np.log(10000.0) / D)).astype(np.float32)
    ang = (np.arange(SEQ, dtype=np.float32)[:, None] * freq[None, :]).astype(np.float32)
    B["L0a", "cos"] = np.concatenate([np.cos(ang).T] * 2).astype(np.float32)
    B["L0a", "sin"] = np.concatenate([np.sin(ang).T] * 2).astype(np.float32)
    rot = np.zeros((D, D), np.float32)
    for j in range(D // 2):
        rot[j + D // 2, j] = -1.0
        rot[j, j + D // 2] = 1.0
    B["L0a", "rot"] = rot
    B["const", "ident"] = np.eye(P, dtype=np.float32)
    B["const", "desc"] = rows(np.arange(8, 0, -1).astype(np.float32))
    B["const", "half"] = np.full((P, 8), -0.5, np.float32)
    B["const", "one"] = np.ones((P, P), np.float32)
    more_layout(i, B)
    return pack(R_AT, R_N, {x: v for x, v in B.items() if x in R_AT})


def bf16_consts():
    out = np.zeros((P, B_N), np.float32)

    def put(n, m):
        at, c = B_AT["b", n]
        out[:m.shape[0], at:at + c] = m
    put("ident", np.eye(P))
    q, kk = np.arange(P)[:, None], np.arange(P)[None, :]
    put("tri", np.where(kk > q, MASKED, 0.0))
    put("triT", np.where(q > kk, MASKED, 0.0))
    sel = np.zeros((12, 4, P))
    for hh in range(4):
        for p in range(PARTS):
            sel[p * 4 + hh, hh, :] = 1.0
    put("sel", sel.reshape(12, -1))
    she = np.zeros((64, 4, 8, P))
    for pair in range(4):
        for e in range(8):
            for a in range(2):
                she[(2 * pair + a) * 8 + e, pair, e, 64 * a:64 * a + 64] = 1.0
    put("selhe", she.reshape(64, -1))
    return out.astype(mybir.dt.np(BF16))


def more_layout(i, B):
    g = lambda n: i["L0_ffn_" + n]
    for n, key in (("w1", "w1_w"), ("w2", "w2_w")):
        B["L0f", n] = g(key).T
    for n, key in (("h1", "h1_w"), ("h2", "h2_w"), ("w3", "w3_w")):
        B["L0f", n] = tiles(g(key).T)
    B["L0f", "s3"] = rows(g("w3_s"))
    cols = lambda v: v.reshape(-1, P).T
    for n, key in (("s1", "w1_s"), ("s2", "w2_s"), ("t1", "h1_s"), ("t2", "h2_s")):
        B["L0f", n] = cols(g(key))
    m = lambda n: i["L1_attn_" + n]
    B["L1m", "w_in"], B["L1m", "w_x"], B["L1m", "w_dt"] = m("W_in"), tiles(m("W_x")), m("W_dt")
    B["L1m", "w_out"], B["L1m", "conv"] = tiles(m("W_out")), tiles(m("conv_w"))
    B["L1m", "cb"], B["L1m", "bdt"], B["L1m", "dskip"] = cols(m("conv_b")), cols(m("b_dt")), cols(m("D"))
    B["L1m", "alog"] = tiles(m("A_log"))
    B["L1g", "wq"], B["L1g", "wk"], B["L1g", "gate"] = (i["L1_ffn_" + n] for n in ("w_q", "w_k", "w_gate"))
    B["L2a", "wq"], B["L2a", "wkv"], B["L2a", "wo"] = i["L2_attn_w_q"], i["L2_attn_w_kv"], tiles(i["L2_attn_w_o"])
    B["L2a", "kw"] = cols(i["L2_attn_k_weights"].reshape(-1))
    f = lambda n: i["L2_ffn_" + n]
    B["L2f", "conv"], B["L2f", "cb"] = f("dw_kernel")[:, 0, :], f("dw_bias").reshape(-1, 1)
    B["L2f", "pw"], B["L2f", "pwb"] = f("pw_w").T, f("pw_b").reshape(-1, 1)
    B["L2f", "router"], B["L2f", "rb"] = f("router_w").T, rows(f("router_b"))
    B["L2f", "experts"], B["L2f", "eb"] = f("expert_w").transpose(2, 0, 1).reshape(P, -1), rows(f("expert_b").reshape(-1))
    B["L2f", "out"], B["L2f", "ob"], B["L2f", "norm"] = f("out_w").T, rows(f("out_b")), rows(f("norm_w"))
    B["L2f", "down"], B["L2f", "downb"] = f("ff_down_w").T, f("ff_down_b").reshape(-1, 1)
    B["L2f", "up"], B["L2f", "upb"] = f("ff_up_w").T, rows(f("ff_up_b"))
    B["L3f", "wr"], B["L3f", "rb"] = i["L3_ffn_Wr"], rows(i["L3_ffn_routing_bias"])


def by_query(m):
    m = m.reshape(BATCH, NT, P, CTX).transpose(0, 2, 1, 3).reshape(BATCH, P, NT * CTX)
    return np.ascontiguousarray(m).view(np.int32)


def by_key(m):
    m = m.reshape(BATCH, SEQ, 2, KT2).transpose(0, 3, 2, 1).reshape(BATCH, KT2, 2 * SEQ)
    return np.ascontiguousarray(m).view(np.int32)


def kernel(**inputs):
    import concourse.bacc as _bacc
    from concourse.bass_utils import run_bass_kernel_spmd as _run

    nc = _bacc.Bacc("TRN2", target_bir_lowering=False, num_devices=1)
    i = {n: np.asarray(a) for n, a in inputs.items()}
    m1 = i["mask_BxSxS2_ik1"]
    m3 = i["mask_Bx1xSxS2_bk1"].reshape(BATCH, SEQ, CTX)
    arrays = {
        "x_in": i["x"], "xT_in": i["x"].transpose(0, 2, 1), "ctxT_in": i["ctx_1024"].transpose(0, 2, 1),
        "mask1_qk": by_query(m1), "mask1_kq": by_key(m1), "mask3_qk": by_query(m3), "mask3_kq": by_key(m3),
        "weights_in": lay_out(i), "ffn_in": lay_out_streamed(i, "L0f"), "value_output_in": lay_out_streamed(i, "L1e"),
        "gate_up_down_in": lay_out_streamed(i, "L3e"), "bconst_in": bf16_consts(),
    }
    arrays = {n: np.ascontiguousarray(a) for n, a in arrays.items()}
    aps = [nc.dram_tensor(n, a.shape, mybir.dt.from_np(a.dtype), kind="ExternalInput").ap() for n, a in arrays.items()]
    out = nc.dram_tensor("out_dram", (BATCH, SEQ, D), F32, kind="ExternalOutput").ap()
    build(nc, *aps, out)
    r = _run(nc, [arrays], core_ids=[0])
    return r.results[0]["out_dram"]


def lay_out_streamed(i, g):
    at, n = S_AT[g]
    B = {}
    if g == "L0f":
        more_layout(i, B)
        B = {x: v for x, v in B.items() if x in at}
    elif g == "L1e":
        B[g, "value"] = i["L1_ffn_value_experts"].transpose(2, 0, 1, 3).reshape(P, 4096)
        B[g, "output"] = i["L1_ffn_output_experts"].reshape(8, 4, P, D).transpose(2, 0, 1, 3).reshape(P, 4096)
    else:
        for name, a, b in (("gate", "L3_ffn_shared_gate", "L3_ffn_routed_gate"), ("up", "L3_ffn_shared_up", "L3_ffn_routed_up")):
            B[g, name] = np.concatenate([i[a][None], i[b]]).transpose(1, 0, 2).reshape(P, -1)
        down = np.concatenate([i["L3_ffn_shared_down"][None], i["L3_ffn_routed_down"]])
        d3 = np.zeros((8, 3, P, D), np.float32)
        for t, (at0, nr) in enumerate(HID_TILES):
            d3[:, t, :nr] = down[:, at0:at0 + nr]
        B[g, "down"] = d3.transpose(2, 0, 1, 3).reshape(P, -1)
    return pack(at, n, B)
```

```python
from contextlib import ExitStack, contextmanager

import numpy as np
import concourse.bass as bass
from concourse import mybir

F32 = mybir.dt.float32
BF16 = mybir.dt.bfloat16
I32 = mybir.dt.int32
U8 = mybir.dt.uint8
ACT = mybir.ActivationFunctionType
ALU = mybir.AluOpType
AX = mybir.AxisListType

P = 128
BATCH, SEQ, CTX, D = 4, 512, 154, 128
NT = SEQ // P
KT2 = CTX // 2
H, DH = 16, 8
PARTS = 3
TERMS = PARTS * PARTS
ROWS = TERMS * DH
TWO_ONES = float(np.array([0x3F803F80], np.uint32).view(np.float32)[0])
MASKED = -float(2 ** 40)
EPS = 1e-5
PB = 2
VW = 32


SMALL = ["wq", "wk", "wv", "wo", "bv", "bo", "bq", "bk"]
RESIDENT = {}
for _a in ("L0a", "L0x", "L1x", "L2x", "L3a", "L3x"):
    RESIDENT[_a] = [(n, 1 if n in ("bq", "bk") else D) for n in SMALL]
RESIDENT["L0a"] += [("cos", SEQ), ("sin", SEQ), ("rot", D)]
RESIDENT["L0x"] += [("gamma", D), ("beta", D)]
RESIDENT["L1m"] = [("w_in", 512), ("w_x", 208), ("w_dt", 256), ("w_out", 256), ("conv", 8), ("cb", 2), ("bdt", 2),
                   ("alog", 32), ("dskip", 2)]
RESIDENT["L1g"] = [("wq", 512), ("wk", 512), ("gate", 64)]
RESIDENT["L2a"] = [("wq", 1024), ("wkv", 1024), ("wo", 1024), ("kw", 8)]
RESIDENT["L2f"] = [("conv", 3), ("cb", 1), ("pw", D), ("pwb", 1), ("router", 8), ("rb", 8), ("experts", 1024),
                   ("eb", 1024), ("out", D), ("ob", D), ("norm", D), ("down", 32), ("downb", 1), ("up", D), ("upb", D)]
RESIDENT["L3a"] += [("down", D)]
RESIDENT["L3f"] = [("wr", 7), ("rb", 7)]
HID = 352
HID_TILES = [(0, 128), (128, 128), (256, 96)]
EXPERTS3 = 8
STREAMED = {"L0f": [("w1", 512), ("w2", 512), ("h1", 2048), ("h2", 2048), ("w3", 512), ("s3", D),
                    ("s1", 4), ("s2", 4), ("t1", 4), ("t2", 4)],
            "L1e": [("value", 4096), ("output", 4096)],
            "L3e": [("gate", 8 * HID), ("up", 8 * HID), ("down", 8 * 3 * D)]}
CONSTS = [("ident", P), ("desc", 8), ("half", 8), ("one", P), ("spread", 2 * P)]


def columns(groups):
    at, out = 0, {}
    for g, items in groups.items():
        for n, c in items:
            out[g, n] = (at, c)
            at += c
    return out, at


R_AT, R_N = columns({"const": CONSTS} | RESIDENT)
S_AT = {g: columns({g: items}) for g, items in STREAMED.items()}
S_N = max(n for _, n in S_AT.values())
GROUPS = ["const"] + list(RESIDENT)
B_CONSTS = [("ident", P), ("tri", P), ("triT", P), ("sel", 4 * P), ("selhe", 4 * 8 * P), ("stacked", 32)]
B_AT, B_N = columns({"b": B_CONSTS})


@contextmanager
def phase(k, *names):
    nc = k.nc

    assert len(names) <= len(k.pool), (len(names), len(k.pool))
    s = dict(zip(names, k.pool))
    with nc.Block() as block:
        yield block, s
    used = k.pool[:len(names)]
    nc.sync.sem_clear(range(used[0].num, used[-1].num + 1))
    nc.all_engine_barrier()


class Chain:

    def __init__(self, eng, sem):
        self.eng, self.sem, self.n = eng, sem, 0

    def __call__(self, ins):
        ins.then_inc(self.sem, 1)
        self.n += 1
        self.eng.wait_ge(self.sem, self.n)


def w(k, group, name, rows=P):
    at, n = R_AT[group, name]
    return k.weights[0:rows, at:at + n]


def ws(k, group, name, rows=P):
    at, n = S_AT[group][0][group, name]
    return k.stream[0:rows, at:at + n]


def wb(k, name, rows=P):
    at, n = B_AT["b", name]
    return k.bconst[0:rows, at:at + n]


def norm_vector(k, dve, chain, s, y, bias=None):
    chain(dve.tensor_tensor(k.resid[:, :, :], y, k.x[:, :, :], ALU.add))
    norm_stats(k, dve, chain, s["var_ready"], s["rstd_ready"], 1)
    for t in range(NT):
        last = dve.tensor_scalar(k.x[:, t, :], k.resid[:, t, :], k.mv[:, t, 0:1], k.rstd[:, t:t + 1],
                                 ALU.subtract, ALU.mult)
    last.then_inc(s["x_ready"], 1)


def norm_stats(k, dve, chain, var_ready, rstd_ready, n):
    for t in range(NT):
        last = dve.bn_stats(k.stats[:, t, :], k.resid[:, t, :])
    chain(last)
    for t in range(NT):
        last = dve.bn_aggr(k.mv[:, t, :], k.stats[:, t, :])
    last.then_inc(var_ready, 1)
    dve.wait_ge(rstd_ready, n)


def norm_gpsimd(k, pool, s, n=1, eps=EPS):
    pool.wait_ge(s["var_ready"], n)
    pool.tensor_scalar(k.vareps[:, :], k.mv[:, :, 1], eps, None, ALU.add).then_inc(s["eps_added"], 1)
    pool.wait_ge(s["eps_added"], n)
    pool.tensor_tensor(k.rstd[:, :], k.vareps[:, :], k.minus_half, ALU.pow).then_inc(s["rstd_ready"], 1)


def norm_tensor(k, pe, s, bank):
    pe.wait_ge(s["x_ready"], 1)
    for t in range(NT):
        last = pe.transpose(k.ps[:, bank, t * P:(t + 1) * P], k.x[:, t, :], k.ident)
    last.then_inc(s["xT_ready"], 1)


def norm_scalar(k, act, s, bank):
    act.wait_ge(s["xT_ready"], 1)
    act.copy(k.xT[:, :], k.ps[:, bank, :])


NORM_SEMS = ("var_ready", "eps_added", "rstd_ready", "x_ready", "xT_ready")


def small_attention(k, name, scale, keys, kv_rows, q_src, kv_src, biased=True, v_biased=True, masks=None,
                    scrambled=False):
    nc, ps = k.nc, k.ps
    NK = keys // kv_rows
    self_ = keys == SEQ
    with ExitStack() as ctx:
        def sb(n, shape, dt):
            return ctx.enter_context(nc.sbuf_tensor(f"{name}_{n}", shape, dt))

        qs = sb("qs", [P, H, SEQ], BF16)
        ks = sb("ks", [P, H, keys], BF16)
        v = sb("v", [P, NK, H, VW], F32)
        z = sb("z", [P, H // 4, SEQ], F32)
        probs = sb("probs", [P, PB, NK, SEQ], F32)
        if masks:
            mask_q = sb("mask_q", [P, NT, CTX], BF16)
            mask_k = sb("mask_k", [KT2, 2, SEQ], BF16)

        with ExitStack() as inner:
            def sbi(n, shape, dt):
                return inner.enter_context(nc.sbuf_tensor(f"{name}_{n}", shape, dt))

            qf = sbi("qf", [P, SEQ], F32)
            kf = sbi("kf", [P, keys], F32)
            rq = sbi("rq", [P, SEQ], F32)
            rk = sbi("rk", [P, keys], F32)
            qp = sbi("qp", [P, PARTS, SEQ], BF16)
            kp = sbi("kp", [P, PARTS, keys], BF16)
            if masks:
                wide_q = sbi("raw_q", [P, masks[0].shape[2]], I32)
                wide_k = sbi("raw_k", [KT2, masks[1].shape[2]], I32)
                raw_q, raw_k = wide_q[:, :], wide_k[:, :]
                if masks[0].shape[2] != NT * CTX:
                    raw_q, raw_k = raw_q.bitcast(U8), raw_k.bitcast(U8)
                raw_q = raw_q.rearrange("p (t k) -> p t k", t=NT)
                raw_k = raw_k.rearrange("p (t q) -> p t q", t=2)

            with phase(k, "chain", "q_proj", "k_proj", "v_proj", "q_sb", "k_sb", "q_parts", "k_parts", "q_stacked",
                       "k_stacked", "q_turned", "k_turned", "cleared",
                       "ones", "masks_in", "source", "rot") as (block, s):
                @block.tensor
                def _(pe):
                    if name == "L0a":
                        pe.matmul(ps[:, 7, :], w(k, name, "rot"), k.xT[:, :], start=True, stop=True).then_inc(s["rot"], 1)
                        pe.wait_ge(s["source"], 1)
                    if name == "L3a":
                        pe.matmul(ps[:, 7, :], w(k, name, "down"), k.xT[:, :], start=True, stop=True).then_inc(s["rot"], 1)
                        pe.wait_ge(s["source"], 1)
                    pe.matmul(ps[:, 0, :], w(k, name, "wq"), q_src[:, :], start=True, stop=True).then_inc(s["q_proj"], 1)
                    pe.matmul(ps[:, 1, 0:keys], w(k, name, "wk"), kv_src[:, :], start=True, stop=True
                              ).then_inc(s["k_proj"], 1)
                    for t in range(NK):
                        last = pe.matmul(ps[0:kv_rows, 2, t * D:(t + 1) * D], kv_src[:, t * kv_rows:(t + 1) * kv_rows],
                                         w(k, name, "wv"), start=True, stop=True)
                    last.then_inc(s["v_proj"], 1)

                @block.scalar
                def _(act):
                    if name == "L3a":
                        act.wait_ge(s["rot"], 1)
                        act.copy(k.src[:, :], ps[:, 7, :]).then_inc(s["source"], 1)
                    act.wait_ge(s["q_proj"], 1)
                    qin, qout = ps[:, 0, :], qf[:, :]
                    if scrambled:
                        qin = ps[:, 0, :].rearrange("p (hi lo) -> p lo hi", lo=16)
                        qout = qf[:, :].rearrange("p (lo hi) -> p lo hi", lo=16)
                    act.activation(qout, qin, ACT.Identity, bias=w(k, name, "bq") if biased else 0.0
                                   ).then_inc(s["q_sb"], 1)
                    act.wait_ge(s["k_proj"], 1)
                    act.activation(kf[:, :], ps[:, 1, 0:keys], ACT.Identity, bias=w(k, name, "bk") if biased else 0.0
                                   ).then_inc(s["k_sb"], 1)

                @block.vector
                def _(dve):
                    chain = Chain(dve, s["chain"])
                    if name == "L0a":
                        chain(dve.tensor_tensor(rq[:, :], k.xT[:, :], w(k, name, "cos"), ALU.mult))
                        dve.wait_ge(s["rot"], 1)
                        chain(dve.tensor_tensor(qf[:, :], ps[:, 7, :], w(k, name, "sin"), ALU.mult))
                        dve.tensor_tensor(k.src[:, :], rq[:, :], qf[:, :], ALU.add).then_inc(s["source"], 1)
                        dve.wait_ge(s["source"], 1)
                    chain(dve.memset(v[:, :, :, :], 0.0))
                    dve.memset(v[0:kv_rows, :, :, DH:DH + 1], 1.0)
                    for full, rest, parts, ready, done in ((qf, rq, qp, s["q_sb"], s["q_parts"]),
                                                           (kf, rk, kp, s["k_sb"], s["k_parts"])):
                        dve.wait_ge(ready, 1)
                        chain(dve.tensor_copy(parts[:, 0, :], full[:, :]))
                        chain(dve.tensor_tensor(rest[:, :], full[:, :], parts[:, 0, :], ALU.subtract))
                        chain(dve.tensor_copy(parts[:, 1, :], rest[:, :]))
                        dve.tensor_tensor(parts[:, 2, :], rest[:, :], parts[:, 1, :], ALU.subtract).then_inc(done, 1)
                    if kv_rows < P:
                        dve.memset(probs[64:P, :, :, :], 0.0)
                    dve.wait_ge(s["v_proj"], 1)
                    for t in range(NK):
                        out = v[0:kv_rows, t, :, 0:DH]
                        pv = ps[0:kv_rows, 2, t * D:(t + 1) * D].rearrange("p (h d) -> p h d", h=H)
                        if v_biased:
                            dve.tensor_tensor(out, pv, w(k, name, "bv", kv_rows).rearrange("p (h d) -> p h d", h=H),
                                              ALU.add)
                        else:
                            dve.tensor_copy(out, pv)
                    if masks:
                        dve.wait_ge(s["masks_in"], 32)
                        dve.tensor_scalar(mask_q[:, :, :], raw_q, 0.0, MASKED, masks[2], ALU.mult)
                        dve.tensor_scalar(mask_k[:, :, :], raw_k, 0.0, MASKED, masks[2], ALU.mult)

                @block.gpsimd
                def _(pool):
                    pool.memset(qs[64:P, :, :].rearrange("p h t -> p (h t)").bitcast(F32), 0.0).then_inc(s["cleared"], 1)
                    pool.memset(ks[64:P, :, :].rearrange("p h t -> p (h t)").bitcast(F32), TWO_ONES
                                ).then_inc(s["ones"], 1)

                @block.sync
                def _(sp):
                    if masks:
                        sp.dma_start(wide_q[:, :], masks[0][bass.ds(k.b, 1)].rearrange("o p k -> p (o k)")
                                     ).then_inc(s["masks_in"], 16)
                        sp.dma_start(wide_k[:, :], masks[1][bass.ds(k.b, 1)].rearrange("o p q -> p (o q)")
                                     ).then_inc(s["masks_in"], 16)
                    N = PARTS * DH
                    sp.wait_ge(s["q_parts"], 1)
                    for p in range(PARTS):
                        sp.dma_start(qs[DH * p:DH * (p + 1), :, :], qp[:, p, :]).then_inc(s["q_stacked"], 16)
                    sp.wait_ge(s["k_parts"], 1)
                    for p in range(PARTS):
                        sp.dma_start(ks[DH * p:DH * (p + 1), :, :], kp[:, p, :]).then_inc(s["k_stacked"], 16)
                    sp.wait_ge(s["q_stacked"], 16 * PARTS)
                    sp.wait_ge(s["cleared"], 1)
                    for to, at, n in ((N, DH, 2 * DH), (N + 2 * DH, 0, DH), (2 * N, 2 * DH, DH), (2 * N + DH, 0, 2 * DH)):
                        sp.dma_start(qs[to:to + n, :, :], qs[at:at + n, :, :]).then_inc(s["q_turned"], 16)
                    sp.wait_ge(s["k_stacked"], 16 * PARTS)
                    sp.wait_ge(s["ones"], 1)
                    for to in (N, 2 * N):
                        sp.dma_start(ks[to:to + N, :, :], ks[0:N, :, :]).then_inc(s["k_turned"], 16)
                    sp.wait_ge(s["q_turned"], 16 * 4)
                    sp.wait_ge(s["k_turned"], 16 * 2)

        attend(k, name, scale, keys, kv_rows, NK, self_, qs, ks, v, z, probs,
               (mask_q, mask_k) if masks else None, sb)
        small_output(k, name, z, scrambled, sb, biased=name not in ("L3x",))


def attend(k, name, scale, keys, kv_rows, NK, self_, qs, ks, v, z, probs, masks, sb):
    nc, ps = k.nc, k.ps
    G = 4
    LOOK = 6 if self_ else 7
    UNITS = NT if self_ else 2
    PER = NT // UNITS
    RING = 3
    MT_BANK, ST_BANK, Z_BANK = 3, 4, 6
    negmax = sb("negmax", [P, NT, H], F32)
    rest = sb("rest", [P, H // G, NT, G], F32)
    mparts = sb("mparts", [P, H // G, NT, PARTS, G], BF16)
    mt = sb("mt", [PARTS * G, H // G, SEQ], BF16)
    mt_ps = ps[:, MT_BANK, :].bitcast(BF16)

    with phase(k, "chain", "scores", "maxed", "split", "mt_ready", "mt_sb", "mt_row", "scoresT", "exped", "head_done",
               "z_out") as (block, s):
        @block.tensor
        def _(pe):
            def scores(h, qt):
                i, t = h * UNITS + qt // PER, qt % PER
                if t == 0 and i >= RING:
                    pe.wait_ge(s["maxed"], i - RING + 1)
                out = ps[:, i % RING, 256 * t:256 * t + keys]
                last = pe.matmul(out, qs[:, h, qt * P:(qt + 1) * P], ks[:, h, :], start=True, stop=not masks)
                if masks:
                    last = pe.matmul(out, wb(k, "ident"), masks[0][:, qt, :], start=False, stop=True)
                if t == PER - 1:
                    last.then_inc(s["scores"], 1)

            def turn_maxima(g):
                pe.wait_ge(s["split"], g + 1)
                if g:
                    pe.wait_ge(s["mt_sb"], g)
                for t in range(NT):
                    last = pe.transpose(mt_ps[0:PARTS * G, t * P:(t + 1) * P],
                                        mparts[:, g, t, :, :].rearrange("p a b -> p (a b)"), wb(k, "ident"))
                last.then_inc(s["mt_ready"], 1)

            def scores_turned(h, t):
                if h % G == 0 and t == 0:
                    pe.wait_ge(s["mt_row"], 16 * (h // G + 1))
                i = h * NK + t
                if i >= 2:
                    pe.wait_ge(s["exped"], i - 1)
                out = ps[0:kv_rows, ST_BANK + i % 2, :]
                last = pe.matmul(out, ks[:, h, t * kv_rows:(t + 1) * kv_rows], qs[:, h, :], start=True, stop=not masks)
                if masks:
                    last = pe.matmul(out, wb(k, "ident")[0:KT2, 0:KT2], masks[1][:, t, :], start=False, stop=True)
                last.then_inc(s["scoresT"], 1)

            def weigh(h, t):
                g, o = h // G, VW * (h % G)
                pe.wait_ge(s["exped"], h * NK + t + 1)
                if h % G == 0 and t == 0 and g >= 2:
                    pe.wait_ge(s["z_out"], g - 1)
                last = pe.matmul(ps[o:o + VW, Z_BANK + g % 2, :], v[:, t, h, :], probs[:, h % PB, t, :],
                                 start=t == 0, stop=t == NK - 1, tile_position=(0, o))
                if t == NK - 1:
                    last.then_inc(s["head_done"], 1)

            for step in range(-LOOK, H + 1):
                if (step + LOOK) % G == 0 and 0 < step + LOOK <= H:
                    turn_maxima((step + LOOK) // G - 1)
                for t in range(NT):
                    if step + LOOK < H:
                        scores(step + LOOK, t)
                    if 0 <= step < H and t < NK:
                        scores_turned(step, t)
                    if 0 <= step - 1 < H and t < NK:
                        weigh(step - 1, t)

        @block.vector
        def _(dve):
            chain = Chain(dve, s["chain"])

            def maxima(h):
                for u in range(UNITS):
                    i = h * UNITS + u
                    dve.wait_ge(s["scores"], i + 1)
                    if self_:
                        src, out = ps[:, i % RING, 0:keys], negmax[:, u, h:h + 1]
                    else:
                        src = ps[:, i % RING, :].rearrange("p (t k) -> p t k", t=2)[:, :, 0:keys]
                        out = negmax[:, 2 * u:2 * u + 2, h]
                    dve.tensor_reduce(out, src, AX.X, ALU.max, negate=True).then_inc(s["maxed"], 1)

            def split(g):
                m = negmax[:, :, g * G:(g + 1) * G]
                dve.wait_ge(s["maxed"], (g + 1) * G * UNITS)
                chain(dve.tensor_copy(mparts[:, g, :, 0, :], m))
                chain(dve.tensor_tensor(rest[:, g], m, mparts[:, g, :, 0, :], ALU.subtract))
                chain(dve.tensor_copy(mparts[:, g, :, 1, :], rest[:, g]))
                dve.tensor_tensor(mparts[:, g, :, 2, :], rest[:, g], mparts[:, g, :, 1, :], ALU.subtract
                                  ).then_inc(s["split"], 1)

            for h in range(H):
                maxima(h)
                if h % G == G - 1:
                    split(h // G)

        @block.scalar
        def _(act):
            def copy_out(g):
                act.wait_ge(s["head_done"], (g + 1) * G)
                act.copy(z[:, g, :], ps[:, Z_BANK + g % 2, :]).then_inc(s["z_out"], 1)

            for step in range(-LOOK, H):
                if (step + LOOK) % G == 0 and 0 < step + LOOK <= H:
                    g = (step + LOOK) // G - 1
                    act.wait_ge(s["mt_ready"], g + 1)
                    act.copy(mt[:, g, :], mt_ps[0:PARTS * G, 0:SEQ]).then_inc(s["mt_sb"], 1)
                if step >= 0:
                    for t in range(NK):
                        i = step * NK + t
                        if step >= PB and t == 0:
                            act.wait_ge(s["head_done"], step - PB + 1)
                        act.wait_ge(s["scoresT"], i + 1)
                        act.activation(probs[0:kv_rows, step % PB, t, :], ps[0:kv_rows, ST_BANK + i % 2, :], ACT.Exp,
                                       scale=scale).then_inc(s["exped"], 1)
                if step >= 2 and (step - 1) % G == G - 1:
                    copy_out((step - 1) // G)
            copy_out(H // G - 1)

        @block.sync
        def _(sp):
            for g in range(H // G):
                sp.wait_ge(s["mt_sb"], g + 1)
                sp.dma_start(qs[ROWS:ROWS + PARTS, g * G:(g + 1) * G, :], mt[:, g, :]).then_inc(s["mt_row"], 16)


def small_output(k, name, z, scrambled, sb, biased):
    nc, ps = k.nc, k.ps
    inv = sb("inv", [P, NT, H, 1], F32)
    zn = sb("zn", [P, NT, H, DH], F32)
    znT = sb("znT", [P, SEQ], F32)
    dec = sb("dec", [P, NT, D], F32)
    with phase(k, "chain", "z_ready", "zn_ready", "znT_ready", "znT_sb", "y_ready", *NORM_SEMS) as (block, s):
        @block.vector
        def _(dve):
            chain = Chain(dve, s["chain"])
            for t in range(NT):
                dve.wait_ge(s["z_ready"], t + 1)
                zq = ps[:, t, :].rearrange("p (h e) -> p h e", e=VW)
                chain(dve.reciprocal(inv[:, t, :, :], zq[:, :, DH:DH + 1]))
                dve.tensor_tensor(zn[:, t, :, :], zq[:, :, 0:DH], inv[:, t, :, :].to_broadcast([P, H, DH]), ALU.mult
                                  ).then_inc(s["zn_ready"], 1)
            if not scrambled:
                dve.wait_ge(s["y_ready"], 1)
                norm_vector(k, dve, chain, s, ps[:, 5, :].rearrange("p (t d) -> p t d", t=NT))
                return
            dve.wait_ge(s["zn_ready"], NT)
            for a in range(4):
                for b in range(4):
                    src = zn[32 * a:32 * a + 32, :, b::4, :].rearrange("p j t d -> p t j d")
                    out = dec[32 * b:32 * b + 32, :, :].rearrange("p t (j a d) -> p t j a d", j=4, a=4)[:, :, :, a, :]
                    last = dve.tensor_copy(out, src)
            chain(last)
            chain(dve.tensor_tensor(k.resid[:, :, :], dec[:, :, :], k.x[:, :, :], ALU.add))
            norm_stats(k, dve, chain, s["var_ready"], s["rstd_ready"], 1)
            for t in range(NT):
                last = dve.tensor_scalar(dec[:, t, :], k.resid[:, t, :], k.mv[:, t, 0:1], k.rstd[:, t:t + 1],
                                         ALU.subtract, ALU.mult)
            chain(last)
            gamma = w(k, name, "gamma").unsqueeze(1).to_broadcast([P, NT, D])
            beta = w(k, name, "beta").unsqueeze(1).to_broadcast([P, NT, D])
            chain(dve.tensor_tensor(zn[:, :, :, :].rearrange("p t h d -> p t (h d)"), dec[:, :, :], gamma, ALU.mult))
            chain(dve.tensor_tensor(dec[:, :, :], zn[:, :, :, :].rearrange("p t h d -> p t (h d)"), beta, ALU.add))
            chain(dve.tensor_tensor(k.resid[:, :, :], dec[:, :, :], k.x[:, :, :], ALU.add))
            norm_stats(k, dve, chain, s["var_ready"], s["rstd_ready"], 2)
            for t in range(NT):
                last = dve.tensor_scalar(k.x[:, t, :], k.resid[:, t, :], k.mv[:, t, 0:1], k.rstd[:, t:t + 1],
                                         ALU.subtract, ALU.mult)
            last.then_inc(s["x_ready"], 1)

        @block.gpsimd
        def _(pool):
            norm_gpsimd(k, pool, s)
            if scrambled:
                norm_gpsimd(k, pool, s, 2)

        @block.tensor
        def _(pe):
            for t in range(NT):
                for g in range(H // 4):
                    last = pe.transpose(ps[:, t, g * P:(g + 1) * P], z[:, g, t * P:(t + 1) * P], k.ident)
                last.then_inc(s["z_ready"], 1)
            if not scrambled:
                for t in range(NT):
                    pe.wait_ge(s["zn_ready"], t + 1)
                    last = pe.transpose(ps[:, 4, t * P:(t + 1) * P], zn[:, t, :, :].rearrange("p h d -> p (h d)"), k.ident)
                last.then_inc(s["znT_ready"], 1)
                pe.wait_ge(s["znT_sb"], 1)
                for t in range(NT):
                    last = pe.matmul(ps[:, 5, t * D:(t + 1) * D], znT[:, t * P:(t + 1) * P], w(k, name, "wo"),
                                     start=True, stop=not biased)
                    if biased:
                        last = pe.matmul(ps[:, 5, t * D:(t + 1) * D], w(k, "const", "one", 1), w(k, name, "bo", 1),
                                         start=False, stop=True)
                last.then_inc(s["y_ready"], 1)
            norm_tensor(k, pe, s, 6)

        @block.scalar
        def _(act):
            if not scrambled:
                act.wait_ge(s["znT_ready"], 1)
                act.copy(znT[:, :], ps[:, 4, :]).then_inc(s["znT_sb"], 1)
            norm_scalar(k, act, s, 6)


def gated_ffn(k, stream_loaded):
    nc, ps = k.nc, k.ps
    M = 4
    name = "L0f"
    w1, w2 = ws(k, name, "w1"), ws(k, name, "w2")
    h1w, h2w = (ws(k, name, n).rearrange("p (t o) -> p t o", t=M) for n in ("h1", "h2"))
    w3 = ws(k, name, "w3").rearrange("p (t o) -> p t o", t=M)
    with ExitStack() as ctx:
        a = ctx.enter_context(nc.sbuf_tensor("ffn_a", [P, M, SEQ], F32))
        g = ctx.enter_context(nc.sbuf_tensor("ffn_g", [P, M, SEQ], F32))
        y = ctx.enter_context(nc.sbuf_tensor("ffn_y", [P, NT, D], F32))
        with phase(k, "chain", "up_ready", "silu_ready", "prod_ready", "h1_ready", "h1_sb", "h2_ready", "h2_sb",
                   "y_ready", *NORM_SEMS) as (block, s):
            @block.tensor
            def _(pe):
                pe.wait_ge(stream_loaded, 16)
                for m in range(M):
                    if m >= 2:
                        pe.wait_ge(s["prod_ready"], m - 1)
                    b = 2 * (m % 2)
                    pe.matmul(ps[:, b, :], w1[:, m * P:(m + 1) * P], k.xT[:, :], start=True, stop=True)
                    pe.matmul(ps[:, b + 1, :], w2[:, m * P:(m + 1) * P], k.xT[:, :], start=True, stop=True
                              ).then_inc(s["up_ready"], 1)
                for src, wt, got, done, freed, b in ((a, h1w, s["prod_ready"], s["h1_ready"], s["h1_sb"], 4),
                                                     (g, h2w, s["h1_sb"], s["h2_ready"], s["h2_sb"], 6)):
                    for m in range(M):
                        if m >= 2:
                            pe.wait_ge(freed, m - 1)
                        for t in range(M):
                            if m == 0:
                                pe.wait_ge(got, t + 1)
                            last = pe.matmul(ps[:, b + m % 2, :], wt[:, t, m * P:(m + 1) * P], src[:, t, :],
                                             start=t == 0, stop=t == M - 1)
                        last.then_inc(done, 1)
                pe.wait_ge(s["h2_sb"], M)
                for t in range(NT):
                    for m in range(M):
                        last = pe.matmul(ps[:, 0, t * D:(t + 1) * D], a[:, m, t * P:(t + 1) * P], w3[:, m, :],
                                         start=m == 0, stop=m == M - 1)
                last.then_inc(s["y_ready"], 1)
                norm_tensor(k, pe, s, 1)

            @block.scalar
            def _(act):
                for m in range(M):
                    act.wait_ge(s["up_ready"], m + 1)
                    act.activation(g[:, m, :], ps[:, 2 * (m % 2), :], ACT.Silu, scale=ws(k, name, "s1")[:, m:m + 1]
                                   ).then_inc(s["silu_ready"], 1)
                for m in range(M):
                    act.wait_ge(s["h1_ready"], m + 1)
                    act.activation(g[:, m, :], ps[:, 4 + m % 2, :], ACT.Gelu, scale=ws(k, name, "t1")[:, m:m + 1]
                                   ).then_inc(s["h1_sb"], 1)
                for m in range(M):
                    act.wait_ge(s["h2_ready"], m + 1)
                    act.activation(a[:, m, :], ps[:, 6 + m % 2, :], ACT.Gelu, scale=ws(k, name, "t2")[:, m:m + 1]
                                   ).then_inc(s["h2_sb"], 1)
                norm_scalar(k, act, s, 1)

            @block.vector
            def _(dve):
                chain = Chain(dve, s["chain"])
                for m in range(M):
                    dve.wait_ge(s["silu_ready"], m + 1)
                    dve.scalar_tensor_tensor(out=a[:, m, :], in0=ps[:, 2 * (m % 2) + 1, :],
                                             scalar=ws(k, name, "s2")[:, m:m + 1], in1=g[:, m, :],
                                             op0=ALU.mult, op1=ALU.mult).then_inc(s["prod_ready"], 1)
                dve.wait_ge(s["y_ready"], 1)
                chain(dve.tensor_tensor(y[:, :, :], ps[:, 0, :].rearrange("p (t d) -> p t d", t=NT),
                                        ws(k, name, "s3").unsqueeze(1).to_broadcast([P, NT, D]), ALU.mult))
                norm_vector(k, dve, chain, s, y[:, :, :])

            @block.gpsimd
            def _(pool):
                norm_gpsimd(k, pool, s)


def mamba(k, next_stream):
    nc, ps = k.nc, k.ps
    name, J, N, R = "L1m", 2, 16, 8
    TAPS = 4
    conv = w(k, name, "conv").rearrange("p (j t) -> p j t", j=J)
    w_x = w(k, name, "w_x").rearrange("p (j n) -> p j n", j=J)
    w_dt = w(k, name, "w_dt", R)
    w_out = w(k, name, "w_out").rearrange("p (j n) -> p j n", j=J)
    with ExitStack() as ctx:
        def sb(n, shape, dt=F32):
            return ctx.enter_context(nc.sbuf_tensor(f"mamba_{n}", shape, dt))

        xc = sb("xc", [P, J, SEQ])
        sz = sb("sz", [P, J, SEQ])
        delta = sb("delta", [P, J, SEQ])
        du = sb("du", [P, J, SEQ])
        xd = sb("xd", [R, SEQ])
        bc = sb("bc", [PARTS * 2 * N, SEQ], BF16)
        aneg = sb("aneg", [P, J * N])
        with ExitStack() as inner:
            def sbi(n, shape):
                return inner.enter_context(nc.sbuf_tensor(f"mamba_{n}", shape, F32))

            xpad = sbi("xpad", [P, J, SEQ + TAPS - 1])
            acc = sbi("acc", [P, J, SEQ])
            vv = sbi("v", [P, J, SEQ])
            low = sbi("low", [P, J, SEQ])
            u = sbi("u", [P, J, SEQ])
            w1 = sbi("w1", [P, J, SEQ])
            ln = sbi("ln", [P, J, SEQ])
            rest = sbi("rest", [PARTS * 2 * N, SEQ])
            with phase(k, "chain", "xz", "xi_sb", "conv_done", "xc_sb", "xd_ready", "xd_sb", "dt_ready", "low_ready",
                       "u_ready", "w1_ready", "ln_ready", "a_ready", "padded", "bc_ready") as (block, s):
                @block.sync
                def _(sp):
                    next_stream(sp)

                @block.tensor
                def _(pe):
                    for m in range(2 * J):
                        pe.matmul(ps[:, m, :], w(k, name, "w_in")[:, m * P:(m + 1) * P], k.xT[:, :], start=True,
                                  stop=True).then_inc(s["xz"], 1)
                    pe.wait_ge(s["xc_sb"], J)
                    for j in range(J):
                        last = pe.matmul(ps[0:R, 4, :], w_x[:, j, 0:R], xc[:, j, :], start=j == 0, stop=j == J - 1)
                    last.then_inc(s["xd_ready"], 1)
                    for j in range(J):
                        last = pe.matmul(ps[0:PARTS * 2 * N, 7, :], w_x[:, j, R:R + PARTS * 2 * N], xc[:, j, :], start=j == 0, stop=j == J - 1)
                    last.then_inc(s["bc_ready"], 1)
                    pe.wait_ge(s["xd_sb"], 1)
                    for j in range(J):
                        last = pe.matmul(ps[:, 5 + j, :], w_dt[:, j * P:(j + 1) * P], xd[0:R, :], start=True, stop=True)
                    last.then_inc(s["dt_ready"], 1)

                @block.scalar
                def _(act):
                    for j in range(J):
                        act.wait_ge(s["xz"], j + 1)
                        act.copy(xpad[:, j, TAPS - 1:], ps[:, j, :]).then_inc(s["xi_sb"], 1)
                    for j in range(J):
                        act.wait_ge(s["xz"], J + j + 1)
                        act.activation(sz[:, j, :], ps[:, J + j, :], ACT.Silu)
                    for j in range(J):
                        act.wait_ge(s["conv_done"], j + 1)
                        act.activation(xc[:, j, :], acc[:, j, :], ACT.Silu, bias=w(k, name, "cb")[:, j:j + 1]
                                       ).then_inc(s["xc_sb"], 1)
                    act.activation(aneg[:, :], w(k, name, "alog"), ACT.Exp).then_inc(s["a_ready"], 1)
                    act.wait_ge(s["xd_ready"], 1)
                    act.copy(xd[:, :], ps[0:R, 4, :]).then_inc(s["xd_sb"], 1)
                    act.wait_ge(s["low_ready"], 1)
                    act.activation(u[:, :, :], low[:, :, :], ACT.Exp).then_inc(s["u_ready"], 1)
                    act.wait_ge(s["w1_ready"], 1)
                    act.activation(ln[:, :, :], w1[:, :, :], ACT.Ln).then_inc(s["ln_ready"], 1)

                @block.gpsimd
                def _(pool):
                    pool.memset(xpad[:, :, 0:TAPS - 1], 0.0).then_inc(s["padded"], 1)

                @block.vector
                def _(dve):
                    chain = Chain(dve, s["chain"])
                    dve.wait_ge(s["padded"], 1)
                    for j in range(J):
                        dve.wait_ge(s["xi_sb"], j + 1)
                        chain(dve.tensor_scalar(acc[:, j, :], xpad[:, j, 0:SEQ], conv[:, j, 0:1], None, ALU.mult))
                        for t in range(1, TAPS):
                            last = dve.scalar_tensor_tensor(out=acc[:, j, :], in0=xpad[:, j, t:t + SEQ],
                                                            scalar=conv[:, j, t:t + 1], in1=acc[:, j, :],
                                                            op0=ALU.mult, op1=ALU.add)
                            if t < TAPS - 1:
                                chain(last)
                        last.then_inc(s["conv_done"], 1)
                    dve.wait_ge(s["a_ready"], 1)
                    chain(dve.tensor_scalar(aneg[:, :], aneg[:, :], -1.0, None, ALU.mult))
                    dve.wait_ge(s["dt_ready"], 1)
                    for j in range(J):
                        last = dve.tensor_scalar(vv[:, j, :], ps[:, 5 + j, :], w(k, name, "bdt")[:, j:j + 1], None, ALU.add)
                    chain(last)
                    dve.scalar_tensor_tensor(out=low[:, :, :], in0=vv[:, :, :], scalar=-1.0, in1=vv[:, :, :],
                                             op0=ALU.mult, op1=ALU.min).then_inc(s["low_ready"], 1)
                    dve.wait_ge(s["bc_ready"], 1)
                    n = PARTS * 2 * N
                    chain(dve.tensor_copy(bc[:, :], ps[0:n, 7, :]))
                    chain(dve.tensor_tensor(rest[:, :], ps[0:n, 7, :], bc[:, :], ALU.subtract))
                    dve.tensor_copy(bc[32:64, :], rest[32:64, :])
                    chain(dve.tensor_copy(bc[64:n, :], rest[64:n, :]))
                    chain(dve.tensor_tensor(bc[64:n, :], rest[64:n, :], bc[64:n, :], ALU.subtract))
                    dve.wait_ge(s["u_ready"], 1)
                    dve.tensor_scalar(w1[:, :, :], u[:, :, :], 1.0, None, ALU.add).then_inc(s["w1_ready"], 1)
                    dve.wait_ge(s["w1_ready"], 1)
                    chain(dve.scalar_tensor_tensor(out=low[:, :, :], in0=w1[:, :, :], scalar=-1.0, in1=u[:, :, :],
                                                   op0=ALU.add, op1=ALU.subtract))
                    dve.wait_ge(s["ln_ready"], 1)
                    chain(dve.scalar_tensor_tensor(out=vv[:, :, :], in0=vv[:, :, :], scalar=0.0, in1=ln[:, :, :],
                                                   op0=ALU.max, op1=ALU.add))
                    chain(dve.tensor_tensor(delta[:, :, :], vv[:, :, :], low[:, :, :], ALU.subtract))
                    chain(dve.tensor_tensor(du[:, :, :], delta[:, :, :], xc[:, :, :], ALU.mult))

        RING = 6
        BC_BANKS = (0, 2, 6)
        AHEAD = len(BC_BANKS)
        bsb = sb("b", [P, AHEAD, SEQ])
        da = sb("da", [P, RING, SEQ])
        dbu = sb("dbu", [P, RING, SEQ])
        hs = sb("h", [P, RING, SEQ])
        hc = sb("hc", [P, RING, SEQ])
        y = sb("y", [P, J, SEQ])
        with phase(k, "chain", "bc_ready", "b_sb", "da_ready", "dbu_ready", "scanned", "hc_ready", "summed", "y_in",
                   "y_ready", *NORM_SEMS) as (block, s):
            @block.tensor
            def _(pe):
                def spread(n):
                    if n >= AHEAD:
                        pe.wait_ge(s["b_sb"], n - AHEAD + 1)
                        pe.wait_ge(s["hc_ready"], J * (n - AHEAD + 1))
                    for c in range(2):
                        rows3 = PARTS * 2 * N
                        last = pe.matmul(ps[:, BC_BANKS[n % AHEAD] + c, :],
                                         wb(k, "stacked", rows3)[:, c * N + n:c * N + n + 1].to_broadcast([rows3, P]),
                                         bc[:, :], start=True, stop=True)
                    last.then_inc(s["bc_ready"], 1)

                for n in range(AHEAD - 1):
                    spread(n)
                for n in range(N):
                    if n + AHEAD - 1 < N:
                        spread(n + AHEAD - 1)
                    for j in range(J):
                        pe.wait_ge(s["hc_ready"], J * n + j + 1)
                        pe.matmul(ps[:, 4 + j, :], k.ident, hc[:, (J * n + j) % RING, :], start=n == 0, stop=n == N - 1
                                  ).then_inc(s["summed"], 1)
                pe.wait_ge(s["y_in"], 1)
                for t in range(NT):
                    for j in range(J):
                        last = pe.matmul(ps[:, 0, t * D:(t + 1) * D], y[:, j, t * P:(t + 1) * P], w_out[:, j, :],
                                         start=j == 0, stop=j == J - 1)
                last.then_inc(s["y_ready"], 1)
                norm_tensor(k, pe, s, 1)

            @block.scalar
            def _(act):
                for n in range(N):
                    act.wait_ge(s["bc_ready"], n + 1)
                    if n >= AHEAD:
                        act.wait_ge(s["dbu_ready"], J * (n - AHEAD + 1))
                    act.copy(bsb[:, n % AHEAD, :], ps[:, BC_BANKS[n % AHEAD], :]).then_inc(s["b_sb"], 1)
                    for j in range(J):
                        i = J * n + j
                        if i >= RING:
                            act.wait_ge(s["scanned"], i - RING + 1)
                        act.activation(da[:, i % RING, :], delta[:, j, :], ACT.Exp, scale=aneg[:, j * N + n:j * N + n + 1]
                                       ).then_inc(s["da_ready"], 1)
                norm_scalar(k, act, s, 1)

            @block.gpsimd
            def _(pool):
                for n in range(N):
                    pool.wait_ge(s["b_sb"], n + 1)
                    for j in range(J):
                        i = J * n + j
                        if i >= RING:
                            pool.wait_ge(s["scanned"], i - RING + 1)
                        pool.tensor_tensor(dbu[:, i % RING, :], du[:, j, :], bsb[:, n % AHEAD, :], ALU.mult
                                           ).then_inc(s["dbu_ready"], 1)
                norm_gpsimd(k, pool, s)

            @block.vector
            def _(dve):
                chain = Chain(dve, s["chain"])

                def scan(i):
                    dve.wait_ge(s["da_ready"], i + 1)
                    dve.wait_ge(s["dbu_ready"], i + 1)
                    if i >= RING:
                        dve.wait_ge(s["hc_ready"], i - RING + 1)
                    dve.tensor_tensor_scan(out=hs[:, i % RING, :], data0=da[:, i % RING, :], data1=dbu[:, i % RING, :],
                                           initial=0.0, op0=ALU.mult, op1=ALU.add).then_inc(s["scanned"], 1)

                scan(0)
                for i in range(J * N):
                    if i + 1 < J * N:
                        scan(i + 1)
                    dve.wait_ge(s["scanned"], i + 1)
                    if i >= RING:
                        dve.wait_ge(s["summed"], i - RING + 1)
                    dve.tensor_tensor(hc[:, i % RING, :], hs[:, i % RING, :], ps[:, BC_BANKS[i // J % AHEAD] + 1, :], ALU.mult
                                      ).then_inc(s["hc_ready"], 1)
                dve.wait_ge(s["summed"], J * N)
                for j in range(J):
                    last = dve.scalar_tensor_tensor(out=y[:, j, :], in0=xc[:, j, :], scalar=w(k, name, "dskip")[:, j:j + 1],
                                                    in1=ps[:, 4 + j, :], op0=ALU.mult, op1=ALU.add)
                chain(last)
                dve.tensor_tensor(y[:, :, :], y[:, :, :], sz[:, :, :], ALU.mult).then_inc(s["y_in"], 1)
                dve.wait_ge(s["y_ready"], 1)
                norm_vector(k, dve, chain, s, ps[:, 0, :].rearrange("p (t d) -> p t d", t=NT))


WD = 64


def wide_attend(k, name, heads, scale, qT, kT, v, zT, sb, gateT=None):
    nc, ps = k.nc, k.ps
    G, LOOK = 4, 6
    PAIRS = heads // 2
    negmax = sb("negmax", [P, NT, heads], F32)
    rest = sb("rest", [P, heads // G, NT, G], F32)
    mparts = sb("mparts", [P, heads // G, NT, PARTS, G], BF16)
    mt = sb("mt", [PARTS * G, 2, SEQ], BF16)
    probs = sb("probs", [P, 2, NT, SEQ], F32)
    sumrow = sb("sumrow", [P, SEQ], F32)
    sums = sb("sums", [G, 2, SEQ], F32)
    mt_ps = ps[:, 3, :].bitcast(BF16)
    sel = wb(k, "sel", PARTS * G).rearrange("p (g n) -> p g n", g=G)
    spread = w(k, "const", "spread", G).rearrange("p (j n) -> p j n", j=2)
    SPREAD, TURNED, OUT = 2, (4, 5), (6, 7)
    EARLY = LOOK * NT

    def scores_bank(i):
        return (0, 1, *OUT)[i % 4] if i < EARLY else i % 2

    with phase(k, "chain", "scores", "maxed", "split", "mt_ready", "mt_sb", "scoresT", "exped", "head_done",
               "z_out", "sums_sb", "sums_in", "inverted", "spread", "z_done") as (block, s):
        @block.tensor
        def _(pe):
            def scores(h, qt):
                i = h * NT + qt
                back = 4 if i < EARLY + 2 else 2
                if i >= back:
                    pe.wait_ge(s["maxed"], i - back + 1)
                n = (qt + 1) * P
                pe.matmul(ps[:, scores_bank(i), 0:n], qT[:, h // 2, qt * P:n], kT[:, h, 0:n],
                          start=True, stop=True)
                pe.matmul(ps[:, scores_bank(i), qt * P:n], wb(k, "ident"), wb(k, "tri"), start=False, stop=True,
                          skip_group_check=True).then_inc(s["scores"], 1)

            def turn_maxima(g):
                pe.wait_ge(s["split"], g + 1)
                if g:
                    pe.wait_ge(s["mt_sb"], g)
                for t in range(NT):
                    last = pe.transpose(mt_ps[0:PARTS * G, t * P:(t + 1) * P],
                                        mparts[:, g, t, :, :].rearrange("p a b -> p (a b)"), wb(k, "ident"))
                last.then_inc(s["mt_ready"], 1)

            def scores_turned(h, t):
                if h % G == 0 and t == 0:
                    pe.wait_ge(s["mt_sb"], h // G + 1)
                i = h * NT + t
                if i >= 2:
                    pe.wait_ge(s["exped"], i - 1)
                q0 = t * P
                bank = TURNED[i % 2]
                pe.matmul(ps[:, bank, q0:], kT[:, h, q0:q0 + P], qT[:, h // 2, q0:],
                          start=True, stop=False)
                pe.matmul(ps[:, bank, q0:q0 + P], wb(k, "ident"), wb(k, "triT"), start=False, stop=False,
                          skip_group_check=True)
                pe.matmul(ps[:, bank, q0:], sel[:, h % G, :], mt[:, h // G % 2, q0:], start=False, stop=True
                          ).then_inc(s["scoresT"], 1)

            def weigh(h, t):
                o = WD * (h % 2)
                pe.wait_ge(s["exped"], h * NT + t + 1)
                if t == 0 and h < 2:
                    pe.wait_ge(s["maxed"], EARLY)
                elif t == 0:
                    pe.wait_ge(s["z_out"], h - 1)
                last = pe.matmul(ps[:, OUT[h % 2], t * P:], v[:, t, h // 2, o:o + 2 * WD], probs[:, h % 2, t, t * P:],
                                 start=t == 0, stop=t == NT - 1, skip_group_check=True)
                if t == NT - 1:
                    last.then_inc(s["head_done"], 1)

            def spread_inverse(r):
                pe.wait_ge(s["inverted"], r // 2 + 1)
                if r:
                    pe.wait_ge(s["z_done"], r)
                pe.matmul(ps[:, SPREAD, :], spread[:, r % 2, :], sums[:, r // 2 % 2, :], start=True, stop=True
                          ).then_inc(s["spread"], 1)

            for step in range(-LOOK, heads + 5):
                if (step + LOOK) % G == 0 and 0 < step + LOOK <= heads:
                    turn_maxima((step + LOOK) // G - 1)
                for t in range(NT):
                    if step + LOOK < heads:
                        scores(step + LOOK, t)
                    if 0 <= step < heads:
                        scores_turned(step, t)
                if 0 < step <= heads:
                    for t in range(NT):
                        weigh(step - 1, t)
                for wait in (3, 4):
                    if step - wait >= G and (step - wait) % G == 0:
                        spread_inverse((step - wait) // 2 - 2 + wait - 3)

        @block.sync
        def _(sp):
            for h in range(heads):
                sp.wait_ge(s["sums_sb"], h + 1)
                row = WD * (1 - h % 2)
                if h >= 2 * G and h % G == 0:
                    sp.wait_ge(s["z_done"], (h // G - 1) * 2)
                sp.dma_start(sums[h % G:h % G + 1, h // G % 2, :], sumrow[row:row + 1, :]
                             ).then_inc(s["sums_in"], 16)
                sp.wait_ge(s["sums_in"], 16 * (h + 1))

        @block.vector
        def _(dve):
            chain = Chain(dve, s["chain"])

            def maxima(h):
                for qt in range(NT):
                    i = h * NT + qt
                    dve.wait_ge(s["scores"], i + 1)
                    dve.tensor_reduce(negmax[:, qt, h:h + 1], ps[:, scores_bank(i), 0:(qt + 1) * P], AX.X,
                                      ALU.max, negate=True).then_inc(s["maxed"], 1)

            def split(g):
                m = negmax[:, :, g * G:(g + 1) * G]
                dve.wait_ge(s["maxed"], (g + 1) * G * NT)
                chain(dve.tensor_copy(mparts[:, g, :, 0, :], m))
                chain(dve.tensor_tensor(rest[:, g], m, mparts[:, g, :, 0, :], ALU.subtract))
                chain(dve.tensor_copy(mparts[:, g, :, 1, :], rest[:, g]))
                dve.tensor_tensor(mparts[:, g, :, 2, :], rest[:, g], mparts[:, g, :, 1, :], ALU.subtract
                                  ).then_inc(s["split"], 1)

            def invert(g, q):
                if q == 0:
                    dve.wait_ge(s["sums_in"], 16 * G * (g + 1))
                at = slice(q * P, (q + 1) * P)
                last = dve.reciprocal(sums[:, g % 2, at], sums[:, g % 2, at])
                if gateT is not None:
                    chain(last)
                    last = dve.tensor_tensor(sums[:, g % 2, at], sums[:, g % 2, at], gateT[:, g, at], ALU.mult)
                if q == NT - 1:
                    last.then_inc(s["inverted"], 1)
                else:
                    chain(last)

            def normalize(r):
                dve.wait_ge(s["spread"], r + 1)
                dve.wait_ge(s["z_out"], 2 * r + 2)
                dve.tensor_tensor(zT[:, r, :], zT[:, r, :], ps[:, SPREAD, :], ALU.mult).then_inc(s["z_done"], 1)

            for step in range(-LOOK, heads + 6):
                h = step + LOOK
                if h < heads:
                    maxima(h)
                    if h % G == G - 1:
                        split(h // G)
                g = step // G - 1
                if step >= G and g < heads // G and step % G == 2:
                    for q in range(NT):
                        invert(g, q)
                for wait in (4, 5):
                    if step - wait >= G and (step - wait) % G == 0:
                        normalize((step - wait) // 2 - 2 + wait - 4)

        @block.scalar
        def _(act):
            def copy_out(h):
                o = WD * (h % 2)
                act.wait_ge(s["head_done"], h + 1)
                if h >= 2:
                    act.wait_ge(s["sums_in"], 16 * (h - 1))
                act.copy(sumrow[WD - o:WD - o + 1, :], ps[WD - o:WD - o + 1, OUT[h % 2], :]
                         ).then_inc(s["sums_sb"], 1)
                act.wait_ge(s["sums_sb"], h + 1)
                act.copy(zT[o:o + WD, h // 2, :], ps[o:o + WD, OUT[h % 2], :]).then_inc(s["z_out"], 1)

            for step in range(-LOOK, heads + 1):
                if (step + LOOK) % G == 0 and 0 < step + LOOK <= heads:
                    g = (step + LOOK) // G - 1
                    act.wait_ge(s["mt_ready"], g + 1)
                    if g >= 2:
                        act.wait_ge(s["scoresT"], (g - 1) * G * NT)
                    act.copy(mt[:, g % 2, :], mt_ps[0:PARTS * G, 0:SEQ]).then_inc(s["mt_sb"], 1)
                for t in range(NT):
                    if 0 <= step < heads:
                        i = step * NT + t
                        if step >= 2 and t == 0:
                            act.wait_ge(s["head_done"], step - 1)
                        act.wait_ge(s["scoresT"], i + 1)
                        act.activation(probs[:, step % 2, t, t * P:], ps[:, TURNED[i % 2], t * P:], ACT.Exp, scale=scale
                                       ).then_inc(s["exped"], 1)
                    if t == 1 and step >= 2:
                        copy_out(step - 2)
            copy_out(heads - 1)


def top_one(k, dve, chain, values, key, best, picked, E):
    S4 = list(values.shape)
    chain(dve.tensor_reduce(best, values, AX.X, ALU.max))
    bc = lambda a: a.to_broadcast(S4)
    chain(dve.tensor_tensor(key, values, bc(best), ALU.is_equal))
    desc = w(k, "const", "desc")[:, 0:E].unsqueeze(1).to_broadcast([P, S4[1], E])
    chain(dve.tensor_tensor(key, key, desc, ALU.mult))
    return key


def expert_attention(k, stream_loaded):
    nc, ps = k.nc, k.ps
    name, HE, E = "L1g", 8, 8
    PAIRS = HE // 2
    at, _ = S_AT["L1e"]
    value = k.stream[:, 0:4096].rearrange("p (e n) -> p e n", e=E)
    output = k.stream[:, 4096:8192].rearrange("p (e r d) -> p e r d", e=E, r=PAIRS)
    with ExitStack() as ctx:
        def sb(n, shape, dt=F32):
            return ctx.enter_context(nc.sbuf_tensor(f"moa_{n}", shape, dt))

        zT = sb("zT", [P, PAIRS, SEQ])
        gate = sb("gate", [P, NT * HE, 1])
        gateT = sb("gateT", [4, HE // 4, SEQ])
        picked_b = sb("picked_b", [P, NT, HE * E], BF16)
        with ExitStack() as inner:
            def sbi(n, shape, dt=F32):
                return inner.enter_context(nc.sbuf_tensor(f"moa_{n}", shape, dt))

            qT = sbi("qT", [P, PAIRS, SEQ])
            kT = sbi("kT", [P, HE, SEQ])
            v = sbi("v", [P, NT, PAIRS, 3 * WD])
            heads_of = lambda t, r0, n: v[:, t, r0:r0 + n, :].rearrange("p r (j d) -> p r j d", j=3)[:, :, 0:3:2, :]
            gates = sbi("gates", [P, NT * HE, E])
            key = sbi("key", [P, NT * HE, E])
            kmax = sbi("kmax", [P, NT * HE, 1])
            picked = sbi("picked", [P, NT, HE, E], I32)
            with phase(k, "chain", "qk", "qk_sb", "logits", "gates", "picked", "values", "chosen", "gate",
                       "gateT_ready", "gateT_sb") as (block, s):
                @block.tensor
                def _(pe):
                    for t in range(NT):
                        last = pe.matmul(ps[:, 2, t * 64:(t + 1) * 64], k.xT[:, t * P:(t + 1) * P], w(k, name, "gate"),
                                         start=True, stop=True)
                    last.then_inc(s["logits"], 1)
                    for m in range(2 * PAIRS):
                        if m >= 2:
                            pe.wait_ge(s["qk_sb"], m - 1)
                        wt = w(k, name, "wq" if m % 2 == 0 else "wk")
                        pe.matmul(ps[:, m % 2, :], wt[:, m // 2 * P:(m // 2 + 1) * P], k.xT[:, :], start=True, stop=True
                                  ).then_inc(s["qk"], 1)
                    pe.wait_ge(stream_loaded, 16)
                    for e in range(E):
                        for t in range(NT):
                            i = e * NT + t
                            if i >= 4:
                                pe.wait_ge(s["chosen"], i - 3)
                            pe.matmul(ps[:, 4 + i % 4, :], k.xT[:, t * P:(t + 1) * P], value[:, e, :], start=True,
                                      stop=True).then_inc(s["values"], 1)
                    pe.wait_ge(s["gate"], 1)
                    pe.wait_ge(s["qk_sb"], 2 * PAIRS)
                    for g in range(HE // 4):
                        for t in range(NT):
                            last = pe.transpose(ps[0:4, g, t * P:(t + 1) * P],
                                                gate[:, t * HE + 4 * g:t * HE + 4 * g + 4, 0], k.ident)
                    last.then_inc(s["gateT_ready"], 1)

                @block.scalar
                def _(act):
                    act.wait_ge(s["logits"], 1)
                    act.activation(gates[:, :, :], ps[:, 2, 0:256].rearrange("p (a e) -> p a e", e=E), ACT.Sigmoid
                                   ).then_inc(s["gates"], 1)
                    for m in range(2 * PAIRS):
                        act.wait_ge(s["qk"], m + 1)
                        if m % 2 == 0:
                            act.copy(qT[:, m // 2, :], ps[:, 0, :]).then_inc(s["qk_sb"], 1)
                        else:
                            act.copy(kT[0:WD, m - 1, :], ps[0:WD, 1, :])
                            act.copy(kT[WD:P, m, :], ps[WD:P, 1, :]).then_inc(s["qk_sb"], 1)
                    act.wait_ge(s["gateT_ready"], 1)
                    act.copy(gateT[:, :, :], ps[0:4, 0:HE // 4, :]).then_inc(s["gateT_sb"], 1)

                @block.gpsimd
                def _(pool):
                    pool.memset(kT[WD:P, 0::2, :], 0.0)
                    pool.memset(kT[0:WD, 1::2, :], 0.0)

                @block.vector
                def _(dve):
                    chain = Chain(dve, s["chain"])
                    chain(dve.memset(v[:, :, :, WD:2 * WD], 1.0))
                    dve.wait_ge(s["gates"], 1)
                    S3 = [P, NT * HE, E]
                    top_one(k, dve, chain, gates[:, :, :], key[:, :, :], gate[:, :, :], None, E)
                    dve.tensor_reduce(kmax[:, :, :], key[:, :, :], AX.X, ALU.max).then_inc(s["gate"], 1)
                    dve.wait_ge(s["gate"], 1)
                    pk = picked[:, :, :, :].rearrange("p t h e -> p (t h) e")
                    chain(dve.tensor_tensor(pk, key[:, :, :], kmax[:, :, :].to_broadcast(S3), ALU.is_equal))
                    chain(dve.tensor_copy(picked_b[:, :, :].rearrange("p t (h e) -> p (t h) e", e=E), pk))
                    for e in range(E):
                        for t in range(NT):
                            i = e * NT + t
                            dve.wait_ge(s["values"], i + 1)
                            if e:
                                dve.wait_ge(s["chosen"], i - NT + 1)
                            got = ps[:, 4 + i % 4, :].rearrange("p (r j d) -> p r j d", r=PAIRS, j=2)
                            if e:
                                mask = picked[:, t, :, e:e + 1].rearrange("p (r j) o -> p r j o", j=2)
                                last = dve.copy_predicated(heads_of(t, 0, PAIRS), mask.to_broadcast([P, PAIRS, 2, WD]),
                                                           got)
                            else:
                                last = dve.tensor_copy(heads_of(t, 0, PAIRS), got)
                            last.then_inc(s["chosen"], 1)
                    dve.wait_ge(s["chosen"], NT * E)
                    for t in range(NT):
                        g = gate[:, t * HE:(t + 1) * HE, :].rearrange("p (r j) o -> p r j o", j=2)
                        at = heads_of(t, 0, PAIRS)
                        dve.tensor_tensor(at, at, g.to_broadcast([P, PAIRS, 2, WD]), ALU.mult)

            wide_attend(k, "L1g", HE, WD ** -0.5, qT, kT, v, zT, gateT=gateT, sb=
                        lambda n, sh, dt: inner.enter_context(nc.sbuf_tensor(f"moa_{n}", sh, dt)))

        pT = sb("pT", [HE * E, SEQ], BF16)
        RING = 4
        xm = sb("xm", [P, RING, SEQ])
        pT_ps = ps[:, 2, :].bitcast(BF16)
        with phase(k, "chain", "pT_ready", "pT_sb", "spread", "masked", "used",
                   "y_ready", *NORM_SEMS) as (block, s):
            @block.tensor
            def _(pe):
                for t in range(NT):
                    last = pe.transpose(pT_ps[0:HE * E, t * P:(t + 1) * P], picked_b[:, t, :], wb(k, "ident"))
                last.then_inc(s["pT_ready"], 1)
                pe.wait_ge(s["pT_sb"], 1)

                def spread(i):
                    if i >= 2:
                        pe.wait_ge(s["masked"], i - 1)
                    pe.matmul(ps[:, 2 + i % 2, :], wb(k, "selhe", HE * E)[:, i * P:(i + 1) * P], pT[:, :],
                              start=True, stop=True).then_inc(s["spread"], 1)

                spread(0)
                for i in range(PAIRS * E):
                    if i + 1 < PAIRS * E:
                        spread(i + 1)
                    pe.wait_ge(s["masked"], i + 1)
                    for t in range(NT):
                        last = pe.matmul(ps[:, 4 + t, 0:D], xm[:, i % RING, t * P:(t + 1) * P], output[:, i % E, i // E, :],
                                         start=i == 0, stop=i == PAIRS * E - 1)
                    last.then_inc(s["used"], 1)
                norm_tensor(k, pe, s, 0)

            @block.scalar
            def _(act):
                act.wait_ge(s["pT_ready"], 1)
                act.copy(pT[:, :], pT_ps[0:HE * E, 0:SEQ]).then_inc(s["pT_sb"], 1)
                norm_scalar(k, act, s, 0)

            @block.gpsimd
            def _(pool):
                norm_gpsimd(k, pool, s)

            @block.vector
            def _(dve):
                chain = Chain(dve, s["chain"])
                for i in range(PAIRS * E):
                    dve.wait_ge(s["spread"], i + 1)
                    if i >= RING:
                        dve.wait_ge(s["used"], i - RING + 1)
                    dve.tensor_tensor(xm[:, i % RING, :], zT[:, i // E, :], ps[:, 2 + i % 2, :], ALU.mult
                                      ).then_inc(s["masked"], 1)
                dve.wait_ge(s["used"], PAIRS * E)
                norm_vector(k, dve, chain, s, ps[:, 4:8, 0:D])


def shared_kv_attention(k):
    nc, ps = k.nc, k.ps
    name, HW = "L2a", 16
    PAIRS = HW // 2
    with ExitStack() as ctx:
        def sb(n, shape, dt=F32):
            return ctx.enter_context(nc.sbuf_tensor(f"skv_{n}", shape, dt))

        zT = sb("zT", [P, PAIRS, SEQ])
        with ExitStack() as inner:
            def sbi(n, shape, dt=F32):
                return inner.enter_context(nc.sbuf_tensor(f"skv_{n}", shape, dt))

            qT = sbi("qT", [P, PAIRS, SEQ])
            kT = k.stream[:, 0:HW * SEQ].rearrange("p (h t) -> p h t", h=HW)
            v = sbi("v", [P, NT, PAIRS, 3 * WD])
            kw1 = sbi("kw1", [P, PAIRS])
            with phase(k, "chain", "q_ready", "k_ready", "v_ready", "q_sb", "k_sb", "v_sb") as (block, s):
                @block.gpsimd
                def _(pool):
                    pool.memset(kT[WD:P, 0::2, :], 0.0)
                    pool.memset(kT[0:WD, 1::2, :], 0.0)

                @block.tensor
                def _(pe):
                    for m in range(PAIRS):
                        if m >= 2:
                            pe.wait_ge(s["q_sb"], m - 1)
                        pe.matmul(ps[:, m % 2, :], w(k, name, "wq")[:, m * P:(m + 1) * P], k.xT[:, :], start=True,
                                  stop=True).then_inc(s["q_ready"], 1)
                        if m >= 2:
                            pe.wait_ge(s["k_sb"], m - 1)
                        pe.matmul(ps[:, 2 + m % 2, :], w(k, name, "wkv")[:, m * P:(m + 1) * P], k.xT[:, :], start=True,
                                  stop=True).then_inc(s["k_ready"], 1)
                        if m >= 2:
                            pe.wait_ge(s["v_sb"], m - 1)
                        t = m // 2
                        pe.matmul(ps[:, 4 + m % 2, :], k.xT[:, t * P:(t + 1) * P],
                                  w(k, name, "wkv")[:, m % 2 * 512:(m % 2 + 1) * 512], start=True, stop=True
                                  ).then_inc(s["v_ready"], 1)

                @block.scalar
                def _(act):
                    for m in range(PAIRS):
                        act.wait_ge(s["q_ready"], m + 1)
                        act.copy(qT[:, m, :], ps[:, m % 2, :]).then_inc(s["q_sb"], 1)

                @block.vector
                def _(dve):
                    chain = Chain(dve, s["chain"])
                    dve.memset(v[:, :, :, WD:2 * WD], 1.0)
                    chain(dve.tensor_scalar(kw1[:, :], w(k, name, "kw"), 1.0, None, ALU.add))
                    for m in range(PAIRS):
                        dve.wait_ge(s["k_ready"], m + 1)
                        dve.tensor_scalar(kT[0:WD, 2 * m, :], ps[0:WD, 2 + m % 2, :], kw1[0:WD, m:m + 1], None, ALU.mult)
                        dve.tensor_scalar(kT[WD:P, 2 * m + 1, :], ps[WD:P, 2 + m % 2, :], kw1[WD:P, m:m + 1], None,
                                          ALU.mult).then_inc(s["k_sb"], 1)
                        dve.wait_ge(s["v_ready"], m + 1)
                        r0 = m % 2 * 4
                        at = v[:, m // 2, r0:r0 + 4, :].rearrange("p r (j d) -> p r j d", j=3)[:, :, 0:3:2, :]
                        dve.tensor_copy(at, ps[:, 4 + m % 2, :].rearrange("p (r j d) -> p r j d", r=4, j=2)
                                        ).then_inc(s["v_sb"], 1)

            wide_attend(k, name, HW, D ** -0.5, qT, kT, v, zT,
                        lambda n, sh, dt: inner.enter_context(nc.sbuf_tensor(f"skv_{n}", sh, dt)))

        wo = w(k, name, "wo").rearrange("p (r d) -> p r d", r=PAIRS)
        with phase(k, "chain", "y_ready", *NORM_SEMS) as (block, s):
            @block.tensor
            def _(pe):
                for r in range(PAIRS):
                    for t in range(NT):
                        last = pe.matmul(ps[:, 4 + t, 0:D], zT[:, r, t * P:(t + 1) * P], wo[:, r, :], start=r == 0,
                                         stop=r == PAIRS - 1)
                last.then_inc(s["y_ready"], 1)
                norm_tensor(k, pe, s, 2)

            @block.scalar
            def _(act):
                norm_scalar(k, act, s, 2)

            @block.gpsimd
            def _(pool):
                norm_gpsimd(k, pool, s)

            @block.vector
            def _(dve):
                chain = Chain(dve, s["chain"])
                dve.wait_ge(s["y_ready"], 1)
                norm_vector(k, dve, chain, s, ps[:, 4:8, 0:D])


def top_two(k, dve, chain, vals, E, b):
    S3 = [P, NT, E]
    top_one(k, dve, chain, vals, b.key[:, :, 0:E], b.best[:, :, :], None, E)
    chain(dve.tensor_reduce(b.kmax[:, :, :], b.key[:, :, 0:E], AX.X, ALU.max))
    chain(dve.tensor_tensor(b.first[:, :, 0:E], b.key[:, :, 0:E], b.kmax[:, :, :].to_broadcast(S3), ALU.is_equal))
    chain(dve.scalar_tensor_tensor(out=b.rest[:, :, 0:E], in0=b.first[:, :, 0:E], scalar=-1e30, in1=vals,
                                   op0=ALU.mult, op1=ALU.add))
    top_one(k, dve, chain, b.rest[:, :, 0:E], b.key[:, :, 0:E], b.second[:, :, :], None, E)
    chain(dve.tensor_reduce(b.kmax[:, :, :], b.key[:, :, 0:E], AX.X, ALU.max))
    chain(dve.tensor_tensor(b.next[:, :, 0:E], b.key[:, :, 0:E], b.kmax[:, :, :].to_broadcast(S3), ALU.is_equal))


class RouterBuffers:

    def __init__(self, sb):
        def wide(n):
            return sb(n, [P, NT, 8])

        def one(n):
            return sb(n, [P, NT, 1])

        self.vals, self.key, self.first, self.next, self.rest = (
            wide("vals"), wide("key"), wide("first"), wide("next"), wide("rest"))
        self.best, self.second, self.kmax, self.e2, self.w1, self.w2 = (
            one("best"), one("second"), one("kmax"), one("e2"), one("w1"), one("w2"))


def conv_experts(k, next_stream):
    nc, ps = k.nc, k.ps
    name, E, TAPS, HID2, RMS_EPS = "L2f", 8, 3, 32, 1e-6
    W = lambda n, r=P: w(k, name, n, r)
    bc = lambda n, c=D: W(n).unsqueeze(1).to_broadcast([P, NT, c])
    with ExitStack() as ctx:
        def sb(n, shape, dt=F32):
            return ctx.enter_context(nc.sbuf_tensor(f"conv_{n}", shape, dt))

        xpad = sb("xpad", [P, SEQ + TAPS - 1])
        acc = sb("acc", [P, SEQ])
        pw = sb("pw", [P, SEQ])
        x1T = sb("x1T", [P, SEQ])
        x1 = sb("x1", [P, NT, D])
        rw = sb("rw", [P, NT, E])
        yb = sb("yb", [P, NT, 2, SEQ])
        comb = sb("comb", [P, NT, D])
        combT = sb("combT", [P, SEQ])
        r = sb("r", [P, NT, D])
        sq = sb("sq", [P, NT, D])
        h = sb("h", [P, NT, D])
        hT = sb("hT", [P, SEQ])
        g = sb("g", [HID2, SEQ])
        b = RouterBuffers(sb)
        tok = lambda bank: ps[:, bank, :].rearrange("p (t d) -> p t d", t=NT)
        with phase(k, "chain", "conv_done", "pw_ready", "pw_sb", "x1T_done", "turned", "logits", "x1_sb", "e_in", "e_out", "ye_in",
                   "ye_out", "comb_ready") as (block, s):
            @block.sync
            def _(sp):
                next_stream(sp)

            @block.tensor
            def _(pe):
                pe.wait_ge(s["conv_done"], 1)
                pe.matmul(ps[:, 0, :], W("pw"), acc[:, :], start=True, stop=True).then_inc(s["pw_ready"], 1)
                pe.wait_ge(s["x1T_done"], 1)
                for t in range(NT):
                    last = pe.matmul(ps[:, 2, t * E:(t + 1) * E], x1T[:, t * P:(t + 1) * P], W("router"), start=True, stop=True)
                last.then_inc(s["logits"], 1)
                for t in range(NT):
                    last = pe.transpose(ps[:, 1, t * P:(t + 1) * P], x1T[:, t * P:(t + 1) * P], k.ident)
                last.then_inc(s["turned"], 1)
                for t in range(NT):
                    for c in range(2):
                        i = 2 * t + c
                        if i >= 4:
                            pe.wait_ge(s["ye_in"], i - 3)
                        pe.matmul(ps[:, 4 + i % 4, :], x1T[:, t * P:(t + 1) * P], W("experts")[:, c * 512:(c + 1) * 512],
                                  start=True, stop=True).then_inc(s["e_in"], 1)

            @block.scalar
            def _(act):
                act.wait_ge(s["pw_ready"], 1)
                act.activation(pw[:, :], ps[:, 0, :], ACT.Silu, bias=W("pwb")).then_inc(s["pw_sb"], 1)
                act.wait_ge(s["turned"], 1)
                act.copy(x1[:, :, :], tok(1))
                for i in range(2 * NT):
                    act.wait_ge(s["ye_in"], i + 1)
                    act.activation(yb[:, i // 2, i % 2, :], yb[:, i // 2, i % 2, :], ACT.Silu).then_inc(s["ye_out"], 1)
                act.wait_ge(s["e_out"], 1)
                act.activation(b.e2[:, :, :], b.e2[:, :, :], ACT.Exp).then_inc(s["x1_sb"], 1)

            @block.vector
            def _(dve):
                chain = Chain(dve, s["chain"])
                dve.memset(xpad[:, 0:TAPS - 1], 0.0)
                chain(dve.tensor_copy(xpad[:, TAPS - 1:], k.xT[:, :]))
                chain(dve.tensor_scalar(acc[:, :], xpad[:, 0:SEQ], W("conv")[:, 0:1], W("cb"), ALU.mult, ALU.add))
                for t in range(1, TAPS):
                    last = dve.scalar_tensor_tensor(out=acc[:, :], in0=xpad[:, t:t + SEQ], scalar=W("conv")[:, t:t + 1],
                                                    in1=acc[:, :], op0=ALU.mult, op1=ALU.add)
                    if t < TAPS - 1:
                        chain(last)
                last.then_inc(s["conv_done"], 1)
                dve.wait_ge(s["pw_sb"], 1)
                dve.tensor_tensor(x1T[:, :], k.xT[:, :], pw[:, :], ALU.add).then_inc(s["x1T_done"], 1)
                dve.wait_ge(s["logits"], 1)
                chain(dve.tensor_tensor(b.vals[:, :, :], ps[:, 2, 0:NT * E].rearrange("p (t e) -> p t e", t=NT),
                                        bc("rb", E), ALU.add))
                top_two(k, dve, chain, b.vals[:, :, :], E, b)
                dve.tensor_tensor(b.e2[:, :, :], b.second[:, :, :], b.best[:, :, :], ALU.subtract).then_inc(s["e_out"], 1)
                for i in range(2 * NT):
                    dve.wait_ge(s["e_in"], i + 1)
                    dve.tensor_tensor(yb[:, i // 2, i % 2, :], ps[:, 4 + i % 4, :],
                                      W("eb")[:, i % 2 * 512:(i % 2 + 1) * 512], ALU.add).then_inc(s["ye_in"], 1)
                dve.wait_ge(s["x1_sb"], 1)
                chain(dve.tensor_scalar(b.w1[:, :, :], b.e2[:, :, :], 1.0, None, ALU.add))
                chain(dve.reciprocal(b.w1[:, :, :], b.w1[:, :, :]))
                chain(dve.tensor_tensor(b.w2[:, :, :], b.e2[:, :, :], b.w1[:, :, :], ALU.mult))
                mix(dve, chain, b, rw[:, :, :], E)
                ye = yb[:, :, :, :].rearrange("p t c (e d) -> p t (c e) d", e=4)
                for e in range(E):
                    for t in range(NT):
                        if e == 0:
                            dve.wait_ge(s["ye_out"], 2 * t + 2)
                            last = dve.tensor_scalar(comb[:, t, :], ye[:, t, e, :], rw[:, t, e:e + 1], None, ALU.mult)
                        else:
                            last = dve.scalar_tensor_tensor(out=comb[:, t, :], in0=ye[:, t, e, :], scalar=rw[:, t, e:e + 1],
                                                            in1=comb[:, t, :], op0=ALU.mult, op1=ALU.add)
                    chain(last)

        with phase(k, "chain", "turned", "turned_sb", "moe_ready", "h_ready", "hT_ready", "hT_sb", "down_ready", "g_ready", "up_ready",
                   "ms_ready", "ms_eps", "rms_ready", *NORM_SEMS) as (block, s):
            @block.tensor
            def _(pe):
                for t in range(NT):
                    last = pe.transpose(ps[:, 0, t * P:(t + 1) * P], comb[:, t, :], k.ident)
                last.then_inc(s["turned"], 1)
                pe.wait_ge(s["turned_sb"], 1)
                for t in range(NT):
                    last = pe.matmul(ps[:, 1, t * D:(t + 1) * D], combT[:, t * P:(t + 1) * P], W("out"), start=True, stop=True)
                last.then_inc(s["moe_ready"], 1)
                pe.wait_ge(s["h_ready"], 1)
                for t in range(NT):
                    last = pe.transpose(ps[:, 2, t * P:(t + 1) * P], h[:, t, :], k.ident)
                last.then_inc(s["hT_ready"], 1)
                pe.wait_ge(s["hT_sb"], 1)
                pe.matmul(ps[0:HID2, 3, :], W("down"), hT[:, :], start=True, stop=True).then_inc(s["down_ready"], 1)
                pe.wait_ge(s["g_ready"], 1)
                for t in range(NT):
                    last = pe.matmul(ps[:, 4, t * D:(t + 1) * D], g[:, t * P:(t + 1) * P], W("up", HID2), start=True, stop=True)
                last.then_inc(s["up_ready"], 1)
                norm_tensor(k, pe, s, 5)

            @block.scalar
            def _(act):
                act.wait_ge(s["turned"], 1)
                act.copy(combT[:, :], ps[:, 0, :]).then_inc(s["turned_sb"], 1)
                act.wait_ge(s["hT_ready"], 1)
                act.copy(hT[:, :], ps[:, 2, :]).then_inc(s["hT_sb"], 1)
                act.wait_ge(s["down_ready"], 1)
                act.activation(g[:, :], ps[0:HID2, 3, :], ACT.Gelu, bias=W("downb", HID2)).then_inc(s["g_ready"], 1)
                norm_scalar(k, act, s, 5)

            @block.gpsimd
            def _(pool):
                pool.wait_ge(s["ms_ready"], 1)
                pool.tensor_scalar(k.vareps[:, :], b.e2[:, :, 0], 1.0 / D, RMS_EPS, ALU.mult, ALU.add).then_inc(s["ms_eps"], 1)
                pool.wait_ge(s["ms_eps"], 1)
                pool.tensor_tensor(k.rstd[:, :], k.vareps[:, :], k.minus_half, ALU.pow).then_inc(s["rms_ready"], 1)
                norm_gpsimd(k, pool, s)

            @block.vector
            def _(dve):
                chain = Chain(dve, s["chain"])
                chain(dve.tensor_tensor(x1[:, :, :], x1[:, :, :], bc("ob"), ALU.add))
                dve.wait_ge(s["moe_ready"], 1)
                chain(dve.tensor_tensor(r[:, :, :], tok(1), x1[:, :, :], ALU.add))
                chain(dve.tensor_tensor(sq[:, :, :], r[:, :, :], r[:, :, :], ALU.mult))
                dve.tensor_reduce(b.e2[:, :, :], sq[:, :, :], AX.X, ALU.add).then_inc(s["ms_ready"], 1)
                dve.wait_ge(s["rms_ready"], 1)
                for t in range(NT):
                    last = dve.scalar_tensor_tensor(out=h[:, t, :], in0=r[:, t, :], scalar=k.rstd[:, t:t + 1],
                                                    in1=W("norm"), op0=ALU.mult, op1=ALU.mult)
                last.then_inc(s["h_ready"], 1)
                dve.wait_ge(s["h_ready"], 1)
                chain(dve.tensor_tensor(r[:, :, :], h[:, :, :], bc("upb"), ALU.add))
                dve.wait_ge(s["up_ready"], 1)
                chain(dve.tensor_tensor(h[:, :, :], tok(4), r[:, :, :], ALU.add))
                norm_vector(k, dve, chain, s, h[:, :, :])


def mix(dve, chain, b, rw, E):
    S3 = [P, NT, E]
    chain(dve.tensor_tensor(b.first[:, :, 0:E], b.first[:, :, 0:E], b.w1[:, :, :].to_broadcast(S3), ALU.mult))
    chain(dve.tensor_tensor(b.next[:, :, 0:E], b.next[:, :, 0:E], b.w2[:, :, :].to_broadcast(S3), ALU.mult))
    chain(dve.tensor_tensor(rw, b.first[:, :, 0:E], b.next[:, :, 0:E], ALU.add))


def routed_ffn(k, stream_loaded):
    nc, ps = k.nc, k.ps
    name, E = "L3f", EXPERTS3 - 1
    at, _ = S_AT["L3e"]
    part = lambda n: k.stream[:, at["L3e", n][0]:sum(at["L3e", n])]
    gate, up = (part(n).rearrange("p (e f) -> p e f", e=EXPERTS3) for n in ("gate", "up"))
    down = part("down").rearrange("p (e t d) -> p e t d", e=EXPERTS3, t=3)
    HT = len(HID_TILES)
    with ExitStack() as ctx:
        def sb(n, shape, dt=F32):
            return ctx.enter_context(nc.sbuf_tensor(f"rffn_{n}", shape, dt))

        b = RouterBuffers(sb)
        rw = sb("rw", [P, NT, EXPERTS3])
        sg = sb("sg", [P, 2, SEQ])
        hid = sb("hid", [P, 2, HT, SEQ])
        acc = sb("acc", [P, NT, D])
        with phase(k, "chain", "logits", "scaled", "probs", "up_ready", "silu_ready", "hid_ready", "down_ready", "added",
                   *NORM_SEMS) as (block, s):
            @block.tensor
            def _(pe):
                for t in range(NT):
                    last = pe.matmul(ps[:, 6, t * E:(t + 1) * E], k.xT[:, t * P:(t + 1) * P], w(k, name, "wr"), start=True,
                                     stop=True)
                last.then_inc(s["logits"], 1)
                pe.wait_ge(stream_loaded, 16)

                def gate_up(e):
                    for t, (a0, nr) in enumerate(HID_TILES):
                        i = e * HT + t
                        if i >= 2:
                            pe.wait_ge(s["hid_ready"], i - 1)
                        bk = 2 * (i % 2)
                        pe.matmul(ps[0:nr, bk, :], gate[:, e, a0:a0 + nr], k.xT[:, :], start=True, stop=True)
                        pe.matmul(ps[0:nr, bk + 1, :], up[:, e, a0:a0 + nr], k.xT[:, :], start=True, stop=True
                                  ).then_inc(s["up_ready"], 1)

                gate_up(0)
                for e in range(EXPERTS3):
                    if e + 1 < EXPERTS3:
                        gate_up(e + 1)
                    pe.wait_ge(s["hid_ready"], (e + 1) * HT)
                    if e >= 2:
                        pe.wait_ge(s["added"], e - 1)
                    for tt in range(NT):
                        for t, (a0, nr) in enumerate(HID_TILES):
                            last = pe.matmul(ps[:, 4 + e % 2, tt * D:(tt + 1) * D], hid[0:nr, e % 2, t, tt * P:(tt + 1) * P],
                                             down[0:nr, e, t, :], start=t == 0, stop=t == HT - 1)
                    last.then_inc(s["down_ready"], 1)
                norm_tensor(k, pe, s, 7)

            @block.scalar
            def _(act):
                act.wait_ge(s["scaled"], 1)
                act.activation(b.vals[:, :, 0:E], b.vals[:, :, 0:E], ACT.Sigmoid).then_inc(s["probs"], 1)
                for e in range(EXPERTS3):
                    for t, (a0, nr) in enumerate(HID_TILES):
                        i = e * HT + t
                        act.wait_ge(s["up_ready"], i + 1)
                        if i >= 2:
                            act.wait_ge(s["hid_ready"], i - 1)
                        act.activation(sg[0:nr, i % 2, :], ps[0:nr, 2 * (i % 2), :], ACT.Silu).then_inc(s["silu_ready"], 1)
                norm_scalar(k, act, s, 7)

            @block.gpsimd
            def _(pool):
                norm_gpsimd(k, pool, s)

            @block.vector
            def _(dve):
                chain = Chain(dve, s["chain"])
                S3 = [P, NT, E]

                def route():
                    top_two(k, dve, chain, b.vals[:, :, 0:E], E, b)
                    chain(dve.tensor_tensor(b.e2[:, :, :], b.best[:, :, :], b.second[:, :, :], ALU.add))
                    chain(dve.reciprocal(b.e2[:, :, :], b.e2[:, :, :]))
                    chain(dve.tensor_tensor(b.w1[:, :, :], b.best[:, :, :], b.e2[:, :, :], ALU.mult))
                    chain(dve.tensor_tensor(b.w2[:, :, :], b.second[:, :, :], b.e2[:, :, :], ALU.mult))
                    chain(dve.memset(rw[:, :, 0:1], 1.0))
                    mix(dve, chain, b, rw[:, :, 1:EXPERTS3], E)

                def add(e):
                    dve.wait_ge(s["down_ready"], e + 1)
                    for t in range(NT):
                        y = ps[:, 4 + e % 2, t * D:(t + 1) * D]
                        if e == 0:
                            last = dve.tensor_scalar(acc[:, t, :], y, rw[:, t, 0:1], None, ALU.mult)
                        else:
                            last = dve.scalar_tensor_tensor(out=acc[:, t, :], in0=y, scalar=rw[:, t, e:e + 1],
                                                            in1=acc[:, t, :], op0=ALU.mult, op1=ALU.add)
                    last.then_inc(s["added"], 1)
                    dve.wait_ge(s["added"], e + 1)

                dve.wait_ge(s["logits"], 1)
                chain(dve.tensor_tensor(b.vals[:, :, 0:E], ps[:, 6, 0:NT * E].rearrange("p (t e) -> p t e", t=NT),
                                        w(k, name, "rb").unsqueeze(1).to_broadcast(S3), ALU.mult))
                dve.memset(b.w1[:, :, :], 0.0).then_inc(s["scaled"], 1)
                dve.wait_ge(s["probs"], 1)
                route()
                for e in range(EXPERTS3):
                    for t, (a0, nr) in enumerate(HID_TILES):
                        i = e * HT + t
                        dve.wait_ge(s["silu_ready"], i + 1)
                        if e >= 2 and t == 0:
                            dve.wait_ge(s["down_ready"], e - 1)
                        dve.tensor_tensor(hid[0:nr, e % 2, t, :], sg[0:nr, i % 2, :], ps[0:nr, 2 * (i % 2) + 1, :], ALU.mult
                                          ).then_inc(s["hid_ready"], 1)
                    if e >= 1:
                        add(e - 1)
                add(EXPERTS3 - 1)
                norm_vector(k, dve, chain, s, acc[:, :, :])


class Kernel:
    pass


def build(nc, xin, xTin, ctxT, m1q, m1k, m3q, m3k, wres, wstr0, wstr1, wstr3, bc, out):
    k = Kernel()
    k.nc = nc
    with ExitStack() as ctx:
        def sb(n, shape, dt=F32):
            return ctx.enter_context(nc.sbuf_tensor(n, shape, dt))

        k.weights = sb("weights", [P, R_N])
        k.stream = sb("stream", [P, S_N])
        k.bconst = sb("bconst", [P, B_N], BF16)
        k.x = sb("x_tok", [P, NT, D])
        k.xT = sb("xT", [P, SEQ])
        k.src = sb("src", [P, SEQ])
        k.ctxT = sb("ctxT", [P, CTX])
        k.resid = sb("resid", [P, NT, D])
        k.stats = sb("stats", [P, NT, 6])
        k.mv = sb("mv", [P, NT, 2])
        k.vareps = sb("vareps", [P, NT])
        k.rstd = sb("rstd", [P, NT])
        k.ps = ctx.enter_context(nc.psum_tensor("ps", [P, 8, 512], F32))
        k.ident = w(k, "const", "ident")
        k.minus_half = w(k, "const", "half")[:, 0:NT]
        loaded = {g: ctx.enter_context(nc.semaphore(f"loaded_{g}")) for g in GROUPS}
        bloaded = ctx.enter_context(nc.semaphore("bloaded"))
        stream_loaded = ctx.enter_context(nc.semaphore("stream_loaded"))
        stored = ctx.enter_context(nc.semaphore("stored"))
        k.pool = [ctx.enter_context(nc.semaphore(f"stage_{i}")) for i in range(18)]

        with nc.Block() as block:
            @block.sync
            def _(sp):
                sp.dma_start(k.bconst[:, :], bc[:, :]).then_inc(bloaded, 16)
                for g in GROUPS:
                    a = min(R_AT[x][0] for x in R_AT if x[0] == g)
                    z = max(sum(R_AT[x]) for x in R_AT if x[0] == g)
                    sp.dma_start(k.weights[:, a:z], wres[:, a:z]).then_inc(loaded[g], 16)
                for g in GROUPS:
                    sp.wait_ge(loaded[g], 16)
                sp.wait_ge(bloaded, 16)

        def stream_in(sp, src):
            sp.sem_clear(stream_loaded)
            sp.dma_start(k.stream[:, 0:src.shape[1]], src[:, :]).then_inc(stream_loaded, 16)

        with nc.Fori(0, BATCH) as b:
            k.b = b
            with phase(k, "x_in") as (block, s):
                @block.sync
                def _(sp):
                    sp.dma_start(k.x[:, :, :], xin[bass.ds(b, 1)].rearrange("o (t p) d -> p (o t) d", p=P)
                                 ).then_inc(s["x_in"], 16)
                    sp.dma_start(k.xT[:, :], xTin[bass.ds(b, 1)].rearrange("o p t -> p (o t)")).then_inc(s["x_in"], 16)
                    sp.dma_start(k.ctxT[:, :], ctxT[bass.ds(b, 1)].rearrange("o p t -> p (o t)")).then_inc(s["x_in"], 16)
                    stream_in(sp, wstr0)
                    sp.wait_ge(s["x_in"], 48)

            R8 = DH ** -0.5
            stages = [
                lambda: small_attention(k, "L0a", R8, SEQ, P, k.src, k.src),
                lambda: small_attention(k, "L0x", 1.0, CTX, KT2, k.xT, k.ctxT, scrambled=True),
                lambda: gated_ffn(k, stream_loaded),
                lambda: mamba(k, lambda sp: stream_in(sp, wstr1)),
                lambda: small_attention(k, "L1x", R8, CTX, KT2, k.xT, k.ctxT, masks=(m1q, m1k, ALU.is_equal)),
                lambda: expert_attention(k, stream_loaded),
                lambda: shared_kv_attention(k),
                lambda: small_attention(k, "L2x", R8, CTX, KT2, k.xT, k.ctxT),
                lambda: conv_experts(k, lambda sp: stream_in(sp, wstr3)),
                lambda: small_attention(k, "L3a", R8, SEQ, P, k.src, k.src, biased=False, v_biased=False),
                lambda: small_attention(k, "L3x", R8, CTX, KT2, k.xT, k.ctxT, biased=False, v_biased=False,
                                        masks=(m3q, m3k, ALU.not_equal)),
                lambda: routed_ffn(k, stream_loaded),
            ]
            for stage in stages:
                stage()
            with phase(k, "x_out") as (block, s):
                @block.sync
                def _(sp):
                    sp.dma_start(out[bass.ds(b, 1)].rearrange("o (t p) d -> p (o t) d", p=P), k.x[:, :, :]
                                 ).then_inc(s["x_out"], 16)
                    sp.wait_ge(s["x_out"], 16)


def block_diagonal(m):
    h, i, j = m.shape
    out = np.zeros((h, j, h, i), m.dtype)
    for n in range(h):
        out[n, :, n, :] = m[n].T
    return out.reshape(h * j, h * i)


def by_dim(m):
    return m.reshape(m.shape[0], H, DH).transpose(0, 2, 1).reshape(m.shape[0], H * DH)


def rows(v):
    return np.broadcast_to(v.reshape(1, -1), (P, v.size))


def tiles(m):
    return m.reshape(-1, P, m.shape[1]).transpose(1, 0, 2).reshape(P, -1)


def pack(at, n, blocks):
    out = np.zeros((P, n), np.float32)
    for key, m in blocks.items():
        c, cols = at[key]
        assert m.ndim == 2 and m.shape[1] == cols and m.shape[0] <= P, (key, m.shape, cols)
        out[:m.shape[0], c:c + cols] = m
    return out


def lay_out(i):
    B = {}
    col = lambda v: v.reshape(-1, 1)
    for a, key, t in (("L0a", "L0_attn_", True), ("L0x", "L0_xattn_", True), ("L1x", "L1_xattn_", True),
                      ("L2x", "L2_xattn_", True), ("L3x", "L3_xattn_", True)):
        g = lambda n: (i[key + n].T if t else i[key + n])
        B[a, "wq"], B[a, "wk"], B[a, "wv"] = by_dim(g("Wq")), by_dim(g("Wk")), g("Wv")
        if key + "Wo" in i:
            B[a, "wo"] = g("Wo")
        if key + "bq" in i:
            B[a, "bq"], B[a, "bk"] = (by_dim(i[key + n].reshape(1, -1)).T for n in ("bq", "bk"))
            B[a, "bv"] = rows(i[key + "bv"])
        if key + "bo" in i:
            B[a, "bo"] = rows(i[key + "bo"])
    B["L0x", "gamma"], B["L0x", "beta"] = rows(i["L0_xattn_gamma"]), rows(i["L0_xattn_beta"])
    B["L3a", "down"] = i["L3_attn_W_down"]
    B["L3a", "wq"] = by_dim(block_diagonal(i["L3_attn_toqueries"]))
    B["L3a", "wk"] = by_dim(block_diagonal(i["L3_attn_tokeys"]))
    B["L3a", "wv"] = block_diagonal(i["L3_attn_tovalues"])
    B["L3a", "wo"], B["L3a", "bo"] = i["L3_attn_W_unify"], rows(i["L3_attn_b_unify"])
    freq = np.exp(np.arange(0, D, 2, dtype=np.float32) * np.float32(-np.log(10000.0) / D)).astype(np.float32)
    ang = (np.arange(SEQ, dtype=np.float32)[:, None] * freq[None, :]).astype(np.float32)
    B["L0a", "cos"] = np.concatenate([np.cos(ang).T] * 2).astype(np.float32)
    B["L0a", "sin"] = np.concatenate([np.sin(ang).T] * 2).astype(np.float32)
    rot = np.zeros((D, D), np.float32)
    for j in range(D // 2):
        rot[j + D // 2, j] = -1.0
        rot[j, j + D // 2] = 1.0
    B["L0a", "rot"] = rot
    B["const", "ident"] = np.eye(P, dtype=np.float32)
    B["const", "desc"] = rows(np.arange(8, 0, -1).astype(np.float32))
    B["const", "half"] = np.full((P, 8), -0.5, np.float32)
    B["const", "one"] = np.ones((P, P), np.float32)
    B["const", "spread"] = np.zeros((P, 2 * P), np.float32)
    for h in range(4):
        B["const", "spread"][h, h * WD:(h + 1) * WD] = 1.0
    more_layout(i, B)
    return pack(R_AT, R_N, {x: v for x, v in B.items() if x in R_AT})


def bf16_consts():
    out = np.zeros((P, B_N), np.float32)

    def put(n, m):
        at, c = B_AT["b", n]
        out[:m.shape[0], at:at + c] = m
    put("ident", np.eye(P))
    q, kk = np.arange(P)[:, None], np.arange(P)[None, :]
    put("tri", np.where(kk > q, MASKED, 0.0))
    put("triT", np.where(q > kk, MASKED, 0.0))
    sel = np.zeros((12, 4, P))
    for hh in range(4):
        for p in range(PARTS):
            sel[p * 4 + hh, hh, :] = 1.0
    put("sel", sel.reshape(12, -1))
    put("stacked", np.concatenate([np.eye(32)] * PARTS))
    she = np.zeros((64, 4, 8, P))
    for pair in range(4):
        for e in range(8):
            for a in range(2):
                she[(2 * pair + a) * 8 + e, pair, e, 64 * a:64 * a + 64] = 1.0
    put("selhe", she.reshape(64, -1))
    return out.astype(mybir.dt.np(BF16))


def more_layout(i, B):
    g = lambda n: i["L0_ffn_" + n]
    for n, key in (("w1", "w1_w"), ("w2", "w2_w")):
        B["L0f", n] = g(key).T
    for n, key in (("h1", "h1_w"), ("h2", "h2_w"), ("w3", "w3_w")):
        B["L0f", n] = tiles(g(key).T)
    B["L0f", "s3"] = rows(g("w3_s"))
    cols = lambda v: v.reshape(-1, P).T
    for n, key in (("s1", "w1_s"), ("s2", "w2_s"), ("t1", "h1_s"), ("t2", "h2_s")):
        B["L0f", n] = cols(g(key))
    m = lambda n: i["L1_attn_" + n]
    B["L1m", "w_in"], B["L1m", "w_x"], B["L1m", "w_dt"] = m("W_in"), tiles(np.concatenate([m("W_x")] + [m("W_x")[:, 8:]] * 2, 1)), m("W_dt")
    B["L1m", "w_out"], B["L1m", "conv"] = tiles(m("W_out")), tiles(m("conv_w"))
    B["L1m", "cb"], B["L1m", "bdt"], B["L1m", "dskip"] = cols(m("conv_b")), cols(m("b_dt")), cols(m("D"))
    B["L1m", "alog"] = tiles(m("A_log"))
    B["L1g", "wq"], B["L1g", "wk"], B["L1g", "gate"] = (i["L1_ffn_" + n] for n in ("w_q", "w_k", "w_gate"))
    B["L2a", "wq"], B["L2a", "wkv"], B["L2a", "wo"] = i["L2_attn_w_q"], i["L2_attn_w_kv"], tiles(i["L2_attn_w_o"])
    B["L2a", "kw"] = cols(i["L2_attn_k_weights"].reshape(-1))
    f = lambda n: i["L2_ffn_" + n]
    B["L2f", "conv"], B["L2f", "cb"] = f("dw_kernel")[:, 0, :], f("dw_bias").reshape(-1, 1)
    B["L2f", "pw"], B["L2f", "pwb"] = f("pw_w").T, f("pw_b").reshape(-1, 1)
    B["L2f", "router"], B["L2f", "rb"] = f("router_w").T, rows(f("router_b"))
    B["L2f", "experts"], B["L2f", "eb"] = f("expert_w").transpose(2, 0, 1).reshape(P, -1), rows(f("expert_b").reshape(-1))
    B["L2f", "out"], B["L2f", "ob"], B["L2f", "norm"] = f("out_w").T, rows(f("out_b")), rows(f("norm_w"))
    B["L2f", "down"], B["L2f", "downb"] = f("ff_down_w").T, f("ff_down_b").reshape(-1, 1)
    B["L2f", "up"], B["L2f", "upb"] = f("ff_up_w").T, rows(f("ff_up_b"))
    B["L3f", "wr"], B["L3f", "rb"] = i["L3_ffn_Wr"], rows(i["L3_ffn_routing_bias"])


def by_query(m):
    m = m.reshape(BATCH, NT, P, CTX).transpose(0, 2, 1, 3).reshape(BATCH, P, NT * CTX)
    return np.ascontiguousarray(m).view(np.int32)


def by_key(m):
    m = m.reshape(BATCH, SEQ, 2, KT2).transpose(0, 3, 2, 1).reshape(BATCH, KT2, 2 * SEQ)
    return np.ascontiguousarray(m).view(np.int32)


def kernel(**inputs):
    import concourse.bacc as _bacc
    from concourse.bass_utils import run_bass_kernel_spmd as _run

    nc = _bacc.Bacc("TRN2", target_bir_lowering=False, num_devices=1)
    i = {n: np.asarray(a) for n, a in inputs.items()}
    m1 = i["mask_BxSxS2_ik1"]
    m3 = i["mask_Bx1xSxS2_bk1"].reshape(BATCH, SEQ, CTX)
    arrays = {
        "x_in": i["x"], "xT_in": i["x"].transpose(0, 2, 1), "ctxT_in": i["ctx_1024"].transpose(0, 2, 1),
        "mask1_qk": by_query(m1), "mask1_kq": by_key(m1), "mask3_qk": by_query(m3), "mask3_kq": by_key(m3),
        "weights_in": lay_out(i), "ffn_in": lay_out_streamed(i, "L0f"), "value_output_in": lay_out_streamed(i, "L1e"),
        "gate_up_down_in": lay_out_streamed(i, "L3e"), "bconst_in": bf16_consts(),
    }
    arrays = {n: np.ascontiguousarray(a) for n, a in arrays.items()}
    aps = [nc.dram_tensor(n, a.shape, mybir.dt.from_np(a.dtype), kind="ExternalInput").ap() for n, a in arrays.items()]
    out = nc.dram_tensor("out_dram", (BATCH, SEQ, D), F32, kind="ExternalOutput").ap()
    build(nc, *aps, out)
    r = _run(nc, [arrays], core_ids=[0])
    return r.results[0]["out_dram"]


def lay_out_streamed(i, g):
    at, n = S_AT[g]
    B = {}
    if g == "L0f":
        more_layout(i, B)
        B = {x: v for x, v in B.items() if x in at}
    elif g == "L1e":
        B[g, "value"] = i["L1_ffn_value_experts"].transpose(2, 0, 1, 3).reshape(P, 4096)
        B[g, "output"] = i["L1_ffn_output_experts"].reshape(8, 4, P, D).transpose(2, 0, 1, 3).reshape(P, 4096)
    else:
        for name, a, b in (("gate", "L3_ffn_shared_gate", "L3_ffn_routed_gate"), ("up", "L3_ffn_shared_up", "L3_ffn_routed_up")):
            B[g, name] = np.concatenate([i[a][None], i[b]]).transpose(1, 0, 2).reshape(P, -1)
        down = np.concatenate([i["L3_ffn_shared_down"][None], i["L3_ffn_routed_down"]])
        d3 = np.zeros((8, 3, P, D), np.float32)
        for t, (at0, nr) in enumerate(HID_TILES):
            d3[:, t, :nr] = down[:, at0:at0 + nr]
        B[g, "down"] = d3.transpose(2, 0, 1, 3).reshape(P, -1)
    return pack(at, n, B)
```
